# Optimizing a Trainium2 kernel written in Bass

```python
import numpy as np
import jax
import jax.numpy as jnp

def _softmax(x, axis=-1):
    return jax.nn.softmax(x, axis=axis)

def _gelu(x):
    return jax.nn.gelu(x, approximate=True)

def _silu(x):
    return jax.nn.silu(x)

def _sigmoid(x):
    return jax.nn.sigmoid(x)

def _layernorm(x, axis=-1, eps=1e-05):
    m = jnp.mean(x, axis=axis, keepdims=True)
    v = jnp.var(x, axis=axis, keepdims=True)
    return (x - m) / jnp.sqrt(v + eps)

def _scatter_add(tgt, idx, src, axis=0):
    return tgt.at[idx].add(src)

def _segment_sum(src, seg, n):
    return jax.ops.segment_sum(src, seg, n)
kernel_name = 'mk_xattn_seq_d4_seqx_r8_741e6a'

def setup_inputs(seed: int=0):
    np.random.seed(seed)
    _w = jnp.asarray

    def _rec_inputs():
        import jax
        import jax.numpy as jnp
        _rk = jax.random.key(seed)
        x = -0.0003929 + 0.9999 * jax.random.normal(jax.random.fold_in(_rk, 1), (8, 256, 256), jnp.float32)
        _lenS = 256 - jax.random.randint(jax.random.fold_in(_rk, 7), (8,), 0, max(1, 256 // 4) + 1, jnp.int32)
        _lenS2 = 1601 - jax.random.randint(jax.random.fold_in(_rk, 8), (8,), 0, max(1, 1601 // 4) + 1, jnp.int32)
        _ctx_1024P = jax.random.normal(jax.random.fold_in(_rk, 11), (8, 16, 128), jnp.float32)
        _ctx_1024c = jax.random.dirichlet(jax.random.fold_in(_rk, 511), 0.3 * jnp.ones((16,), jnp.float32), (8, 1601))
        _ctx_1024t = jnp.einsum('bsk,bkd->bsd', _ctx_1024c, _ctx_1024P)
        _ctx_1024t = _ctx_1024t * jax.lax.rsqrt(jnp.mean(jnp.square(_ctx_1024t)) + 1e-12) * 0.953939
        ctx_1024 = 0.00191187 + 0.999416 * (_ctx_1024t + 0.3 * jax.random.normal(jax.random.fold_in(_rk, 611), (8, 1601, 128), jnp.float32))
        pos_1xS = jnp.broadcast_to(jnp.arange(256, dtype=jnp.int32), (1, 256))
        _validS = jnp.arange(256)[None, :] < _lenS[:, None]
        _validS2 = jnp.arange(1601)[None, :] < _lenS2[:, None]
        _causal = jnp.tril(jnp.ones((256, 256), dtype=bool))
        mask_BxS2_bk0 = jnp.logical_not(jnp.broadcast_to(_validS2[:, :], (8, 1601)))
        mask_BxS_ik0 = jnp.where(jnp.broadcast_to(_validS[:, :], (8, 256)), 0, 1).astype(jnp.int32)
        return (x, ctx_1024, pos_1xS, mask_BxS2_bk0, mask_BxS_ik0)
    x, ctx_1024, pos_1xS, mask_BxS2_bk0, mask_BxS_ik0 = _rec_inputs()

    def _L0_xattn_setup():
        import jax, jax.numpy as jnp
        import numpy as np
        DIM = 256
        DIM_MEDIA = 128
        HEADS = 16
        DIM_HEAD = 64
        INNER = HEADS * DIM_HEAD
        FF_INNER = 4 * DIM
        B, N_TOK, N_LAT = (4, 256, 64)
        EPS = 1e-05

        def layernorm(x, g, b):
            mu = jnp.mean(x, axis=-1, keepdims=True)
            var = jnp.var(x, axis=-1, keepdims=True)
            return (x - mu) * jax.lax.rsqrt(var + EPS) * g + b
        key = jax.random.key(seed)
        ks = jax.random.split(key, 12)
        x = jax.random.normal(ks[0], (B, N_TOK, DIM), dtype=jnp.float32)
        media = jax.random.normal(ks[1], (B, N_LAT, DIM_MEDIA), dtype=jnp.float32)
        media_mask = jax.random.randint(ks[2], (B, N_LAT), 0, 2).astype(bool)
        media_mask = media_mask.at[:, 0].set(True)
        s = lambda d: 1.0 / np.sqrt(d)
        Wq = jax.random.normal(ks[3], (DIM, INNER), dtype=jnp.float32) * s(DIM)
        Wkv = jax.random.normal(ks[4], (DIM_MEDIA, 2 * INNER), dtype=jnp.float32) * s(DIM_MEDIA)
        Wo = jax.random.normal(ks[5], (INNER, DIM), dtype=jnp.float32) * s(INNER)
        W1 = jax.random.normal(ks[6], (DIM, FF_INNER), dtype=jnp.float32) * s(DIM)
        W2 = jax.random.normal(ks[7], (FF_INNER, DIM), dtype=jnp.float32) * s(FF_INNER)
        return {'x': x, 'media': media, 'media_mask': media_mask, 'ln_q_g': jnp.ones((DIM,), jnp.float32), 'ln_q_b': jnp.zeros((DIM,), jnp.float32), 'Wq': Wq, 'Wkv': Wkv, 'Wo': Wo, 'attn_gate': jax.random.normal(ks[8], (1,), jnp.float32) * 0.5, 'ln_ff_g': jnp.ones((DIM,), jnp.float32), 'ln_ff_b': jnp.zeros((DIM,), jnp.float32), 'W1': W1, 'W2': W2, 'ff_gate': jax.random.normal(ks[9], (1,), jnp.float32) * 0.5}
    _L0_xattn_all = _L0_xattn_setup()
    _L0_xattn_in = {k: v for k, v in _L0_xattn_all.items() if k in ('ln_q_g', 'ln_q_b', 'Wq', 'Wkv', 'Wo', 'attn_gate', 'ln_ff_g', 'ln_ff_b', 'W1', 'W2', 'ff_gate')}
    del _L0_xattn_all

    def _L1_xattn_setup():
        import jax, jax.numpy as jnp
        import numpy as np
        H = 256
        NH = 16
        HD = H // NH
        CH = 128
        CC = 128
        CHD = CC // NH
        I = 688
        B = 2
        L = 256
        LE = 128
        EPS = 1e-06

        def rms_norm(x, w):
            xf = x.astype(jnp.float32)
            var = jnp.mean(xf * xf, axis=-1, keepdims=True)
            return (w * (xf * jax.lax.rsqrt(var + EPS))).astype(x.dtype)

        def expert_mask(tt):
            vm = jnp.zeros(tt.shape, dtype=bool)
            vm = vm.at[:, :-1].set((tt[:, :-1] == 1) & (tt[:, 1:] == 1))
            return vm

        def rotate_half(x):
            d = x.shape[-1] // 2
            return jnp.concatenate([-x[..., d:], x[..., :d]], axis=-1)

        def apply_rotary(q, k, position_ids, seq_len):
            inv = 1.0 / 10000.0 ** (jnp.arange(0, HD, 2, dtype=jnp.float32) / HD)
            t = jnp.arange(seq_len, dtype=jnp.float32)
            freqs = jnp.outer(t, inv)
            emb = jnp.concatenate([freqs, freqs], axis=-1)
            cos = jnp.cos(emb)[position_ids][:, None].astype(q.dtype)
            sin = jnp.sin(emb)[position_ids][:, None].astype(q.dtype)
            return (q * cos + rotate_half(q) * sin, k * cos + rotate_half(k) * sin)

        def sdpa(q, k, v, causal):
            scale = 1.0 / np.sqrt(q.shape[-1])
            scores = jnp.einsum('bhqd,bhkd->bhqk', q * scale, k)
            if causal:
                mask = jnp.tril(jnp.ones((q.shape[-2], k.shape[-2]), dtype=bool))
                scores = jnp.where(mask, scores, jnp.finfo(jnp.float32).min)
            p = jax.nn.softmax(scores.astype(jnp.float32), axis=-1).astype(q.dtype)
            return jnp.einsum('bhqk,bhkd->bhqd', p, v)

        def heads(x, nh, hd):
            b, l, _ = x.shape
            return x.reshape(b, l, nh, hd).transpose(0, 2, 1, 3)
        key = jax.random.key(seed)
        ks = jax.random.split(key, 20)
        s = 0.02
        f32 = jnp.float32
        return {'hidden_states': jax.random.normal(ks[0], (B, L, H), f32), 'encoder_outputs': jax.random.normal(ks[1], (B, LE, CH), f32), 'token_type_ids': jax.random.randint(ks[2], (B, L), 0, 2, jnp.int32), 'position_ids': jnp.arange(L, dtype=jnp.int32)[None, :], 'ln_in_w': jnp.ones((H,), f32), 'ln_post_attn_w': jnp.ones((H,), f32), 'ln_post_cross_w': jnp.ones((H,), f32), 'v_qkv': jax.random.normal(ks[3], (H, 3 * H), f32) * s, 'l_qkv': jax.random.normal(ks[4], (H, 3 * H), f32) * s, 'v_dense': jax.random.normal(ks[5], (H, H), f32) * s, 'l_dense': jax.random.normal(ks[6], (H, H), f32) * s, 'cq_w': jax.random.normal(ks[7], (H, CC), f32) * s, 'ckv_w': jax.random.normal(ks[8], (CH, 2 * CC), f32) * s, 'cdense_w': jax.random.normal(ks[9], (CC, H), f32) * s, 'v_gate': jax.random.normal(ks[10], (H, I), f32) * s, 'v_up': jax.random.normal(ks[11], (H, I), f32) * s, 'v_down': jax.random.normal(ks[12], (I, H), f32) * s, 'l_gate': jax.random.normal(ks[13], (H, I), f32) * s, 'l_up': jax.random.normal(ks[14], (H, I), f32) * s, 'l_down': jax.random.normal(ks[15], (I, H), f32) * s}
    _L1_xattn_all = _L1_xattn_setup()
    _L1_xattn_in = {k: v for k, v in _L1_xattn_all.items() if k in ('ln_in_w', 'ln_post_attn_w', 'ln_post_cross_w', 'v_qkv', 'l_qkv', 'v_dense', 'l_dense', 'cq_w', 'ckv_w', 'cdense_w', 'v_gate', 'v_up', 'v_down', 'l_gate', 'l_up', 'l_down')}
    del _L1_xattn_all

    def _L2_xattn_setup():
        import jax, jax.numpy as jnp
        import numpy as np
        EPS = 1e-06

        def _rmsnorm(x, w):
            var = jnp.mean(jnp.square(x), axis=-1, keepdims=True)
            return x * jax.lax.rsqrt(var + EPS) * w
        key = jax.random.key(seed)
        ks = jax.random.split(key, 6)
        B, N, M = (4, 512, 256)
        d_model, memory_dim = (256, 128)
        hidden_states = jax.random.normal(ks[0], (B, N, d_model), dtype=jnp.float32)
        memory = jax.random.normal(ks[1], (B, M, memory_dim), dtype=jnp.float32)
        W_mem = jax.random.normal(ks[2], (d_model, memory_dim), dtype=jnp.float32) / np.sqrt(memory_dim)
        W_gate = jax.random.normal(ks[3], (d_model, 2 * d_model), dtype=jnp.float32) / np.sqrt(2 * d_model)
        b_gate = jax.random.normal(ks[4], (d_model,), dtype=jnp.float32) * 0.01
        norm_w = jnp.ones((d_model,), dtype=jnp.float32)
        return {'hidden_states': hidden_states, 'memory': memory, 'W_mem': W_mem, 'W_gate': W_gate, 'b_gate': b_gate, 'norm_w': norm_w}
    _L2_xattn_all = _L2_xattn_setup()
    _L2_xattn_in = {k: v for k, v in _L2_xattn_all.items() if k in ('W_mem', 'W_gate', 'b_gate', 'norm_w')}
    del _L2_xattn_all

    def _L3_xattn_setup():
        import jax, jax.numpy as jnp
        import numpy as np
        DIM = 256
        DIM_MEDIA = 128
        HEADS = 16
        DIM_HEAD = 64
        INNER = HEADS * DIM_HEAD
        FF_INNER = 4 * DIM
        B, N_TOK, N_LAT = (4, 256, 64)
        EPS = 1e-05

        def layernorm(x, g, b):
            mu = jnp.mean(x, axis=-1, keepdims=True)
            var = jnp.var(x, axis=-1, keepdims=True)
            return (x - mu) * jax.lax.rsqrt(var + EPS) * g + b
        key = jax.random.key(seed)
        ks = jax.random.split(key, 12)
        x = jax.random.normal(ks[0], (B, N_TOK, DIM), dtype=jnp.float32)
        media = jax.random.normal(ks[1], (B, N_LAT, DIM_MEDIA), dtype=jnp.float32)
        media_mask = jax.random.randint(ks[2], (B, N_LAT), 0, 2).astype(bool)
        media_mask = media_mask.at[:, 0].set(True)
        s = lambda d: 1.0 / np.sqrt(d)
        Wq = jax.random.normal(ks[3], (DIM, INNER), dtype=jnp.float32) * s(DIM)
        Wkv = jax.random.normal(ks[4], (DIM_MEDIA, 2 * INNER), dtype=jnp.float32) * s(DIM_MEDIA)
        Wo = jax.random.normal(ks[5], (INNER, DIM), dtype=jnp.float32) * s(INNER)
        W1 = jax.random.normal(ks[6], (DIM, FF_INNER), dtype=jnp.float32) * s(DIM)
        W2 = jax.random.normal(ks[7], (FF_INNER, DIM), dtype=jnp.float32) * s(FF_INNER)
        return {'x': x, 'media': media, 'media_mask': media_mask, 'ln_q_g': jnp.ones((DIM,), jnp.float32), 'ln_q_b': jnp.zeros((DIM,), jnp.float32), 'Wq': Wq, 'Wkv': Wkv, 'Wo': Wo, 'attn_gate': jax.random.normal(ks[8], (1,), jnp.float32) * 0.5, 'ln_ff_g': jnp.ones((DIM,), jnp.float32), 'ln_ff_b': jnp.zeros((DIM,), jnp.float32), 'W1': W1, 'W2': W2, 'ff_gate': jax.random.normal(ks[9], (1,), jnp.float32) * 0.5}
    _L3_xattn_all = _L3_xattn_setup()
    _L3_xattn_in = {k: v for k, v in _L3_xattn_all.items() if k in ('ln_q_g', 'ln_q_b', 'Wq', 'Wkv', 'Wo', 'attn_gate', 'ln_ff_g', 'ln_ff_b', 'W1', 'W2', 'ff_gate')}
    del _L3_xattn_all
    return {'x': x, 'ctx_1024': ctx_1024, 'pos_1xS': pos_1xS, 'mask_BxS2_bk0': mask_BxS2_bk0, 'mask_BxS_ik0': mask_BxS_ik0, 'L0_xattn_ln_q_g': _L0_xattn_in['ln_q_g'], 'L0_xattn_ln_q_b': _L0_xattn_in['ln_q_b'], 'L0_xattn_Wq': _L0_xattn_in['Wq'], 'L0_xattn_Wkv': _L0_xattn_in['Wkv'], 'L0_xattn_Wo': _L0_xattn_in['Wo'], 'L0_xattn_attn_gate': _L0_xattn_in['attn_gate'], 'L0_xattn_ln_ff_g': _L0_xattn_in['ln_ff_g'], 'L0_xattn_ln_ff_b': _L0_xattn_in['ln_ff_b'], 'L0_xattn_W1': _L0_xattn_in['W1'], 'L0_xattn_W2': _L0_xattn_in['W2'], 'L0_xattn_ff_gate': _L0_xattn_in['ff_gate'], 'L1_xattn_ln_in_w': _L1_xattn_in['ln_in_w'], 'L1_xattn_ln_post_attn_w': _L1_xattn_in['ln_post_attn_w'], 'L1_xattn_ln_post_cross_w': _L1_xattn_in['ln_post_cross_w'], 'L1_xattn_v_qkv': _L1_xattn_in['v_qkv'], 'L1_xattn_l_qkv': _L1_xattn_in['l_qkv'], 'L1_xattn_v_dense': _L1_xattn_in['v_dense'], 'L1_xattn_l_dense': _L1_xattn_in['l_dense'], 'L1_xattn_cq_w': _L1_xattn_in['cq_w'], 'L1_xattn_ckv_w': _L1_xattn_in['ckv_w'], 'L1_xattn_cdense_w': _L1_xattn_in['cdense_w'], 'L1_xattn_v_gate': _L1_xattn_in['v_gate'], 'L1_xattn_v_up': _L1_xattn_in['v_up'], 'L1_xattn_v_down': _L1_xattn_in['v_down'], 'L1_xattn_l_gate': _L1_xattn_in['l_gate'], 'L1_xattn_l_up': _L1_xattn_in['l_up'], 'L1_xattn_l_down': _L1_xattn_in['l_down'], 'L2_xattn_W_mem': _L2_xattn_in['W_mem'], 'L2_xattn_W_gate': _L2_xattn_in['W_gate'], 'L2_xattn_b_gate': _L2_xattn_in['b_gate'], 'L2_xattn_norm_w': _L2_xattn_in['norm_w'], 'L3_xattn_ln_q_g': _L3_xattn_in['ln_q_g'], 'L3_xattn_ln_q_b': _L3_xattn_in['ln_q_b'], 'L3_xattn_Wq': _L3_xattn_in['Wq'], 'L3_xattn_Wkv': _L3_xattn_in['Wkv'], 'L3_xattn_Wo': _L3_xattn_in['Wo'], 'L3_xattn_attn_gate': _L3_xattn_in['attn_gate'], 'L3_xattn_ln_ff_g': _L3_xattn_in['ln_ff_g'], 'L3_xattn_ln_ff_b': _L3_xattn_in['ln_ff_b'], 'L3_xattn_W1': _L3_xattn_in['W1'], 'L3_xattn_W2': _L3_xattn_in['W2'], 'L3_xattn_ff_gate': _L3_xattn_in['ff_gate']}

def reference(x, ctx_1024, pos_1xS, mask_BxS2_bk0, mask_BxS_ik0, L0_xattn_ln_q_g, L0_xattn_ln_q_b, L0_xattn_Wq, L0_xattn_Wkv, L0_xattn_Wo, L0_xattn_attn_gate, L0_xattn_ln_ff_g, L0_xattn_ln_ff_b, L0_xattn_W1, L0_xattn_W2, L0_xattn_ff_gate, L1_xattn_ln_in_w, L1_xattn_ln_post_attn_w, L1_xattn_ln_post_cross_w, L1_xattn_v_qkv, L1_xattn_l_qkv, L1_xattn_v_dense, L1_xattn_l_dense, L1_xattn_cq_w, L1_xattn_ckv_w, L1_xattn_cdense_w, L1_xattn_v_gate, L1_xattn_v_up, L1_xattn_v_down, L1_xattn_l_gate, L1_xattn_l_up, L1_xattn_l_down, L2_xattn_W_mem, L2_xattn_W_gate, L2_xattn_b_gate, L2_xattn_norm_w, L3_xattn_ln_q_g, L3_xattn_ln_q_b, L3_xattn_Wq, L3_xattn_Wkv, L3_xattn_Wo, L3_xattn_attn_gate, L3_xattn_ln_ff_g, L3_xattn_ln_ff_b, L3_xattn_W1, L3_xattn_W2, L3_xattn_ff_gate):
    import jax
    import jax.numpy as jnp

    def _L0_xattn_ref(x, media, media_mask, ln_q_g, ln_q_b, Wq, Wkv, Wo, attn_gate, ln_ff_g, ln_ff_b, W1, W2, ff_gate):
        import jax, jax.numpy as jnp
        import numpy as np
        DIM = 256
        DIM_MEDIA = 128
        HEADS = 16
        DIM_HEAD = 64
        INNER = HEADS * DIM_HEAD
        FF_INNER = 4 * DIM
        B, N_TOK, N_LAT = (4, 256, 64)
        EPS = 1e-05

        def layernorm(x, g, b):
            mu = jnp.mean(x, axis=-1, keepdims=True)
            var = jnp.var(x, axis=-1, keepdims=True)
            return (x - mu) * jax.lax.rsqrt(var + EPS) * g + b
        scale = DIM_HEAD ** (-0.5)
        qn = layernorm(x, ln_q_g, ln_q_b)
        q = qn @ Wq * scale
        kv = media @ Wkv
        k, v = jnp.split(kv, 2, axis=-1)
        split_heads = lambda t: t.reshape(t.shape[0], t.shape[1], HEADS, DIM_HEAD).transpose(0, 2, 1, 3)
        q, k, v = (split_heads(q), split_heads(k), split_heads(v))
        sim = jnp.einsum('bhid,bhjd->bhij', q, k)
        neg_inf = jnp.finfo(sim.dtype).min
        sim = jnp.where(media_mask[:, None, None, :], sim, neg_inf)
        attn = jax.nn.softmax(sim, axis=-1)
        out = jnp.einsum('bhij,bhjd->bhid', attn, v)
        out = out.transpose(0, 2, 1, 3).reshape(x.shape[0], x.shape[1], INNER)
        attn_out = out @ Wo
        x = x + jnp.tanh(attn_gate) * attn_out
        h = layernorm(x, ln_ff_g, ln_ff_b)
        h = jax.nn.gelu(h @ W1, approximate=False) @ W2
        x = x + jnp.tanh(ff_gate) * h
        return x

    def _L1_xattn_ref(hidden_states, encoder_outputs, token_type_ids, position_ids, ln_in_w, ln_post_attn_w, ln_post_cross_w, v_qkv, l_qkv, v_dense, l_dense, cq_w, ckv_w, cdense_w, v_gate, v_up, v_down, l_gate, l_up, l_down):
        import jax, jax.numpy as jnp
        import numpy as np
        H = 256
        NH = 16
        HD = H // NH
        CH = 128
        CC = 128
        CHD = CC // NH
        I = 688
        B = 2
        L = 256
        LE = 128
        EPS = 1e-06

        def rms_norm(x, w):
            xf = x.astype(jnp.float32)
            var = jnp.mean(xf * xf, axis=-1, keepdims=True)
            return (w * (xf * jax.lax.rsqrt(var + EPS))).astype(x.dtype)

        def expert_mask(tt):
            vm = jnp.zeros(tt.shape, dtype=bool)
            vm = vm.at[:, :-1].set((tt[:, :-1] == 1) & (tt[:, 1:] == 1))
            return vm

        def rotate_half(x):
            d = x.shape[-1] // 2
            return jnp.concatenate([-x[..., d:], x[..., :d]], axis=-1)

        def apply_rotary(q, k, position_ids, seq_len):
            inv = 1.0 / 10000.0 ** (jnp.arange(0, HD, 2, dtype=jnp.float32) / HD)
            t = jnp.arange(seq_len, dtype=jnp.float32)
            freqs = jnp.outer(t, inv)
            emb = jnp.concatenate([freqs, freqs], axis=-1)
            cos = jnp.cos(emb)[position_ids][:, None].astype(q.dtype)
            sin = jnp.sin(emb)[position_ids][:, None].astype(q.dtype)
            return (q * cos + rotate_half(q) * sin, k * cos + rotate_half(k) * sin)

        def sdpa(q, k, v, causal):
            scale = 1.0 / np.sqrt(q.shape[-1])
            scores = jnp.einsum('bhqd,bhkd->bhqk', q * scale, k)
            if causal:
                mask = jnp.tril(jnp.ones((q.shape[-2], k.shape[-2]), dtype=bool))
                scores = jnp.where(mask, scores, jnp.finfo(jnp.float32).min)
            p = jax.nn.softmax(scores.astype(jnp.float32), axis=-1).astype(q.dtype)
            return jnp.einsum('bhqk,bhkd->bhqd', p, v)

        def heads(x, nh, hd):
            b, l, _ = x.shape
            return x.reshape(b, l, nh, hd).transpose(0, 2, 1, 3)
        b, l, _ = hidden_states.shape
        vm = expert_mask(token_type_ids)[..., None]
        residual = hidden_states
        x = rms_norm(hidden_states, ln_in_w)
        mixed = jnp.where(vm, x @ v_qkv, x @ l_qkv)
        q, k, v = jnp.split(mixed, 3, axis=-1)
        q, k, v = (heads(q, NH, HD), heads(k, NH, HD), heads(v, NH, HD))
        q, k = apply_rotary(q, k, position_ids, l)
        ctx = sdpa(q, k, v, causal=True)
        ctx = ctx.transpose(0, 2, 1, 3).reshape(b, l, H)
        attn_out = jnp.where(vm, ctx @ v_dense, ctx @ l_dense)
        hidden_states = residual + attn_out
        ci = rms_norm(hidden_states, ln_post_cross_w)
        cq = heads(ci @ cq_w, NH, CHD)
        ckv = encoder_outputs @ ckv_w
        ck, cv = jnp.split(ckv, 2, axis=-1)
        ck, cv = (heads(ck, NH, CHD), heads(cv, NH, CHD))
        cctx = sdpa(cq, ck, cv, causal=False)
        cctx = cctx.transpose(0, 2, 1, 3).reshape(b, l, CC)
        hidden_states = hidden_states + cctx @ cdense_w
        mi = rms_norm(hidden_states, ln_post_attn_w)
        v_out = jax.nn.silu(mi @ v_gate) * (mi @ v_up) @ v_down
        l_out = jax.nn.silu(mi @ l_gate) * (mi @ l_up) @ l_down
        hidden_states = hidden_states + jnp.where(vm, v_out, l_out)
        return hidden_states

    def _L2_xattn_ref(hidden_states, memory, W_mem, W_gate, b_gate, norm_w):
        import jax, jax.numpy as jnp
        import numpy as np
        EPS = 1e-06

        def _rmsnorm(x, w):
            var = jnp.mean(jnp.square(x), axis=-1, keepdims=True)
            return x * jax.lax.rsqrt(var + EPS) * w
        D = hidden_states.shape[-1]
        memory_proj = jnp.einsum('bme,de->bmd', memory, W_mem)
        scores = jnp.einsum('bnd,bmd->bnm', hidden_states, memory_proj) / jnp.sqrt(jnp.float32(D))
        attn = jax.nn.softmax(scores, axis=-1)
        memory_context = jnp.einsum('bnm,bmd->bnd', attn, memory_proj)
        gate_input = jnp.concatenate([hidden_states, memory_context], axis=-1)
        gate = jax.nn.sigmoid(jnp.einsum('bnf,df->bnd', gate_input, W_gate) + b_gate)
        fused = hidden_states + gate * memory_context
        return _rmsnorm(fused, norm_w)

    def _L3_xattn_ref(x, media, media_mask, ln_q_g, ln_q_b, Wq, Wkv, Wo, attn_gate, ln_ff_g, ln_ff_b, W1, W2, ff_gate):
        import jax, jax.numpy as jnp
        import numpy as np
        DIM = 256
        DIM_MEDIA = 128
        HEADS = 16
        DIM_HEAD = 64
        INNER = HEADS * DIM_HEAD
        FF_INNER = 4 * DIM
        B, N_TOK, N_LAT = (4, 256, 64)
        EPS = 1e-05

        def layernorm(x, g, b):
            mu = jnp.mean(x, axis=-1, keepdims=True)
            var = jnp.var(x, axis=-1, keepdims=True)
            return (x - mu) * jax.lax.rsqrt(var + EPS) * g + b
        scale = DIM_HEAD ** (-0.5)
        qn = layernorm(x, ln_q_g, ln_q_b)
        q = qn @ Wq * scale
        kv = media @ Wkv
        k, v = jnp.split(kv, 2, axis=-1)
        split_heads = lambda t: t.reshape(t.shape[0], t.shape[1], HEADS, DIM_HEAD).transpose(0, 2, 1, 3)
        q, k, v = (split_heads(q), split_heads(k), split_heads(v))
        sim = jnp.einsum('bhid,bhjd->bhij', q, k)
        neg_inf = jnp.finfo(sim.dtype).min
        sim = jnp.where(media_mask[:, None, None, :], sim, neg_inf)
        attn = jax.nn.softmax(sim, axis=-1)
        out = jnp.einsum('bhij,bhjd->bhid', attn, v)
        out = out.transpose(0, 2, 1, 3).reshape(x.shape[0], x.shape[1], INNER)
        attn_out = out @ Wo
        x = x + jnp.tanh(attn_gate) * attn_out
        h = layernorm(x, ln_ff_g, ln_ff_b)
        h = jax.nn.gelu(h @ W1, approximate=False) @ W2
        x = x + jnp.tanh(ff_gate) * h
        return x
    x = _L0_xattn_ref(x, ctx_1024, mask_BxS2_bk0, L0_xattn_ln_q_g, L0_xattn_ln_q_b, L0_xattn_Wq, L0_xattn_Wkv, L0_xattn_Wo, L0_xattn_attn_gate, L0_xattn_ln_ff_g, L0_xattn_ln_ff_b, L0_xattn_W1, L0_xattn_W2, L0_xattn_ff_gate)
    x = _L1_xattn_ref(x, ctx_1024, mask_BxS_ik0, pos_1xS, L1_xattn_ln_in_w, L1_xattn_ln_post_attn_w, L1_xattn_ln_post_cross_w, L1_xattn_v_qkv, L1_xattn_l_qkv, L1_xattn_v_dense, L1_xattn_l_dense, L1_xattn_cq_w, L1_xattn_ckv_w, L1_xattn_cdense_w, L1_xattn_v_gate, L1_xattn_v_up, L1_xattn_v_down, L1_xattn_l_gate, L1_xattn_l_up, L1_xattn_l_down)
    x = _L2_xattn_ref(x, ctx_1024, L2_xattn_W_mem, L2_xattn_W_gate, L2_xattn_b_gate, L2_xattn_norm_w)
    x = _L3_xattn_ref(x, ctx_1024, mask_BxS2_bk0, L3_xattn_ln_q_g, L3_xattn_ln_q_b, L3_xattn_Wq, L3_xattn_Wkv, L3_xattn_Wo, L3_xattn_attn_gate, L3_xattn_ln_ff_g, L3_xattn_ln_ff_b, L3_xattn_W1, L3_xattn_W2, L3_xattn_ff_gate)
    return x

_drawn_inputs = setup_inputs


def setup_inputs(seed=0):
    import zlib

    import numpy as np

    out = dict(_drawn_inputs(seed))
    spreads = {'L0_xattn_ln_q_g': (1.0, 0.6),
     'L0_xattn_ln_q_b': (0.0, 0.8),
     'L0_xattn_ln_ff_g': (1.0, 0.6),
     'L0_xattn_ln_ff_b': (0.0, 0.8),
     'L1_xattn_ln_in_w': (1.0, 0.6),
     'L1_xattn_ln_post_attn_w': (1.0, 0.6),
     'L1_xattn_ln_post_cross_w': (1.0, 0.6),
     'L2_xattn_norm_w': (1.0, 0.2),
     'L3_xattn_ln_q_g': (1.0, 0.6),
     'L3_xattn_ln_q_b': (0.0, 0.8),
     'L3_xattn_ln_ff_g': (1.0, 0.6),
     'L3_xattn_ln_ff_b': (0.0, 0.8)}
    factors = {'L0_xattn_W1': 2.688,
     'L1_xattn_v_qkv': 8.0,
     'L1_xattn_v_dense': 8.0,
     'L1_xattn_l_dense': 2.781,
     'L1_xattn_cq_w': 60.633,
     'L1_xattn_v_gate': 5.621,
     'L1_xattn_v_up': 5.545,
     'L1_xattn_v_down': 5.569,
     'L2_xattn_b_gate': 57.876,
     'L3_xattn_W1': 2.89}
    for name, (base, spread) in spreads.items():
        noise = np.random.default_rng([zlib.crc32(name.encode()), seed]).standard_normal(out[name].shape)
        drawn = base * np.exp(spread * noise) if base else spread * noise
        out[name] = jnp.asarray(drawn.astype(out[name].dtype))
    for name, factor in factors.items():
        out[name] = (out[name] * factor).astype(out[name].dtype)
    return out
```

```python
from contextlib import ExitStack

import concourse.bass as bass
from concourse import mybir

ALU = mybir.AluOpType
ACT = mybir.ActivationFunctionType
AX_X = mybir.AxisListType.X
F32 = mybir.dt.float32
I32 = mybir.dt.int32
U8 = mybir.dt.uint8

P = 128
B = 8
Q = 256
D = 256
C = 128
S = 1601
NT = B * Q // P
KT = (S + P - 1) // P
SP = KT * P
KLAST = S - (KT - 1) * P
BANK = 512
MASK_WORDS = (S + 3) // 4
NEG = 1e30
BIG = 3e38

SCORE_CHUNKS = [(c, min(BANK, S - c)) for c in range(0, S, BANK)]
TURN_GROUPS = [range(k, min(k + 4, KT)) for k in range(0, KT, 4)]


class Phase:

    def __init__(self, nc, name):
        self.nc, self.name, self.ctx, self.sems = nc, name, ExitStack(), []

    def __enter__(self):
        self.ctx.__enter__()
        return self

    def __exit__(self, *error):
        self.ctx.__exit__(*error)
        self.nc.clear_and_free_semaphores(self.sems)
        self.nc.all_engine_barrier()

    def sb(self, name, shape, dt=F32):
        return self.ctx.enter_context(self.nc.sbuf_tensor(f"{self.name}_{name}", shape, dt))

    def ps(self, name, shape, dt=F32):
        return self.ctx.enter_context(self.nc.psum_tensor(f"{self.name}_{name}", shape, dt))

    def sem(self, name):
        self.sems.append(self.nc.alloc_semaphore(f"{self.name}_{name}"))
        return self.sems[-1]

    def block(self):
        return self.ctx.enter_context(self.nc.Block())


def load_phase(nc, st, io):
    with Phase(nc, "load") as ph:
        loaded = ph.sem("loaded")
        block = ph.block()

        @block.sync
        def _(sp):
            sp.dma_start(st.ident[:, :], io["ident"]).then_inc(loaded, 16)
            sp.dma_start(st.X[:, :, :], io["x"].rearrange("(j p) d -> p j d", p=P)).then_inc(loaded, 16)
            sp.wait_ge(loaded, 32)


def store_phase(nc, st, io):
    with Phase(nc, "store") as ph:
        stored = ph.sem("stored")
        block = ph.block()

        @block.sync
        def _(sp):
            sp.dma_start(io["out"].rearrange("(j p) d -> p j d", p=P), st.X[:, :, :]).then_inc(stored, 16)
            sp.wait_ge(stored, 16)


def row_statistics(dve, chain, X, stats, rows, eps, rms, root_asked, root_taken):
    with dve.Fori(0, NT) as j:
        dve.bn_stats(stats[:, j, :], X[:, j, :]).then_inc(chain.sem, 1)
    chain.add(NT)
    chain.wait()
    even, odd = stats[:, :, 1], stats[:, :, 4]
    chain(dve.tensor_tensor(rows[:, 2, :], even, odd, ALU.add))
    chain(dve.tensor_tensor(rows[:, 3, :], even, odd, ALU.subtract))
    chain(dve.scalar_tensor_tensor(out=rows[:, 3, :], in0=rows[:, 3, :], scalar=0.25, in1=rows[:, 3, :],
                                   op0=ALU.mult, op1=ALU.mult))
    chain(dve.tensor_tensor(rows[:, 1, :], stats[:, :, 2], stats[:, :, 5], ALU.add))
    chain(dve.scalar_tensor_tensor(out=rows[:, 1, :], in0=rows[:, 1, :], scalar=1.0 / D, in1=rows[:, 3, :],
                                   op0=ALU.mult, op1=ALU.add))
    chain(dve.tensor_scalar(rows[:, 0, :], rows[:, 2, :], 0.5, None, ALU.mult))
    if rms:
        chain(dve.tensor_tensor(rows[:, 3, :], rows[:, 0, :], rows[:, 0, :], ALU.mult))
        chain(dve.tensor_tensor(rows[:, 1, :], rows[:, 1, :], rows[:, 3, :], ALU.add))
    dve.tensor_scalar(rows[:, 1, :], rows[:, 1, :], eps, None, ALU.add).then_inc(root_asked, 1)
    dve.wait_ge(root_taken, 1)
    chain(dve.reciprocal(rows[:, 1, :], rows[:, 1, :]))


class Chain:

    def __init__(self, eng, sem):
        self.eng, self.sem, self.count = eng, sem, 0

    def __call__(self, instruction):
        instruction.then_inc(self.sem, 1)
        self.count += 1
        self.wait()

    def add(self, n):
        self.count += n

    def wait(self):
        self.eng.wait_ge(self.sem, self.count)


def norm_phase(nc, st, io, name, kind, gain=None, shift=None, eps=0.0):
    with Phase(nc, name) as ph:
        xn = [ph.sb(f"xn{i}", [P, D]) for i in range(2)]
        stats = ph.sb("stats", [P, NT, 6])
        rows = ph.sb("rows", [P, 4, NT])
        gs = ph.sb("gs", [P, 2, 2])
        turned = [ph.ps(f"turned{i}", [P, BANK]) for i in range(2)]
        weights = ph.sem("weights")
        chain_sem = ph.sem("chain")
        root_asked = ph.sem("root_asked")
        root_taken = ph.sem("root_taken")
        xn_ready = ph.sem("xn_ready")
        turn_done = ph.sem("turn_done")
        copied = ph.sem("copied")
        block = ph.block()

        @block.sync
        def _(sp):
            if gain:
                sp.dma_start(gs[:, 0, :], io[gain]).then_inc(weights, 16)
            if shift:
                sp.dma_start(gs[:, 1, :], io[shift]).then_inc(weights, 16)

        @block.vector
        def _(dve):
            chain = Chain(dve, chain_sem)
            if kind != "plain":
                row_statistics(dve, chain, st.X, stats, rows, eps, kind == "rms", root_asked, root_taken)
            with dve.Fori(0, NT // 2) as i:
                for par in range(2):
                    j = 2 * i + par
                    dve.wait_ge(turn_done, j + 1)
                    if kind == "ln":
                        ins = dve.tensor_scalar(xn[par][:, :], st.X[:, j, :], rows[:, 0, bass.ds(j, 1)],
                                                rows[:, 1, bass.ds(j, 1)], ALU.subtract, ALU.mult)
                    elif kind == "rms":
                        ins = dve.tensor_scalar(xn[par][:, :], st.X[:, j, :], rows[:, 1, bass.ds(j, 1)], None,
                                                ALU.mult)
                    else:
                        ins = dve.tensor_copy(xn[par][:, :], st.X[:, j, :])
                    ins.then_inc(xn_ready, 1)

        @block.tensor
        def _(pe):
            pe.sem_inc(turn_done, 2)
            with pe.Fori(0, NT // 2) as i:
                for par in range(2):
                    pe.wait_ge(xn_ready, 2 * i + par + 1)
                    pe.wait_ge(copied, 2 * i + par + 1)
                    for f in range(2):
                        ins = pe.transpose(turned[par][:, f * P:(f + 1) * P], xn[par][:, f * P:(f + 1) * P],
                                           st.ident[:, :])
                    ins.then_inc(turn_done, 1)

        @block.scalar
        def _(act):
            act.sem_inc(copied, 2)
            if kind != "plain":
                act.wait_ge(root_asked, 1)
                act.activation(rows[:, 1, :], rows[:, 1, :], ACT.Sqrt).then_inc(root_taken, 1)
            if gain:
                act.wait_ge(weights, 32 if shift else 16)
            with act.Fori(0, NT // 2) as i:
                for par in range(2):
                    j = 2 * i + par
                    act.wait_ge(turn_done, j + 3)
                    for f in range(2):
                        to = st.XT[:, f, bass.ts(j, P)]
                        src = turned[par][:, f * P:(f + 1) * P]
                        if kind == "ln":
                            ins = act.activation(to, src, ACT.Identity, scale=gs[:, 0, f:f + 1],
                                                 bias=gs[:, 1, f:f + 1])
                        elif kind == "rms":
                            ins = act.activation(to, src, ACT.Copy, scale=gs[:, 0, f:f + 1])
                        else:
                            ins = act.activation(to, src, ACT.Copy)
                    ins.then_inc(copied, 1)


def weights_phase(nc, st, io, name, heads, width, scale, gate=None):
    with Phase(nc, name) as ph:
        wq = ph.sb("wq", [width, heads, D])
        wk = ph.sb("wk", [width, heads, C])
        wv = ph.sb("wv", [width, heads, C])
        wo = ph.sb("wo", [width, heads, D])
        g = ph.sb("g", [P, 2])
        prod = [ph.ps(f"prod{i}", [P, BANK]) for i in range(4)]
        loaded = ph.sem("loaded")
        gate_ready = ph.sem("gate_ready")
        made = ph.sem("made")
        copied = ph.sem("copied")
        block = ph.block()

        @block.sync
        def _(sp):
            for t, n in ((wq, "wq"), (wk, "wk"), (wv, "wv"), (wo, "wo")):
                sp.dma_start(t[:, :, :], io[f"{name}_{n}"]).then_inc(loaded, 16)
            if gate:
                sp.dma_start(g[:, 0:1], io[gate].to_broadcast([P, 1])).then_inc(loaded, 16)

        need = 80 if gate else 64
        groups = [("A", h, f) for h in range(0, heads, 4) for f in range(2)] + \
                 [("B", h, 0) for h in range(0, heads, 2)]

        @block.tensor
        def _(pe):
            pe.wait_ge(loaded, need)
            for n, (what, h0, f) in enumerate(groups):
                if n >= 4:
                    pe.wait_ge(copied, n - 3)
                for i in range(4 if what == "A" else 2):
                    h = h0 + i
                    if what == "A":
                        ins = pe.matmul(prod[n % 4][:, i * C:(i + 1) * C], wq[:, h, f * P:(f + 1) * P],
                                        wk[:, h, :], start=True, stop=True)
                    else:
                        ins = pe.matmul(prod[n % 4][:, i * D:(i + 1) * D], wv[:, h, :], wo[:, h, :],
                                        start=True, stop=True)
                ins.then_inc(made, 1)

        @block.scalar
        def _(act):
            if gate:
                act.wait_ge(loaded, need)
                act.activation(g[:, 1:2], g[:, 0:1], ACT.Tanh).then_inc(gate_ready, 1)

        @block.vector
        def _(dve):
            if gate:
                dve.wait_ge(gate_ready, 1)
            for n, (what, h, f) in enumerate(groups):
                dve.wait_ge(made, n + 1)
                if what == "A":
                    to, by = st.A[:, f, h * C:(h + 4) * C], scale
                else:
                    to, by = st.Bw[:, h * D:(h + 2) * D], (g[:, 1:2] if gate else 1.0)
                dve.tensor_scalar(to, prod[n % 4][:, :], by, None, ALU.mult).then_inc(copied, 1)


def attention_phase(nc, st, io, name, heads, masked, into_context=False):
    with Phase(nc, name) as ph:
        ctxT_in = ph.sb("ctxT_in", [P, S])
        ctx_in = ph.sb("ctx_in", [P, KT, C])
        ctxT = ph.sb("ctxT", [P, S])
        ctx = ph.sb("ctx", [P, KT, C])
        bias = ph.sb("bias", [P, S])
        mask_in = ph.sb("mask_in", [P, MASK_WORDS], I32)
        mask_bytes = mask_in[:, :].bitcast(U8)[:, 0:S]
        a_slot = [ph.sb(f"a_slot{i}", [P, 2, C]) for i in range(2)]
        g_sb = [ph.sb(f"g_sb{i}", [P, Q]) for i in range(2)]
        neg = [ph.sb(f"neg{i}", [P, S]) for i in range(2)]
        probs = [ph.sb(f"probs{i}", [P, S]) for i in range(2)]
        negmax = ph.sb("negmax", [P, 2])
        rowsum = ph.sb("rowsum", [P, 2, 2])
        inv = ph.sb("inv", [P, 2])
        pT = [ph.sb(f"pT{i}", [P, KT, Q]) for i in range(2)]
        u_sb = ph.sb("u_sb", [P, Q])
        ps_s = ph.ps("ps_s", [P, 4 * BANK])
        ps_t = [ph.ps(f"ps_t{i}", [P, BANK]) for i in range(2)]
        ps_gu = ph.ps("ps_gu", [P, BANK])
        ps_g, ps_u = ps_gu[:, 0:Q], ps_gu[:, Q:2 * Q]
        ps_o = ph.ps("ps_o", [P, 2, D])

        ctx_loaded = ph.sem("ctx_loaded")
        mask_loaded = ph.sem("mask_loaded")
        staged_out = ph.sem("staged_out")
        ctxT_ready = ph.sem("ctxT_ready")
        ctx_ready = ph.sem("ctx_ready")
        bias_ready = ph.sem("bias_ready")
        a_ready = ph.sem("a_ready")
        g_made = ph.sem("g_made")
        g_copied = ph.sem("g_copied")
        scored = ph.sem("scored")
        maxed = ph.sem("maxed")
        exped = ph.sem("exped")
        turned = ph.sem("turned")
        turn_act = ph.sem("turn_act")
        turn_dve = ph.sem("turn_dve")
        pv_done = ph.sem("pv_done")
        u_copied = ph.sem("u_copied")
        out_made = ph.sem("out_made")
        inverted = ph.sem("inverted")
        summed = ph.sem("summed")
        dve_passed = ph.sem("dve_passed")
        pool_passed = ph.sem("pool_passed")
        block = ph.block()

        NG = len(TURN_GROUPS)

        def drive(eng, first, step, last):
            with eng.Fori(0, B) as b:
                first(b)
                if heads > 1:
                    with eng.Fori(0, (heads - 2) // 2) as k:
                        step(b, 2 * k + 1, 1, False)
                        step(b, 2 * k + 2, 0, False)
                    step(b, heads - 1, 1, True)
                last(b)

        @block.sync
        def _(sp):
            with sp.Fori(0, B) as b:
                sp.wait_ge(staged_out, 3 * b + 3)
                sp.dma_start(ctxT_in[:, :], io["ctxT"][bass.ds(b, 1), :, :].rearrange("a c s -> (a c) s")).then_inc(ctx_loaded, 16)
                sp.dma_start(ctx_in[:, :, :], io["ctx"][bass.ds(b, 1), :, :, :].rearrange("a p k c -> (a p) k c")).then_inc(ctx_loaded, 16)
                if masked:
                    sp.dma_start(mask_in[:, :], io["mask"][bass.ds(b, 1), :].to_broadcast([P, MASK_WORDS])).then_inc(mask_loaded, 16)

        @block.gpsimd
        def _(pool):
            pool.sem_inc(staged_out, 3)
            if not masked:
                pool.memset(bias[:, :], 0.0).then_inc(bias_ready, 1)

            def slot(b, h, par):
                n = b * heads + h
                pool.wait_ge(g_made, n + 1)
                pool.sem_inc(pool_passed, 1)
                pool.tensor_copy(a_slot[par][:, :, :], st.A[:, :, bass.ts(h, C)]).then_inc(a_ready, 1)

            def first(b):
                pool.wait_ge(ctx_loaded, 32 * b + 32)
                pool.wait_ge(scored, 2 * heads * b + 1)
                pool.sem_inc(pool_passed, 1)
                pool.tensor_copy(ctxT[:, :], ctxT_in[:, :]).then_inc(ctxT_ready, 1)
                pool.wait_ge(ctxT_ready, b + 1)
                pool.sem_inc(staged_out, 1)
                if masked:
                    pool.wait_ge(mask_loaded, 16 * b + 16)
                    pool.wait_ge(maxed, 2 * heads * b + 1)
                    pool.sem_inc(pool_passed, 1)
                    pool.tensor_scalar(bias[:, :], mask_bytes, NEG, -NEG, ALU.mult, ALU.add).then_inc(bias_ready, 1)
                    pool.wait_ge(bias_ready, b + 1)
                pool.sem_inc(staged_out, 1)
                pool.wait_ge(pv_done, heads * b + 1)
                pool.sem_inc(pool_passed, 1)
                pool.tensor_copy(ctx[:, :, :], ctx_in[:, :, :]).then_inc(ctx_ready, 1)
                pool.wait_ge(ctx_ready, b + 1)
                pool.sem_inc(staged_out, 1)
                slot(b, 0, 0)
                if heads > 1:
                    slot(b, 1, 1)

            def step(b, h, par, at_end):
                if not at_end:
                    slot(b, h + 1, 1 - par)

            with pool.Fori(0, B) as b:
                first(b)
                if heads > 1:
                    with pool.Fori(0, (heads - 2) // 2) as k:
                        step(b, 2 * k + 1, 1, False)
                        step(b, 2 * k + 2, 0, False)

        @block.tensor
        def _(pe):
            pe.sem_inc(g_made, 2)
            pe.sem_inc(scored, 1)
            pe.sem_inc(pv_done, 1)
            pe.sem_inc(turned, 2 * NG)

            def scores(n, par, qt):
                pe.wait_ge(g_copied, n + 2)
                pe.wait_ge(maxed, 2 * n + qt + 1)
                for c, w in SCORE_CHUNKS:
                    ins = pe.matmul(ps_s[:, c:c + w], g_sb[par][:, qt * P:(qt + 1) * P], ctxT[:, c:c + w],
                                    start=True, stop=True)
                ins.then_inc(scored, 1)

            def make_g(b, n, par):
                pe.wait_ge(a_ready, n + 1)
                pe.wait_ge(g_copied, n + 1)
                for f in range(2):
                    ins = pe.matmul(ps_g, a_slot[par][:, f, :], st.XT[:, f, bass.ts(b, Q)],
                                    start=(f == 0), stop=(f == 1))
                ins.then_inc(g_made, 1)

            def turn(n, qt):
                pe.wait_ge(exped, 2 * n + qt + 3)
                for g, tiles in enumerate(TURN_GROUPS):
                    pe.wait_ge(turn_dve if g % 2 else turn_act, 4 * n + 2 * qt + g // 2 + 1)
                    for k in tiles:
                        w = min(P, S - k * P)
                        ins = pe.transpose(ps_t[g % 2][0:w, (k % 4) * P:(k % 4 + 1) * P],
                                           probs[qt][:, k * P:k * P + w], st.ident[:, :])
                    ins.then_inc(turned, 1)

            def pv(n, par):
                pe.wait_ge(turn_act, 4 * n + 5)
                pe.wait_ge(turn_dve, 4 * n + 5)
                for k in range(KT):
                    w = min(P, S - k * P)
                    ins = pe.matmul(ps_u, ctx[0:w, k, :], pT[par][0:w, k, :], start=(k == 0), stop=(k == KT - 1))
                ins.then_inc(pv_done, 1)

            def output(n, h):
                pe.wait_ge(u_copied, n + 1)
                pe.wait_ge(summed, n + 1)
                for qt in range(2):
                    ins = pe.matmul(ps_o[:, qt, :], u_sb[:, qt * P:(qt + 1) * P], st.Bw[:, bass.ts(h, D)],
                                    start=True, stop=True)
                ins.then_inc(out_made, 1)

            def first(b):
                n = b * heads
                make_g(b, n, 0)
                pe.wait_ge(ctxT_ready, b + 1)
                scores(n, 0, 0)
                if heads > 1:
                    make_g(b, n + 1, 1)
                scores(n, 0, 1)
                turn(n, 0)

            def step(b, h, par, at_end):
                n = b * heads + h
                scores(n, par, 0)
                if not at_end:
                    make_g(b, n + 1, 1 - par)
                    turn(n - 1, 1)
                    pe.wait_ge(g_copied, n + 3)
                else:
                    turn(n - 1, 1)
                pe.wait_ge(ctx_ready, b + 1)
                pv(n - 1, 1 - par)
                scores(n, par, 1)
                output(n - 1, h - 1)
                turn(n, 0)

            def last(b):
                n = b * heads + heads - 1
                turn(n, 1)
                pe.wait_ge(ctx_ready, b + 1)
                pv(n, (heads - 1) % 2)
                output(n, heads - 1)

            drive(pe, first, step, last)

        @block.vector
        def _(dve):
            dve.sem_inc(maxed, 1)
            dve.sem_inc(turn_dve, 1)
            dve.sem_inc(summed, 1)

            def rowmax(n, qt):
                dve.wait_ge(scored, 2 * n + qt + 2)
                dve.wait_ge(exped, 2 * n + qt + 1)
                dve.sem_inc(dve_passed, 1)
                dve.tensor_tensor_reduce(out=neg[qt][:, :], in0=ps_s[:, 0:S], in1=bias[:, :], scale=-1.0, scalar=BIG,
                                         op0=ALU.add, op1=ALU.min, accum_out=negmax[:, qt:qt + 1]).then_inc(maxed, 1)

            def copy_turned(n, qt, par):
                for g in (1, 3):
                    tiles = TURN_GROUPS[g]
                    w = min(P, S - tiles[0] * P)
                    dve.wait_ge(turned, NG * (2 * n + qt) + g + 1 + 2 * NG)
                    dve.tensor_copy(pT[par][0:w, tiles[0]:tiles[-1] + 1, qt * P:(qt + 1) * P],
                                    ps_t[1][0:w, 0:P * len(tiles)].rearrange("p (k q) -> p k q", q=P)).then_inc(turn_dve, 1)

            def accumulate(b, n, par):
                dve.wait_ge(exped, 2 * n + 4)
                dve.wait_ge(summed, n + 1)
                dve.reciprocal(inv[:, :], rowsum[:, par, :]).then_inc(inverted, 1)
                dve.wait_ge(inverted, n + 1)
                dve.wait_ge(out_made, n + 1)
                for qt in range(2):
                    if into_context:
                        ins = dve.tensor_scalar(st.MC[:, 2 * b + qt, :], ps_o[:, qt, :], inv[:, qt:qt + 1], None, ALU.mult)
                    else:
                        ins = dve.scalar_tensor_tensor(out=st.X[:, 2 * b + qt, :], in0=ps_o[:, qt, :],
                                                       scalar=inv[:, qt:qt + 1], in1=st.X[:, 2 * b + qt, :],
                                                       op0=ALU.mult, op1=ALU.add)
                ins.then_inc(summed, 1)

            def first(b):
                n = b * heads
                dve.wait_ge(bias_ready, b + 1 if masked else 1)
                rowmax(n, 0)
                rowmax(n, 1)
                copy_turned(n, 0, 0)

            def step(b, h, par, at_end):
                n = b * heads + h
                rowmax(n, 0)
                copy_turned(n - 1, 1, 1 - par)
                rowmax(n, 1)
                accumulate(b, n - 1, 1 - par)
                copy_turned(n, 0, par)

            def last(b):
                n = b * heads + heads - 1
                copy_turned(n, 1, (heads - 1) % 2)
                accumulate(b, n, (heads - 1) % 2)

            drive(dve, first, step, last)

        @block.scalar
        def _(act):
            act.sem_inc(g_copied, 1)
            act.sem_inc(exped, 2)
            act.sem_inc(turn_act, 1)

            def copy_g(n, par):
                act.wait_ge(g_made, n + 3)
                act.activation(g_sb[par][:, :], ps_g, ACT.Copy).then_inc(g_copied, 1)

            def exponential(n, par, qt):
                act.wait_ge(maxed, 2 * n + qt + 2)
                act.wait_ge(turned, NG * (2 * n + qt + 1))
                act.activation(probs[qt][:, :], neg[qt][:, :], ACT.Exp, scale=-1.0, bias=negmax[:, qt:qt + 1],
                               accum_out=rowsum[:, par, qt:qt + 1]).then_inc(exped, 1)

            def copy_turned(n, qt, par):
                for g in (0, 2):
                    tiles = TURN_GROUPS[g]
                    act.wait_ge(turned, NG * (2 * n + qt) + g + 1 + 2 * NG)
                    act.activation(pT[par][:, tiles[0]:tiles[-1] + 1, qt * P:(qt + 1) * P],
                                   ps_t[0][:, :].rearrange("p (k q) -> p k q", q=P), ACT.Copy).then_inc(turn_act, 1)

            def copy_u(n):
                act.wait_ge(pv_done, n + 2)
                act.activation(u_sb[:, :], ps_u, ACT.Copy).then_inc(u_copied, 1)

            def first(b):
                n = b * heads
                copy_g(n, 0)
                if heads > 1:
                    copy_g(n + 1, 1)
                exponential(n, 0, 0)
                copy_turned(n, 0, 0)
                exponential(n, 0, 1)

            def step(b, h, par, at_end):
                n = b * heads + h
                if not at_end:
                    copy_g(n + 1, 1 - par)
                copy_turned(n - 1, 1, 1 - par)
                exponential(n, par, 0)
                copy_u(n - 1)
                copy_turned(n, 0, par)
                exponential(n, par, 1)

            def last(b):
                n = b * heads + heads - 1
                copy_turned(n, 1, (heads - 1) % 2)
                copy_u(n)

            drive(act, first, step, last)


def mlp_phase(nc, st, io, name, gate):
    F = 4 * D
    FT = F // P
    TC = BANK
    NC = B * Q // TC
    with Phase(nc, name) as ph:
        w1 = ph.sb("w1", [P, 2, F])
        w2 = ph.sb("w2", [P, FT, D])
        g = ph.sb("g", [P, 2])
        hid = [ph.sb(f"hid{i}", [P, FT, TC]) for i in range(2)]
        ps_h = [ph.ps(f"ps_h{i}", [P, TC]) for i in range(2)]
        ps_y = [ph.ps(f"ps_y{i}", [P, D]) for i in range(2)]
        loaded = ph.sem("loaded")
        gate_ready = ph.sem("gate_ready")
        hid_made = ph.sem("hid_made")
        hid_ready = ph.sem("hid_ready")
        y_made = ph.sem("y_made")
        y_added = ph.sem("y_added")
        block = ph.block()

        @block.sync
        def _(sp):
            sp.dma_start(w1[:, :, :], io[f"{name}_w1"]).then_inc(loaded, 16)
            sp.dma_start(w2[:, :, :], io[f"{name}_w2"]).then_inc(loaded, 16)
            sp.dma_start(g[:, 0:1], io[gate].to_broadcast([P, 1])).then_inc(loaded, 16)

        @block.tensor
        def _(pe):
            pe.wait_ge(loaded, 48)
            with pe.Fori(0, NC // 2) as i:
                for par in range(2):
                    c = 2 * i + par
                    for t in range(FT):
                        m = c * FT + t
                        pe.wait_ge(hid_ready, m + 1)
                        for f in range(2):
                            ins = pe.matmul(ps_h[t % 2][:, :], w1[:, f, t * P:(t + 1) * P], st.XT[:, f, bass.ts(c, TC)],
                                            start=(f == 0), stop=(f == 1))
                        ins.then_inc(hid_made, 1)
                for par in range(2):
                    c = 2 * i + par
                    pe.wait_ge(hid_ready, FT * (c + 1) + 2)
                    for r in range(TC // P):
                        pe.wait_ge(y_added, 4 * c + r + 1)
                        for t in range(FT):
                            ins = pe.matmul(ps_y[r % 2][:, :], hid[par][:, t, r * P:(r + 1) * P], w2[:, t, :],
                                            start=(t == 0), stop=(t == FT - 1))
                        ins.then_inc(y_made, 1)

        @block.scalar
        def _(act):
            act.sem_inc(hid_ready, 2)
            act.wait_ge(loaded, 48)
            act.activation(g[:, 1:2], g[:, 0:1], ACT.Tanh).then_inc(gate_ready, 1)
            with act.Fori(0, NC // 2) as i:
                for par in range(2):
                    for t in range(FT):
                        act.wait_ge(hid_made, (2 * i + par) * FT + t + 1)
                        act.activation(hid[par][:, t, :], ps_h[t % 2][:, :], ACT.Gelu).then_inc(hid_ready, 1)

        @block.vector
        def _(dve):
            dve.sem_inc(y_added, 2)
            dve.wait_ge(gate_ready, 1)
            with dve.Fori(0, NC) as c:
                for r in range(TC // P):
                    j = 4 * c + r
                    dve.wait_ge(y_made, j + 1)
                    dve.scalar_tensor_tensor(out=st.X[:, j, :], in0=ps_y[r % 2][:, :], scalar=g[:, 1:2],
                                             in1=st.X[:, j, :], op0=ALU.mult, op1=ALU.add).then_inc(y_added, 1)


def expert_masks_phase(nc, st, io):
    with Phase(nc, "masks") as ph:
        types = ph.sb("types", [P, B, Q], I32)
        is_one = ph.sb("is_one", [P, B, Q])
        pos_in = ph.sb("pos_in", [P, Q], I32)
        pos = ph.sb("pos", [P, 2, Q])
        rows = ph.sb("rows", [P, 2])
        onehot = ph.sb("onehot", [P, 2, Q])
        table = ph.sb("table", [P, 2, 24])
        picked = ph.ps("picked", [P, 2, 24])
        loaded = ph.sem("loaded")
        chain_sem = ph.sem("chain")
        onehot_ready = ph.sem("onehot_ready")
        picks_done = ph.sem("picks_done")
        block = ph.block()

        @block.sync
        def _(sp):
            sp.dma_start(types[:, :, :], io["types"].rearrange("b q -> (b q)").unsqueeze(0).to_broadcast([P, B * Q]).rearrange("p (b q) -> p b q", b=B)).then_inc(loaded, 16)
            sp.dma_start(pos_in[:, :], io["positions"].to_broadcast([P, Q])).then_inc(loaded, 16)
            sp.dma_start(rows[:, :], io["row_numbers"]).then_inc(loaded, 16)
            sp.dma_start(table[:, :, :], io["rope_table"]).then_inc(loaded, 16)
            sp.dma_start(st.head_rows[:, :], io["head_rows"]).then_inc(loaded, 16)

        @block.vector
        def _(dve):
            chain = Chain(dve, chain_sem)
            dve.wait_ge(loaded, 80)
            chain(dve.tensor_scalar(pos[:, 0, :], pos_in[:, :], 0.0, float(Q), ALU.is_lt, ALU.mult))
            chain(dve.tensor_tensor(pos[:, 1, :], pos_in[:, :], pos[:, 0, :], ALU.add))
            chain(dve.tensor_scalar(pos[:, 0, :], pos[:, 1, :], 0.0, float(Q - 1), ALU.max, ALU.min))
            for k in range(2):
                ins = dve.tensor_scalar(onehot[:, k, :], pos[:, 0, :], rows[:, k:k + 1], None, ALU.is_equal)
            ins.then_inc(onehot_ready, 1)
            chain(dve.tensor_scalar(is_one[:, :, :], types[:, :, :], 1.0, None, ALU.is_equal))
            dve.tensor_tensor(st.vm[:, :, 0:Q - 1], is_one[:, :, 0:Q - 1], is_one[:, :, 1:Q], ALU.mult)
            dve.memset(st.vm[:, :, Q - 1:Q], 0.0)
            dve.wait_ge(picks_done, 1)
            dve.tensor_copy(st.rope[:, :, :], picked[:, :, :])

        @block.tensor
        def _(pe):
            pe.wait_ge(onehot_ready, 1)
            for t in range(2):
                for k in range(2):
                    ins = pe.matmul(picked[:, t, :], onehot[:, k, t * P:(t + 1) * P], table[:, k, :],
                                    start=(k == 0), stop=(k == 1))
            ins.then_inc(picks_done, 1)


def self_attention_phase(nc, st, io):
    H, W = 16, 16
    with Phase(nc, "self") as ph:
        wqkv = ph.sb("wqkv", [P, 2, 2, 3 * D])
        wd = ph.sb("wd", [P, 2, 2, D])
        causal = ph.sb("causal", [P, Q])
        z = ph.sb("z", [P, 2, 2, Q])
        rot_a = ph.sb("rot_a", [P, 2, 2 * D])
        rot_b = ph.sb("rot_b", [P, 2, 2 * D])
        v_sb = ph.sb("v_sb", [P, 2, D])
        kT = ph.sb("kT", [P, 2, Q])
        qT = ph.sb("qT", [P, 2, Q])
        qm = ph.sb("qm", [P, H, Q])
        neg = ph.sb("neg", [P, 2, 3 * P])
        probs = ph.sb("probs", [P, 2, 3 * P])
        negmax = ph.sb("negmax", [P, 2, 2])
        rowsum = ph.sb("rowsum", [P, 2, H])
        inv = ph.sb("inv", [P, 2, H])
        pT = ph.sb("pT", [P, 2, 3 * P])
        o_sb = ph.sb("o_sb", [P, 2, D])
        oT = ph.sb("oT", [P, 2, 2, Q])
        ps_qk = [ph.ps(f"ps_qk{i}", [P, BANK]) for i in range(2)]
        ps_v = ph.ps("ps_v", [P, 2, D])
        ps_t = [ph.ps(f"ps_t{i}", [P, BANK]) for i in range(2)]
        ps_oT = ph.ps("ps_oT", [P, 2, Q])
        ps_y = ph.ps("ps_y", [P, 2, D])
        loaded = ph.sem("loaded")
        z_ready = ph.sem("z_ready")
        qk_made = ph.sem("qk_made")
        v_made = ph.sem("v_made")
        v_ready = ph.sem("v_ready")
        chain = ph.sem("chain")
        rot_ready = ph.sem("rot_ready")
        qkT_made = ph.sem("qkT_made")
        qkT_ready = ph.sem("qkT_ready")
        qm_ready = ph.sem("qm_ready")
        scored = ph.sem("scored")
        maxed = ph.sem("maxed")
        exped = ph.sem("exped")
        turned = ph.sem("turned")
        pT_ready = ph.sem("pT_ready")
        pv_done = ph.sem("pv_done")
        inverted = ph.sem("inverted")
        o_ready = ph.sem("o_ready")
        oT_made = ph.sem("oT_made")
        oT_ready = ph.sem("oT_ready")
        y_made = ph.sem("y_made")
        y_added = ph.sem("y_added")
        dve_passed = ph.sem("dve_passed")
        pool_passed = ph.sem("pool_passed")
        block = ph.block()

        @block.sync
        def _(sp):
            for e, n in enumerate("vl"):
                sp.dma_start(wqkv[:, e, :, :], io[f"L1_{n}_qkv"]).then_inc(loaded, 16)
                sp.dma_start(wd[:, e, :, :], io[f"L1_{n}_dense"]).then_inc(loaded, 16)
            sp.dma_start(causal[:, :], io["causal"]).then_inc(loaded, 16)

        @block.tensor
        def _(pe):
            pe.sem_inc(turned, 2)
            pe.sem_inc(pv_done, 2)
            pe.wait_ge(loaded, 80)
            with pe.Fori(0, B) as b:
                n0 = b * H
                pe.wait_ge(z_ready, b + 1)
                pe.wait_ge(y_added, b + 1)
                for t in range(2):
                    for i in range(4):
                        e, f = divmod(i, 2)
                        ins = pe.matmul(ps_qk[t][:, :], z[:, e, f, t * P:(t + 1) * P], wqkv[:, e, f, 0:2 * D],
                                        start=(i == 0), stop=(i == 3))
                    ins.then_inc(qk_made, 1)
                for t in range(2):
                    for i in range(4):
                        e, f = divmod(i, 2)
                        ins = pe.matmul(ps_v[:, t, :], z[:, e, f, t * P:(t + 1) * P], wqkv[:, e, f, 2 * D:3 * D],
                                        start=(i == 0), stop=(i == 3))
                ins.then_inc(v_made, 1)
                for t in range(2):
                    pe.wait_ge(rot_ready, 2 * b + t + 1)
                    for i in range(4):
                        ins = pe.transpose(ps_t[t][:, i * P:(i + 1) * P], rot_a[:, t, i * P:(i + 1) * P],
                                           st.ident[:, :])
                    ins.then_inc(qkT_made, 1)
                for h in range(H + 2):
                    if h < H:
                        n = n0 + h
                        f = h // 8
                        if h == 0:
                            pe.wait_ge(qkT_ready, 2 * b + 2)
                        pe.wait_ge(qm_ready, n + 1)
                        pe.wait_ge(maxed, 2 * n + 2)
                        s = ps_qk[h % 2]
                        pe.matmul(s[:, 0:P], qm[:, h, 0:P], kT[:, f, 0:P], start=True, stop=True)
                        pe.matmul(s[:, P:3 * P], qm[:, h, P:2 * P], kT[:, f, :], start=True, stop=True)\
                            .then_inc(scored, 1)
                    if 1 <= h <= H:
                        n = n0 + h - 1
                        p = (h - 1) % 2
                        pe.wait_ge(exped, 2 * n + 6)
                        pe.wait_ge(pT_ready, n + 1)
                        for i in range(3):
                            ins = pe.transpose(ps_t[p][:, i * P:(i + 1) * P], probs[:, p, i * P:(i + 1) * P],
                                               st.ident[:, :])
                        ins.then_inc(turned, 1)
                    if h >= 2:
                        n = n0 + h - 2
                        p = (h - 2) % 2
                        c = slice((h - 2) * W, (h - 1) * W)
                        pe.wait_ge(pT_ready, n + 3)
                        if h == 2:
                            pe.wait_ge(v_ready, b + 1)
                        pe.matmul(ps_v[:, 0, c], pT[:, p, 0:P], v_sb[:, 0, c], start=True, stop=True)
                        pe.matmul(ps_v[:, 1, c], pT[:, p, P:2 * P], v_sb[:, 0, c], start=True, stop=False)
                        pe.matmul(ps_v[:, 1, c], pT[:, p, 2 * P:3 * P], v_sb[:, 1, c], start=False, stop=True)\
                            .then_inc(pv_done, 1)
                pe.wait_ge(o_ready, b + 1)
                for f in range(2):
                    for t in range(2):
                        ins = pe.transpose(ps_oT[:, f, t * P:(t + 1) * P], o_sb[:, t, f * P:(f + 1) * P],
                                           st.ident[:, :])
                ins.then_inc(oT_made, 1)
                pe.wait_ge(oT_ready, b + 1)
                for t in range(2):
                    for i in range(4):
                        e, f = divmod(i, 2)
                        ins = pe.matmul(ps_y[:, t, :], oT[:, e, f, t * P:(t + 1) * P], wd[:, e, f, :],
                                        start=(i == 0), stop=(i == 3))
                ins.then_inc(y_made, 1)

        @block.vector
        def _(dve):
            dve.sem_inc(maxed, 4)
            dve.sem_inc(y_added, 1)
            dve.wait_ge(loaded, 80)

            def pick(to, src, b, sem, seen):
                for f in range(2):
                    ins = dve.tensor_tensor(to[:, 0, f, :], src[:, f, :], st.vm[:, bass.ds(b, 1), :].squeeze(1), ALU.mult)
                ins.then_inc(chain, 1)
                dve.wait_ge(chain, seen)
                dve.tensor_tensor(to[:, 1, :, :], src, to[:, 0, :, :], ALU.subtract).then_inc(sem, 1)

            with dve.Fori(0, B) as b:
                n0 = b * H
                k0 = 8 * b
                pick(z, st.XT[:, :, bass.ts(b, Q)], b, z_ready, k0 + 1)
                for t in range(2):
                    k = k0 + 1 + 3 * t
                    cos = st.rope[:, t, 0:8].unsqueeze(1).to_broadcast([P, 64, 8])
                    msin = st.rope[:, t, 8:16].unsqueeze(1).to_broadcast([P, 32, 8])
                    sin = st.rope[:, t, 16:24].unsqueeze(1).to_broadcast([P, 32, 8])
                    pairs = ps_qk[t][:, :].rearrange("p (g h e) -> p g h e", h=2, e=8)
                    rb = rot_b[:, t, :].rearrange("p (g h e) -> p g h e", h=2, e=8)
                    dve.wait_ge(qk_made, 2 * b + t + 1)
                    dve.tensor_tensor(rot_a[:, t, :].rearrange("p (g e) -> p g e", e=8),
                                      ps_qk[t][:, :].rearrange("p (g e) -> p g e", e=8), cos, ALU.mult).then_inc(chain, 1)
                    dve.tensor_tensor(rb[:, :, 0, :], pairs[:, :, 1, :], msin, ALU.mult).then_inc(chain, 1)
                    dve.tensor_tensor(rb[:, :, 1, :], pairs[:, :, 0, :], sin, ALU.mult).then_inc(chain, 1)
                    dve.wait_ge(chain, k + 3)
                    dve.tensor_tensor(rot_a[:, t, :], rot_a[:, t, :], rot_b[:, t, :], ALU.add).then_inc(rot_ready, 1)
                for h in range(H):
                    n = n0 + h
                    p = h % 2
                    dve.wait_ge(exped, 2 * n + 2)
                    dve.wait_ge(scored, n + 1)
                    dve.sem_inc(dve_passed, 1)
                    dve.tensor_tensor_reduce(out=neg[:, p, 0:P], in0=ps_qk[p][:, 0:P], in1=causal[:, P:2 * P],
                                             scale=-1.0, scalar=BIG, op0=ALU.add, op1=ALU.min,
                                             accum_out=negmax[:, p, 0:1]).then_inc(maxed, 1)
                    dve.tensor_tensor_reduce(out=neg[:, p, P:3 * P], in0=ps_qk[p][:, P:3 * P], in1=causal[:, :],
                                             scale=-1.0, scalar=BIG, op0=ALU.add, op1=ALU.min,
                                             accum_out=negmax[:, p, 1:2]).then_inc(maxed, 1)
                dve.wait_ge(exped, 2 * n0 + 2 * H + 4)
                dve.reciprocal(inv[:, :, :], rowsum[:, :, :]).then_inc(inverted, 1)
                dve.wait_ge(inverted, b + 1)
                dve.wait_ge(pv_done, n0 + H + 2)
                dve.tensor_tensor(o_sb[:, :, :].rearrange("p t (h w) -> p (t h) w", w=W),
                                  ps_v[:, :, :].rearrange("p t (h w) -> p (t h) w", w=W),
                                  inv[:, :, :].rearrange("p t h -> p (t h)").unsqueeze(2).to_broadcast([P, 2 * H, W]),
                                  ALU.mult).then_inc(o_ready, 1)
                dve.wait_ge(oT_made, b + 1)
                pick(oT, ps_oT[:, :, :], b, oT_ready, k0 + 8)
                dve.wait_ge(y_made, b + 1)
                dve.tensor_tensor(st.X[:, bass.ds(2 * b, 2), :], ps_y[:, :, :], st.X[:, bass.ds(2 * b, 2), :],
                                  ALU.add).then_inc(y_added, 1)

        @block.scalar
        def _(act):
            act.sem_inc(exped, 4)
            act.sem_inc(pT_ready, 2)
            with act.Fori(0, B) as b:
                n0 = b * H
                act.wait_ge(v_made, b + 1)
                act.activation(v_sb[:, :, :], ps_v[:, :, :], ACT.Copy).then_inc(v_ready, 1)
                for t in range(2):
                    act.wait_ge(qkT_made, 2 * b + t + 1)
                    act.activation(qT[:, :, t * P:(t + 1) * P],
                                   ps_t[t][:, 0:2 * P].rearrange("p (f q) -> p f q", f=2), ACT.Copy)
                    act.activation(kT[:, :, t * P:(t + 1) * P],
                                   ps_t[t][:, 2 * P:4 * P].rearrange("p (f q) -> p f q", f=2),
                                   ACT.Copy).then_inc(qkT_ready, 1)
                for h in range(H + 1):
                    if h < H:
                        n = n0 + h
                        p = h % 2
                        for t in range(2):
                            act.wait_ge(maxed, 2 * n + t + 5)
                            act.wait_ge(turned, n + 1)
                            cols = slice(0, P) if t == 0 else slice(P, 3 * P)
                            act.activation(probs[:, p, cols], neg[:, p, cols], ACT.Exp, scale=-1.0,
                                           bias=negmax[:, p, t:t + 1],
                                           accum_out=rowsum[:, t, h:h + 1]).then_inc(exped, 1)
                    if h >= 1:
                        n = n0 + h - 1
                        p = (h - 1) % 2
                        act.wait_ge(turned, n + 3)
                        act.wait_ge(pv_done, n + 1)
                        act.activation(pT[:, p, :], ps_t[p][:, 0:3 * P], ACT.Copy).then_inc(pT_ready, 1)

        @block.gpsimd
        def _(pool):
            with pool.Fori(0, B) as b:
                pool.wait_ge(qkT_ready, 2 * b + 2)
                pool.sem_inc(pool_passed, 1)
                for h in range(H):
                    pool.tensor_scalar(qm[:, h, :], qT[:, h // 8, :], st.head_rows[:, h % 8:h % 8 + 1], None,
                                       ALU.mult).then_inc(qm_ready, 1)


def expert_mlp_phase(nc, st, io):
    F = 688
    FT = (F + P - 1) // P
    TC = BANK
    NC = B * Q // TC
    with Phase(nc, "experts") as ph:
        wg = ph.sb("wg", [P, 2, 2, F])
        wu = ph.sb("wu", [P, 2, 2, F])
        wd = ph.sb("wd", [P, 2, FT, D])
        zv = ph.sb("zv", [P, 2, TC])
        zl = ph.sb("zl", [P, 2, TC])
        act_g = [ph.sb(f"act_g{i}", [P, TC]) for i in range(2)]
        hid = [ph.sb(f"hid{i}", [P, TC]) for i in range(2)]
        hx = ph.sb("hx", [P, 2, FT, TC])
        ps_g = [ph.ps(f"ps_g{i}", [P, TC]) for i in range(2)]
        ps_u = [ph.ps(f"ps_u{i}", [P, TC]) for i in range(2)]
        ps_y = [ph.ps(f"ps_y{i}", [P, D]) for i in range(2)]
        loaded = ph.sem("loaded")
        split = ph.sem("split")
        z_ready = ph.sem("z_ready")
        g_made = ph.sem("g_made")
        silu_done = ph.sem("silu_done")
        hid_ready = ph.sem("hid_ready")
        v_done = ph.sem("v_done")
        h_split = ph.sem("h_split")
        y_made = ph.sem("y_made")
        y_added = ph.sem("y_added")
        pool_passed = ph.sem("pool_passed")
        block = ph.block()

        @block.sync
        def _(sp):
            for e, n in enumerate("vl"):
                sp.dma_start(wg[:, e, :, :], io[f"L1_{n}_gate"]).then_inc(loaded, 16)
                sp.dma_start(wu[:, e, :, :], io[f"L1_{n}_up"]).then_inc(loaded, 16)
                sp.dma_start(wd[:, e, :, :], io[f"L1_{n}_down"]).then_inc(loaded, 16)

        vm_flat = st.vm[:, :, :].rearrange("p b q -> p (b q)")

        @block.tensor
        def _(pe):
            pe.sem_inc(g_made, 2)
            pe.wait_ge(loaded, 96)
            with pe.Fori(0, NC) as c:
                pe.wait_ge(z_ready, c + 1)
                for t in range(FT):
                    w = min(P, F - t * P)
                    m = c * FT + t
                    pe.wait_ge(hid_ready, m + 1)
                    for out, weights in ((ps_g, wg), (ps_u, wu)):
                        for i in range(4):
                            e, f = divmod(i, 2)
                            ins = pe.matmul(out[t % 2][0:w, :], weights[:, e, f, t * P:t * P + w],
                                            (zl if e else zv)[:, f, :], start=(i == 0), stop=(i == 3))
                    ins.then_inc(g_made, 1)
                pe.wait_ge(h_split, FT * (c + 1) + 2)
                for r in range(TC // P):
                    pe.wait_ge(y_added, 4 * c + r + 1)
                    for t in range(FT):
                        w = min(P, F - t * P)
                        for e in range(2):
                            ins = pe.matmul(ps_y[r % 2][:, :], hx[0:w, e, t, r * P:(r + 1) * P], wd[0:w, e, t, :],
                                            start=(t == 0 and e == 0), stop=(t == FT - 1 and e == 1))
                    ins.then_inc(y_made, 1)

        @block.scalar
        def _(act):
            with act.Fori(0, NC) as c:
                for t in range(FT):
                    w = min(P, F - t * P)
                    m = c * FT + t
                    act.wait_ge(hid_ready, m + 1)
                    act.wait_ge(g_made, m + 3)
                    act.activation(act_g[t % 2][0:w, :], ps_g[t % 2][0:w, :], ACT.Silu).then_inc(silu_done, 1)

        @block.vector
        def _(dve):
            dve.sem_inc(hid_ready, 2)
            dve.sem_inc(y_added, 2)
            with dve.Fori(0, NC) as c:
                dve.wait_ge(g_made, FT * c + 2)
                for f in range(2):
                    ins = dve.tensor_tensor(zv[:, f, :], st.XT[:, f, bass.ts(c, TC)], vm_flat[:, bass.ts(c, TC)],
                                            ALU.mult)
                ins.then_inc(split, 1)
                dve.wait_ge(split, c + 1)
                dve.tensor_tensor(zl[:, :, :], st.XT[:, :, bass.ts(c, TC)], zv[:, :, :],
                                  ALU.subtract).then_inc(z_ready, 1)
                for t in range(FT):
                    w = min(P, F - t * P)
                    m = c * FT + t
                    dve.wait_ge(h_split, m + 1)
                    dve.wait_ge(silu_done, m + 1)
                    dve.tensor_tensor(hid[t % 2][0:w, :], act_g[t % 2][0:w, :], ps_u[t % 2][0:w, :],
                                      ALU.mult).then_inc(hid_ready, 1)
                for r in range(TC // P):
                    j = 4 * c + r
                    dve.wait_ge(y_made, j + 1)
                    dve.tensor_tensor(st.X[:, bass.ds(j, 1), :].squeeze(1), ps_y[r % 2][:, :],
                                      st.X[:, bass.ds(j, 1), :].squeeze(1), ALU.add).then_inc(y_added, 1)

        @block.gpsimd
        def _(pool):
            pool.sem_inc(h_split, 2)
            with pool.Fori(0, NC) as c:
                pool.wait_ge(y_added, 4 * c + 2)
                for t in range(FT):
                    w = min(P, F - t * P)
                    m = c * FT + t
                    pool.wait_ge(hid_ready, m + 3)
                    pool.sem_inc(pool_passed, 1)
                    pool.tensor_tensor(hx[0:w, 0, t, :], hid[t % 2][0:w, :], vm_flat[0:w, bass.ts(c, TC)],
                                       ALU.mult).then_inc(v_done, 1)
                    pool.wait_ge(v_done, m + 1)
                    pool.tensor_tensor(hx[0:w, 1, t, :], hid[t % 2][0:w, :], hx[0:w, 0, t, :],
                                       ALU.subtract).then_inc(h_split, 1)


def memory_weights_phase(nc, st, io):
    with Phase(nc, "memw") as ph:
        w = ph.sb("w", [P, 2, C])
        loaded = ph.sem("loaded")
        block = ph.block()

        @block.sync
        def _(sp):
            sp.dma_start(w[:, :, :], io["L2_mem"]).then_inc(loaded, 16)
            sp.dma_start(st.Bw[:, 0:D], io["L2_memT"]).then_inc(loaded, 16)
            sp.wait_ge(loaded, 32)

        @block.vector
        def _(dve):
            dve.wait_ge(loaded, 32)
            dve.tensor_scalar(st.A[:, :, 0:C], w[:, :, :], D ** -0.5, None, ALU.mult)


def gate_phase(nc, st, io):
    with Phase(nc, "gate") as ph:
        wg = ph.sb("wg", [P, 4, D])
        bias = ph.sb("bias", [P, D])
        norm_w = ph.sb("norm_w", [P, D])
        mc = [ph.sb(f"mc{i}", [P, D]) for i in range(2)]
        zT = [ph.sb(f"zT{i}", [P, 4, P]) for i in range(2)]
        g = [ph.sb(f"g{i}", [P, D]) for i in range(2)]
        stats = ph.sb("stats", [P, NT, 6])
        rows = ph.sb("rows", [P, 4, NT])
        ps_t = [ph.ps(f"ps_t{i}", [P, BANK]) for i in range(2)]
        ps_z = [ph.ps(f"ps_z{i}", [P, D]) for i in range(2)]
        loaded = ph.sem("loaded")
        mc_ready = ph.sem("mc_ready")
        hs_ready = ph.sem("hs_ready")
        turned = ph.sem("turned")
        zT_ready = ph.sem("zT_ready")
        z_made = ph.sem("z_made")
        summed = ph.sem("summed")
        pool_passed = ph.sem("pool_passed")
        sig_done = ph.sem("sig_done")
        scaled = ph.sem("scaled")
        fused = ph.sem("fused")
        chain_sem = ph.sem("chain")
        root_asked = ph.sem("root_asked")
        root_taken = ph.sem("root_taken")
        block = ph.block()

        @block.sync
        def _(sp):
            sp.dma_start(wg[:, :, :], io["L2_gateT"]).then_inc(loaded, 16)
            sp.dma_start(bias[:, :], io["L2_gate_b"].to_broadcast([P, D])).then_inc(loaded, 16)
            sp.dma_start(norm_w[:, :], io["L2_norm_w"].to_broadcast([P, D])).then_inc(loaded, 16)

        @block.gpsimd
        def _(pool):
            pool.wait_ge(loaded, 48)
            with pool.Fori(0, NT // 2) as i:
                for par in range(2):
                    j = 2 * i + par
                    pool.wait_ge(turned, j + 1)
                    pool.sem_inc(pool_passed, 1)
                    pool.tensor_copy(mc[par][:, :], st.MC[:, bass.ds(j, 1), :].squeeze(1)).then_inc(mc_ready, 1)
                    pool.wait_ge(z_made, j + 1)
                    pool.sem_inc(pool_passed, 1)
                    pool.tensor_copy(zT[par][:, 0:2, :], st.XT[:, :, bass.ts(j, P)]).then_inc(hs_ready, 1)

        @block.tensor
        def _(pe):
            pe.sem_inc(turned, 2)
            pe.sem_inc(z_made, 2)
            pe.wait_ge(loaded, 48)
            with pe.Fori(0, NT // 2) as i:
                for par in range(2):
                    j = 2 * i + par
                    pe.wait_ge(mc_ready, j + 1)
                    pe.wait_ge(zT_ready, j + 1)
                    for f in range(2):
                        ins = pe.transpose(ps_t[par][:, f * P:(f + 1) * P], mc[par][:, f * P:(f + 1) * P],
                                           st.ident[:, :])
                    ins.then_inc(turned, 1)
                for par in range(2):
                    j = 2 * i + par
                    pe.wait_ge(hs_ready, j + 1)
                    pe.wait_ge(zT_ready, j + 3)
                    pe.wait_ge(summed, j + 1)
                    for f in range(4):
                        ins = pe.matmul(ps_z[par][:, :], zT[par][:, f, :], wg[:, f, :], start=(f == 0), stop=(f == 3))
                    ins.then_inc(z_made, 1)

        @block.scalar
        def _(act):
            act.sem_inc(zT_ready, 2)
            with act.Fori(0, NT // 2) as i:
                for par in range(2):
                    j = 2 * i + par
                    act.wait_ge(turned, j + 3)
                    act.wait_ge(z_made, j + 1)
                    act.activation(zT[par][:, 2:4, :], ps_t[par][:, 0:2 * P].rearrange("p (f q) -> p f q", f=2),
                                   ACT.Copy).then_inc(zT_ready, 1)
                for par in range(2):
                    j = 2 * i + par
                    act.wait_ge(summed, j + 3)
                    act.activation(g[par][:, :], g[par][:, :], ACT.Sigmoid).then_inc(sig_done, 1)
            act.wait_ge(root_asked, 1)
            act.activation(rows[:, 1, :], rows[:, 1, :], ACT.Sqrt).then_inc(root_taken, 1)

        @block.vector
        def _(dve):
            dve.sem_inc(summed, 2)
            dve.sem_inc(fused, 2)
            dve.wait_ge(loaded, 48)
            with dve.Fori(0, NT // 2) as i:
                for par in range(2):
                    dve.wait_ge(fused, 2 * i + par + 1)
                    dve.wait_ge(z_made, 2 * i + par + 3)
                    dve.tensor_tensor(g[par][:, :], ps_z[par][:, :], bias[:, :], ALU.add).then_inc(summed, 1)
                for par in range(2):
                    j = 2 * i + par
                    dve.wait_ge(sig_done, j + 1)
                    dve.tensor_tensor(g[par][:, :], g[par][:, :], st.MC[:, bass.ds(j, 1), :].squeeze(1),
                                      ALU.mult).then_inc(scaled, 1)
                    dve.wait_ge(scaled, j + 1)
                    dve.tensor_tensor(st.X[:, bass.ds(j, 1), :].squeeze(1), g[par][:, :],
                                      st.X[:, bass.ds(j, 1), :].squeeze(1), ALU.add).then_inc(fused, 1)
            dve.wait_ge(fused, NT + 2)
            chain = Chain(dve, chain_sem)
            row_statistics(dve, chain, st.X, stats, rows, 1e-6, True, root_asked, root_taken)
            with dve.Fori(0, NT) as j:
                x = st.X[:, bass.ds(j, 1), :].squeeze(1)
                dve.scalar_tensor_tensor(out=x, in0=x, scalar=rows[:, 1, bass.ds(j, 1)], in1=norm_w[:, :],
                                         op0=ALU.mult, op1=ALU.mult)


class State:
    pass


def build(nc, io, stages):
    st = State()
    with ExitStack() as ctx:
        def sb(name, shape):
            return ctx.enter_context(nc.sbuf_tensor(name, shape, F32))

        st.ident = sb("ident", [P, P])
        st.X = sb("X", [P, NT, D])
        st.XT = sb("XT", [P, 2, B * Q])
        st.A = sb("A", [P, 2, 16 * C])
        st.Bw = sb("Bw", [P, 16 * D])
        st.vm = sb("vm", [P, B, Q])
        st.rope = sb("rope", [P, 2, 24])
        st.head_rows = sb("head_rows", [P, 8])
        st.MC = sb("MC", [P, NT, D])
        for stage, args in stages:
            stage(nc, st, io, *args)


def perceiver_stages(n):
    return [
        (norm_phase, (f"{n}_norm1", "ln", f"{n}_ln_q_g", f"{n}_ln_q_b", 1e-5)),
        (weights_phase, (f"{n}_w", 16, 64, 64 ** -0.5, f"{n}_attn_gate")),
        (attention_phase, (f"{n}_attn", 16, True)),
        (norm_phase, (f"{n}_norm2", "ln", f"{n}_ln_ff_g", f"{n}_ln_ff_b", 1e-5)),
        (mlp_phase, (f"{n}_mlp", f"{n}_ff_gate")),
    ]


EXPERT_STAGES = [
    (expert_masks_phase, ()),
    (norm_phase, ("L1_norm1", "rms", "L1_ln_in_w", None, 1e-6)),
    (self_attention_phase, ()),
    (norm_phase, ("L1_norm2", "rms", "L1_ln_post_cross_w", None, 1e-6)),
    (weights_phase, ("L1_w", 16, 8, 8 ** -0.5)),
    (attention_phase, ("L1_attn", 16, False)),
    (norm_phase, ("L1_norm3", "rms", "L1_ln_post_attn_w", None, 1e-6)),
    (expert_mlp_phase, ()),
]

MEMORY_STAGES = [
    (norm_phase, ("L2_turn", "plain")),
    (memory_weights_phase, ()),
    (attention_phase, ("L2_attn", 1, False, True)),
    (gate_phase, ()),
]

STAGES = ([(load_phase, ())] + perceiver_stages("L0") + EXPERT_STAGES + MEMORY_STAGES
          + perceiver_stages("L3") + [(store_phase, ())])


def layout(inputs):
    import numpy as np

    def heads_first(w, width):
        w = np.asarray(w)
        return w.reshape(w.shape[0], -1, width).transpose(2, 1, 0)

    def row_heads(w, width):
        w = np.asarray(w)
        return w.reshape(-1, width, w.shape[1]).transpose(1, 0, 2)

    def tiled(w):
        w = np.asarray(w)
        return w.reshape(-1, P, w.shape[1]).transpose(1, 0, 2)

    def halves(v):
        return np.asarray(v).reshape(2, P).T

    ctx = np.asarray(inputs["ctx_1024"])
    padded = np.zeros((B, SP, C), ctx.dtype)
    padded[:, :S] = ctx
    mask = np.zeros((B, 4 * MASK_WORDS), np.bool_)
    mask[:, :S] = np.asarray(inputs["mask_BxS2_bk0"])
    a = {
        "ident": np.eye(P, dtype=np.float32),
        "x": np.asarray(inputs["x"]).reshape(B * Q, D),
        "ctxT": ctx.transpose(0, 2, 1),
        "ctx": padded.reshape(B, KT, P, C).transpose(0, 2, 1, 3),
        "mask": mask.view(np.int32),
    }
    for n in ("L0", "L3"):
        def w(k):
            return np.asarray(inputs[f"{n}_xattn_{k}"])
        for k in ("ln_q_g", "ln_q_b", "ln_ff_g", "ln_ff_b"):
            a[f"{n}_{k}"] = halves(w(k))
        kv = w("Wkv")
        a[f"{n}_w_wq"] = heads_first(w("Wq"), 64)
        a[f"{n}_w_wk"] = heads_first(kv[:, :1024], 64)
        a[f"{n}_w_wv"] = heads_first(kv[:, 1024:], 64)
        a[f"{n}_w_wo"] = row_heads(w("Wo"), 64)
        a[f"{n}_attn_gate"] = w("attn_gate").reshape(1, 1)
        a[f"{n}_ff_gate"] = w("ff_gate").reshape(1, 1)
        a[f"{n}_mlp_w1"] = tiled(w("W1"))
        a[f"{n}_mlp_w2"] = tiled(w("W2"))
    def w(k):
        return np.asarray(inputs[f"L1_xattn_{k}"])
    for k in ("ln_in_w", "ln_post_attn_w", "ln_post_cross_w"):
        a[f"L1_{k}"] = halves(w(k))
    for e in "vl":
        a[f"L1_{e}_qkv"] = tiled(w(f"{e}_qkv"))
        a[f"L1_{e}_dense"] = tiled(w(f"{e}_dense"))
        a[f"L1_{e}_gate"] = tiled(w(f"{e}_gate"))
        a[f"L1_{e}_up"] = tiled(w(f"{e}_up"))
        down = np.zeros((768, D), np.float32)
        down[:688] = w(f"{e}_down")
        a[f"L1_{e}_down"] = tiled(down)
    ckv = w("ckv_w")
    a["L1_w_wq"] = heads_first(w("cq_w"), 8)
    a["L1_w_wk"] = heads_first(ckv[:, :C], 8)
    a["L1_w_wv"] = heads_first(ckv[:, C:], 8)
    a["L1_w_wo"] = row_heads(w("cdense_w"), 8)
    a["L2_mem"] = tiled(inputs["L2_xattn_W_mem"])
    a["L2_memT"] = np.asarray(inputs["L2_xattn_W_mem"]).T
    a["L2_gateT"] = tiled(np.asarray(inputs["L2_xattn_W_gate"]).T)
    a["L2_gate_b"] = np.asarray(inputs["L2_xattn_b_gate"]).reshape(1, D)
    a["L2_norm_w"] = np.asarray(inputs["L2_xattn_norm_w"]).reshape(1, D)
    a["types"] = np.asarray(inputs["mask_BxS_ik0"])
    a["positions"] = np.asarray(inputs["pos_1xS"])
    freqs = np.outer(np.arange(Q, dtype=np.float32),
                     (1.0 / 10000.0 ** (np.arange(0, 16, 2, dtype=np.float32) / np.float32(16))).astype(np.float32))
    cos, sin = np.cos(freqs).astype(np.float32), np.sin(freqs).astype(np.float32)
    a["rope_table"] = tiled(np.concatenate([cos, -sin, sin], axis=1))
    a["row_numbers"] = np.arange(Q, dtype=np.float32).reshape(2, P).T
    a["head_rows"] = np.kron(np.eye(8, dtype=np.float32), np.full((16, 1), 0.25, np.float32))
    a["causal"] = np.concatenate([np.zeros((P, P), np.float32),
                                  np.triu(np.full((P, P), -NEG, np.float32), 1)], axis=1)
    return a


def kernel(**inputs):
    import numpy as np
    import concourse.bacc as bacc
    from concourse.bass_utils import run_bass_kernel_spmd

    nc = bacc.Bacc("TRN2", target_bir_lowering=False, num_devices=1)
    arrays = {k: np.ascontiguousarray(v) for k, v in layout(inputs).items()}
    io = {k: nc.dram_tensor(f"in_{k}", v.shape, mybir.dt.from_np(v.dtype), kind="ExternalInput").ap()
          for k, v in arrays.items()}
    io["out"] = nc.dram_tensor("out", (B * Q, D), F32, kind="ExternalOutput").ap()
    build(nc, io, STAGES)
    r = run_bass_kernel_spmd(nc, [{f"in_{k}": v for k, v in arrays.items()}], core_ids=[0])
    return r.results[0]["out"].reshape(B, Q, D)
```

```python
from contextlib import ExitStack

import concourse.bass as bass
from concourse import mybir

ALU = mybir.AluOpType
ACT = mybir.ActivationFunctionType
AX_X = mybir.AxisListType.X
F32 = mybir.dt.float32
I32 = mybir.dt.int32
U8 = mybir.dt.uint8
F32R = mybir.dt.float32r

P = 128
B = 8
Q = 256
D = 256
C = 128
S = 1601
NT = B * Q // P
KT = (S + P - 1) // P
SP = KT * P
KLAST = S - (KT - 1) * P
BANK = 512
MASK_WORDS = (S + 3) // 4
NEG = 1e30
BIG = 3e38
S_EVEN = S + S % 2

SCORE_CHUNKS = [(c, min(BANK, S - c)) for c in range(0, S, BANK)]
EVEN_CHUNKS = [(c, min(BANK, S_EVEN - c)) for c in range(0, S_EVEN, BANK)]
TURN_GROUPS = [range(k, min(k + 4, KT)) for k in range(0, KT, 4)]


class Phase:

    def __init__(self, nc, name):
        self.nc, self.name, self.ctx, self.sems = nc, name, ExitStack(), []

    def __enter__(self):
        self.ctx.__enter__()
        return self

    def __exit__(self, *error):
        self.ctx.__exit__(*error)
        self.nc.clear_and_free_semaphores(self.sems)
        self.nc.all_engine_barrier()

    def sb(self, name, shape, dt=F32):
        return self.ctx.enter_context(self.nc.sbuf_tensor(f"{self.name}_{name}", shape, dt))

    def ps(self, name, shape, dt=F32):
        return self.ctx.enter_context(self.nc.psum_tensor(f"{self.name}_{name}", shape, dt))

    def sem(self, name):
        self.sems.append(self.nc.alloc_semaphore(f"{self.name}_{name}"))
        return self.sems[-1]

    def block(self):
        return self.ctx.enter_context(self.nc.Block())


def load_phase(nc, st, io):
    with Phase(nc, "load") as ph:
        loaded = ph.sem("loaded")
        block = ph.block()

        @block.sync
        def _(sp):
            sp.dma_start(st.ident[:, :], io["ident"]).then_inc(loaded, 16)
            sp.dma_start(st.X[:, :, :], io["x"].rearrange("(j p) d -> p j d", p=P)).then_inc(loaded, 16)
            sp.wait_ge(loaded, 32)


def store_phase(nc, st, io):
    with Phase(nc, "store") as ph:
        stored = ph.sem("stored")
        block = ph.block()

        @block.sync
        def _(sp):
            sp.dma_start(io["out"].rearrange("(j p) d -> p j d", p=P), st.X[:, :, :]).then_inc(stored, 16)
            sp.wait_ge(stored, 16)


def row_statistics(dve, chain, X, stats, rows, eps, rms, root_asked, root_taken):
    with dve.Fori(0, NT) as j:
        dve.bn_stats(stats[:, j, :], X[:, j, :]).then_inc(chain.sem, 1)
    chain.add(NT)
    chain.wait()
    even, odd = stats[:, :, 1], stats[:, :, 4]
    chain(dve.tensor_tensor(rows[:, 2, :], even, odd, ALU.add))
    chain(dve.tensor_tensor(rows[:, 3, :], even, odd, ALU.subtract))
    chain(dve.scalar_tensor_tensor(out=rows[:, 3, :], in0=rows[:, 3, :], scalar=0.25, in1=rows[:, 3, :],
                                   op0=ALU.mult, op1=ALU.mult))
    chain(dve.tensor_tensor(rows[:, 1, :], stats[:, :, 2], stats[:, :, 5], ALU.add))
    chain(dve.scalar_tensor_tensor(out=rows[:, 1, :], in0=rows[:, 1, :], scalar=1.0 / D, in1=rows[:, 3, :],
                                   op0=ALU.mult, op1=ALU.add))
    chain(dve.tensor_scalar(rows[:, 0, :], rows[:, 2, :], 0.5, None, ALU.mult))
    if rms:
        chain(dve.tensor_tensor(rows[:, 3, :], rows[:, 0, :], rows[:, 0, :], ALU.mult))
        chain(dve.tensor_tensor(rows[:, 1, :], rows[:, 1, :], rows[:, 3, :], ALU.add))
    dve.tensor_scalar(rows[:, 1, :], rows[:, 1, :], eps, None, ALU.add).then_inc(root_asked, 1)
    dve.wait_ge(root_taken, 1)
    chain(dve.reciprocal(rows[:, 1, :], rows[:, 1, :]))


class Chain:

    def __init__(self, eng, sem):
        self.eng, self.sem, self.count = eng, sem, 0

    def __call__(self, instruction):
        instruction.then_inc(self.sem, 1)
        self.count += 1
        self.wait()

    def add(self, n):
        self.count += n

    def wait(self):
        self.eng.wait_ge(self.sem, self.count)


def norm_phase(nc, st, io, name, kind, gain=None, shift=None, eps=0.0):
    with Phase(nc, name) as ph:
        xn = [ph.sb(f"xn{i}", [P, D]) for i in range(2)]
        stats = ph.sb("stats", [P, NT, 6])
        rows = ph.sb("rows", [P, 4, NT])
        gs = ph.sb("gs", [P, 2, 2])
        turned = [ph.ps(f"turned{i}", [P, BANK]) for i in range(2)]
        weights = ph.sem("weights")
        chain_sem = ph.sem("chain")
        root_asked = ph.sem("root_asked")
        root_taken = ph.sem("root_taken")
        xn_ready = ph.sem("xn_ready")
        turn_done = ph.sem("turn_done")
        copied = ph.sem("copied")
        block = ph.block()

        @block.sync
        def _(sp):
            if gain:
                sp.dma_start(gs[:, 0, :], io[gain]).then_inc(weights, 16)
            if shift:
                sp.dma_start(gs[:, 1, :], io[shift]).then_inc(weights, 16)

        @block.vector
        def _(dve):
            chain = Chain(dve, chain_sem)
            if kind != "plain":
                row_statistics(dve, chain, st.X, stats, rows, eps, kind == "rms", root_asked, root_taken)
            with dve.Fori(0, NT // 2) as i:
                for par in range(2):
                    j = 2 * i + par
                    dve.wait_ge(turn_done, j + 1)
                    if kind == "ln":
                        ins = dve.tensor_scalar(xn[par][:, :], st.X[:, j, :], rows[:, 0, bass.ds(j, 1)],
                                                rows[:, 1, bass.ds(j, 1)], ALU.subtract, ALU.mult)
                    elif kind == "rms":
                        ins = dve.tensor_scalar(xn[par][:, :], st.X[:, j, :], rows[:, 1, bass.ds(j, 1)], None,
                                                ALU.mult)
                    else:
                        ins = dve.tensor_copy(xn[par][:, :], st.X[:, j, :])
                    ins.then_inc(xn_ready, 1)

        @block.tensor
        def _(pe):
            pe.sem_inc(turn_done, 2)
            with pe.Fori(0, NT // 2) as i:
                for par in range(2):
                    pe.wait_ge(xn_ready, 2 * i + par + 1)
                    pe.wait_ge(copied, 2 * i + par + 1)
                    for f in range(2):
                        ins = pe.transpose(turned[par][:, f * P:(f + 1) * P], xn[par][:, f * P:(f + 1) * P],
                                           st.ident[:, :])
                    ins.then_inc(turn_done, 1)

        @block.scalar
        def _(act):
            act.sem_inc(copied, 2)
            if kind != "plain":
                act.wait_ge(root_asked, 1)
                act.activation(rows[:, 1, :], rows[:, 1, :], ACT.Sqrt).then_inc(root_taken, 1)
            if gain:
                act.wait_ge(weights, 32 if shift else 16)
            with act.Fori(0, NT // 2) as i:
                for par in range(2):
                    j = 2 * i + par
                    act.wait_ge(turn_done, j + 3)
                    for f in range(2):
                        to = st.XT[:, f, bass.ts(j, P)]
                        src = turned[par][:, f * P:(f + 1) * P]
                        if kind == "ln":
                            ins = act.activation(to, src, ACT.Identity, scale=gs[:, 0, f:f + 1],
                                                 bias=gs[:, 1, f:f + 1])
                        elif kind == "rms":
                            ins = act.activation(to, src, ACT.Copy, scale=gs[:, 0, f:f + 1])
                        else:
                            ins = act.activation(to, src, ACT.Copy)
                    ins.then_inc(copied, 1)


def weights_phase(nc, st, io, name, heads, width, scale):
    with Phase(nc, name) as ph:
        wq = ph.sb("wq", [width, heads, D])
        wk = ph.sb("wk", [width, heads, C])
        wv = ph.sb("wv", [width, heads, C])
        wo = ph.sb("wo", [width, heads, D])
        prod = [ph.ps(f"prod{i}", [P, BANK]) for i in range(4)]
        loaded = ph.sem("loaded")
        made = ph.sem("made")
        copied = ph.sem("copied")
        block = ph.block()

        @block.sync
        def _(sp):
            for t, n in ((wq, "wq"), (wk, "wk"), (wv, "wv"), (wo, "wo")):
                sp.dma_start(t[:, :, :], io[f"{name}_{n}"]).then_inc(loaded, 16)

        groups = [("A", h, f) for h in range(0, heads, 4) for f in range(2)] + \
                 [("B", h, 0) for h in range(0, heads, 2)]

        @block.tensor
        def _(pe):
            pe.wait_ge(loaded, 64)
            for n, (what, h0, f) in enumerate(groups):
                if n >= 4:
                    pe.wait_ge(copied, n - 3)
                for i in range(4 if what == "A" else 2):
                    h = h0 + i
                    if what == "A":
                        ins = pe.matmul(prod[n % 4][:, i * C:(i + 1) * C], wq[:, h, f * P:(f + 1) * P],
                                        wk[:, h, :], start=True, stop=True)
                    else:
                        ins = pe.matmul(prod[n % 4][:, i * D:(i + 1) * D], wv[:, h, :], wo[:, h, :],
                                        start=True, stop=True)
                ins.then_inc(made, 1)

        @block.vector
        def _(dve):
            for n, (what, h, f) in enumerate(groups):
                dve.wait_ge(made, n + 1)
                if what == "A":
                    to, by = st.A[:, f, h * C:(h + 4) * C], scale
                else:
                    to, by = st.Bw[:, h * D:(h + 2) * D], 1.0
                dve.tensor_scalar(to, prod[n % 4][:, :], by, None, ALU.mult).then_inc(copied, 1)


def gated_weights_phase(nc, st, io, name, heads, width, scale, gate):
    with Phase(nc, name) as ph:
        wq = ph.sb("wq", [width, heads, D])
        wk = ph.sb("wk", [width, heads, C])
        g = ph.sb("g", [P, 2])
        prod = [ph.ps(f"prod{i}", [P, BANK]) for i in range(4)]
        loaded = ph.sem("loaded")
        wo_loaded = ph.sem("wo_loaded")
        gate_ready = ph.sem("gate_ready")
        made = ph.sem("made")
        copied = ph.sem("copied")
        block = ph.block()
        groups = [(h, f) for h in range(0, heads, 4) for f in range(2)]

        @block.sync
        def _(sp):
            sp.dma_start(wq[:, :, :], io[f"{name}_wq"]).then_inc(loaded, 16)
            sp.dma_start(wk[:, :, :], io[f"{name}_wk"]).then_inc(loaded, 16)
            sp.dma_start(g[:, 0:1], io[gate].to_broadcast([P, 1])).then_inc(wo_loaded, 16)
            sp.dma_start(st.Wo[:, :], io[f"{name}_wo"].rearrange("p t d -> p (t d)")).then_inc(wo_loaded, 16)
            sp.dma_start(st.Wv[:, :], io[f"{name}_wv"]).then_inc(wo_loaded, 16)
            sp.wait_ge(wo_loaded, 48)

        @block.tensor
        def _(pe):
            pe.wait_ge(loaded, 32)
            for n, (h0, f) in enumerate(groups):
                if n >= 4:
                    pe.wait_ge(copied, n - 3)
                for i in range(4):
                    ins = pe.matmul(prod[n % 4][:, i * C:(i + 1) * C], wq[:, h0 + i, f * P:(f + 1) * P],
                                    wk[:, h0 + i, :], start=True, stop=True)
                ins.then_inc(made, 1)

        @block.scalar
        def _(act):
            act.wait_ge(wo_loaded, 48)
            act.activation(g[:, 1:2], g[:, 0:1], ACT.Tanh).then_inc(gate_ready, 1)

        @block.vector
        def _(dve):
            for n, (h, f) in enumerate(groups):
                dve.wait_ge(made, n + 1)
                dve.tensor_scalar(st.A[:, f, h * C:(h + 4) * C], prod[n % 4][:, :], scale, None,
                                  ALU.mult).then_inc(copied, 1)
            dve.wait_ge(gate_ready, 1)
            dve.tensor_scalar(st.Wo[:, :], st.Wo[:, :], g[:, 1:2], None, ALU.mult)


def attention_phase(nc, st, io, name, heads, masked, into_context=False):
    with Phase(nc, name) as ph:
        ctxT_in = ph.sb("ctxT_in", [P, S_EVEN])
        ctx_in = ph.sb("ctx_in", [P, KT, C])
        ctxT = ph.sb("ctxT", [P, S])
        ctx = ph.sb("ctx", [P, KT, C])
        bias = ph.sb("bias", [P, S])
        mask_in = ph.sb("mask_in", [P, MASK_WORDS], I32)
        mask_bytes = mask_in[:, :].bitcast(U8)[:, 0:S]
        a_slot = [ph.sb(f"a_slot{i}", [P, 2, C]) for i in range(2)]
        g_sb = [ph.sb(f"g_sb{i}", [P, Q]) for i in range(2)]
        neg = [ph.sb(f"neg{i}", [P, S]) for i in range(2)]
        probs = [ph.sb(f"probs{i}", [P, S]) for i in range(2)]
        negmax = ph.sb("negmax", [P, 2])
        rowsum = ph.sb("rowsum", [P, 2, 2])
        inv = ph.sb("inv", [P, 2])
        pT = [ph.sb(f"pT{i}", [P, KT, Q]) for i in range(2)]
        u_sb = ph.sb("u_sb", [P, Q])
        ps_s = ph.ps("ps_s", [P, 4 * BANK])
        ps_t = [ph.ps(f"ps_t{i}", [P, BANK]) for i in range(2)]
        ps_gu = ph.ps("ps_gu", [P, BANK])
        ps_g, ps_u = ps_gu[:, 0:Q], ps_gu[:, Q:2 * Q]
        ps_o = ph.ps("ps_o", [P, 2, D])

        ctx_loaded = ph.sem("ctx_loaded")
        mask_loaded = ph.sem("mask_loaded")
        staged_out = ph.sem("staged_out")
        ctxT_ready = ph.sem("ctxT_ready")
        ctx_ready = ph.sem("ctx_ready")
        bias_ready = ph.sem("bias_ready")
        a_ready = ph.sem("a_ready")
        g_made = ph.sem("g_made")
        g_copied = ph.sem("g_copied")
        scored = ph.sem("scored")
        maxed = ph.sem("maxed")
        exped = ph.sem("exped")
        turned = ph.sem("turned")
        turn_act = ph.sem("turn_act")
        turn_dve = ph.sem("turn_dve")
        pv_done = ph.sem("pv_done")
        u_copied = ph.sem("u_copied")
        out_made = ph.sem("out_made")
        inverted = ph.sem("inverted")
        summed = ph.sem("summed")
        dve_passed = ph.sem("dve_passed")
        pool_passed = ph.sem("pool_passed")
        block = ph.block()

        NG = len(TURN_GROUPS)

        def drive(eng, first, step, last):
            with eng.Fori(0, B) as b:
                first(b)
                if heads > 1:
                    with eng.Fori(0, (heads - 2) // 2) as k:
                        step(b, 2 * k + 1, 1, False)
                        step(b, 2 * k + 2, 0, False)
                    step(b, heads - 1, 1, True)
                last(b)

        @block.sync
        def _(sp):
            with sp.Fori(0, B) as b:
                sp.wait_ge(staged_out, 3 * b + 3)
                sp.dma_start(ctxT_in[:, :], io["ctxT"][bass.ds(b, 1), :, :].rearrange("a c s -> (a c) s")).then_inc(ctx_loaded, 16)
                sp.dma_start(ctx_in[:, :, :], io["ctx"][bass.ds(b, 1), :, :, :].rearrange("a p k c -> (a p) k c")).then_inc(ctx_loaded, 16)
                if masked:
                    sp.dma_start(mask_in[:, :], io["mask"][bass.ds(b, 1), :].to_broadcast([P, MASK_WORDS])).then_inc(mask_loaded, 16)

        @block.gpsimd
        def _(pool):
            pool.sem_inc(staged_out, 3)
            if not masked:
                pool.memset(bias[:, :], 0.0).then_inc(bias_ready, 1)

            def slot(b, h, par):
                n = b * heads + h
                pool.wait_ge(g_made, n + 1)
                pool.sem_inc(pool_passed, 1)
                pool.tensor_copy(a_slot[par][:, :, :], st.A[:, :, bass.ts(h, C)]).then_inc(a_ready, 1)

            def first(b):
                pool.wait_ge(ctx_loaded, 32 * b + 32)
                pool.wait_ge(scored, 2 * heads * b + 1)
                pool.sem_inc(pool_passed, 1)
                pool.tensor_copy(ctxT[:, :], ctxT_in[:, 0:S]).then_inc(ctxT_ready, 1)
                pool.wait_ge(ctxT_ready, b + 1)
                pool.sem_inc(staged_out, 1)
                if masked:
                    pool.wait_ge(mask_loaded, 16 * b + 16)
                    pool.wait_ge(maxed, 2 * heads * b + 1)
                    pool.sem_inc(pool_passed, 1)
                    pool.tensor_scalar(bias[:, :], mask_bytes, NEG, -NEG, ALU.mult, ALU.add).then_inc(bias_ready, 1)
                    pool.wait_ge(bias_ready, b + 1)
                pool.sem_inc(staged_out, 1)
                pool.wait_ge(pv_done, heads * b + 1)
                pool.sem_inc(pool_passed, 1)
                pool.tensor_copy(ctx[:, :, :], ctx_in[:, :, :]).then_inc(ctx_ready, 1)
                pool.wait_ge(ctx_ready, b + 1)
                pool.sem_inc(staged_out, 1)
                slot(b, 0, 0)
                if heads > 1:
                    slot(b, 1, 1)

            def step(b, h, par, at_end):
                if not at_end:
                    slot(b, h + 1, 1 - par)

            with pool.Fori(0, B) as b:
                first(b)
                if heads > 1:
                    with pool.Fori(0, (heads - 2) // 2) as k:
                        step(b, 2 * k + 1, 1, False)
                        step(b, 2 * k + 2, 0, False)

        @block.tensor
        def _(pe):
            pe.sem_inc(g_made, 2)
            pe.sem_inc(scored, 1)
            pe.sem_inc(pv_done, 1)
            pe.sem_inc(turned, 2 * NG)

            def scores(n, par, qt):
                pe.wait_ge(g_copied, n + 2)
                pe.wait_ge(maxed, 2 * n + qt + 1)
                for c, w in SCORE_CHUNKS:
                    ins = pe.matmul(ps_s[:, c:c + w], g_sb[par][:, qt * P:(qt + 1) * P], ctxT[:, c:c + w],
                                    start=True, stop=True)
                ins.then_inc(scored, 1)

            def make_g(b, n, par):
                pe.wait_ge(a_ready, n + 1)
                pe.wait_ge(g_copied, n + 1)
                for f in range(2):
                    ins = pe.matmul(ps_g, a_slot[par][:, f, :], st.XT[:, f, bass.ts(b, Q)],
                                    start=(f == 0), stop=(f == 1))
                ins.then_inc(g_made, 1)

            def turn(n, qt):
                pe.wait_ge(exped, 2 * n + qt + 3)
                for g, tiles in enumerate(TURN_GROUPS):
                    pe.wait_ge(turn_dve if g % 2 else turn_act, 4 * n + 2 * qt + g // 2 + 1)
                    for k in tiles:
                        w = min(P, S - k * P)
                        ins = pe.transpose(ps_t[g % 2][0:w, (k % 4) * P:(k % 4 + 1) * P],
                                           probs[qt][:, k * P:k * P + w], st.ident[:, :])
                    ins.then_inc(turned, 1)

            def pv(n, par):
                pe.wait_ge(turn_act, 4 * n + 5)
                pe.wait_ge(turn_dve, 4 * n + 5)
                for k in range(KT):
                    w = min(P, S - k * P)
                    ins = pe.matmul(ps_u, ctx[0:w, k, :], pT[par][0:w, k, :], start=(k == 0), stop=(k == KT - 1))
                ins.then_inc(pv_done, 1)

            def output(n, h):
                pe.wait_ge(u_copied, n + 1)
                pe.wait_ge(summed, n + 1)
                for qt in range(2):
                    ins = pe.matmul(ps_o[:, qt, :], u_sb[:, qt * P:(qt + 1) * P], st.Bw[:, bass.ts(h, D)],
                                    start=True, stop=True)
                ins.then_inc(out_made, 1)

            def first(b):
                n = b * heads
                make_g(b, n, 0)
                pe.wait_ge(ctxT_ready, b + 1)
                scores(n, 0, 0)
                if heads > 1:
                    make_g(b, n + 1, 1)
                scores(n, 0, 1)
                turn(n, 0)

            def step(b, h, par, at_end):
                n = b * heads + h
                scores(n, par, 0)
                if not at_end:
                    make_g(b, n + 1, 1 - par)
                    turn(n - 1, 1)
                    pe.wait_ge(g_copied, n + 3)
                else:
                    turn(n - 1, 1)
                pe.wait_ge(ctx_ready, b + 1)
                pv(n - 1, 1 - par)
                scores(n, par, 1)
                output(n - 1, h - 1)
                turn(n, 0)

            def last(b):
                n = b * heads + heads - 1
                turn(n, 1)
                pe.wait_ge(ctx_ready, b + 1)
                pv(n, (heads - 1) % 2)
                output(n, heads - 1)

            drive(pe, first, step, last)

        @block.vector
        def _(dve):
            dve.sem_inc(maxed, 1)
            dve.sem_inc(turn_dve, 1)
            dve.sem_inc(summed, 1)

            def rowmax(n, qt):
                dve.wait_ge(scored, 2 * n + qt + 2)
                dve.wait_ge(exped, 2 * n + qt + 1)
                dve.sem_inc(dve_passed, 1)
                dve.tensor_tensor_reduce(out=neg[qt][:, :], in0=ps_s[:, 0:S], in1=bias[:, :], scale=-1.0, scalar=BIG,
                                         op0=ALU.add, op1=ALU.min, accum_out=negmax[:, qt:qt + 1]).then_inc(maxed, 1)

            def copy_turned(n, qt, par):
                for g in (1, 3):
                    tiles = TURN_GROUPS[g]
                    w = min(P, S - tiles[0] * P)
                    dve.wait_ge(turned, NG * (2 * n + qt) + g + 1 + 2 * NG)
                    dve.tensor_copy(pT[par][0:w, tiles[0]:tiles[-1] + 1, qt * P:(qt + 1) * P],
                                    ps_t[1][0:w, 0:P * len(tiles)].rearrange("p (k q) -> p k q", q=P)).then_inc(turn_dve, 1)

            def accumulate(b, n, par):
                dve.wait_ge(exped, 2 * n + 4)
                dve.wait_ge(summed, n + 1)
                dve.reciprocal(inv[:, :], rowsum[:, par, :]).then_inc(inverted, 1)
                dve.wait_ge(inverted, n + 1)
                dve.wait_ge(out_made, n + 1)
                for qt in range(2):
                    if into_context:
                        ins = dve.tensor_scalar(st.MC[:, 2 * b + qt, :], ps_o[:, qt, :], inv[:, qt:qt + 1], None, ALU.mult)
                    else:
                        ins = dve.scalar_tensor_tensor(out=st.X[:, 2 * b + qt, :], in0=ps_o[:, qt, :],
                                                       scalar=inv[:, qt:qt + 1], in1=st.X[:, 2 * b + qt, :],
                                                       op0=ALU.mult, op1=ALU.add)
                ins.then_inc(summed, 1)

            def first(b):
                n = b * heads
                dve.wait_ge(bias_ready, b + 1 if masked else 1)
                rowmax(n, 0)
                rowmax(n, 1)
                copy_turned(n, 0, 0)

            def step(b, h, par, at_end):
                n = b * heads + h
                rowmax(n, 0)
                copy_turned(n - 1, 1, 1 - par)
                rowmax(n, 1)
                accumulate(b, n - 1, 1 - par)
                copy_turned(n, 0, par)

            def last(b):
                n = b * heads + heads - 1
                copy_turned(n, 1, (heads - 1) % 2)
                accumulate(b, n, (heads - 1) % 2)

            drive(dve, first, step, last)

        @block.scalar
        def _(act):
            act.sem_inc(g_copied, 1)
            act.sem_inc(exped, 2)
            act.sem_inc(turn_act, 1)

            def copy_g(n, par):
                act.wait_ge(g_made, n + 3)
                act.activation(g_sb[par][:, :], ps_g, ACT.Copy).then_inc(g_copied, 1)

            def exponential(n, par, qt):
                act.wait_ge(maxed, 2 * n + qt + 2)
                act.wait_ge(turned, NG * (2 * n + qt + 1))
                act.activation(probs[qt][:, :], neg[qt][:, :], ACT.Exp, scale=-1.0, bias=negmax[:, qt:qt + 1],
                               accum_out=rowsum[:, par, qt:qt + 1]).then_inc(exped, 1)

            def copy_turned(n, qt, par):
                for g in (0, 2):
                    tiles = TURN_GROUPS[g]
                    act.wait_ge(turned, NG * (2 * n + qt) + g + 1 + 2 * NG)
                    act.activation(pT[par][:, tiles[0]:tiles[-1] + 1, qt * P:(qt + 1) * P],
                                   ps_t[0][:, :].rearrange("p (k q) -> p k q", q=P), ACT.Copy).then_inc(turn_act, 1)

            def copy_u(n):
                act.wait_ge(pv_done, n + 2)
                act.activation(u_sb[:, :], ps_u, ACT.Copy).then_inc(u_copied, 1)

            def first(b):
                n = b * heads
                copy_g(n, 0)
                if heads > 1:
                    copy_g(n + 1, 1)
                exponential(n, 0, 0)
                copy_turned(n, 0, 0)
                exponential(n, 0, 1)

            def step(b, h, par, at_end):
                n = b * heads + h
                if not at_end:
                    copy_g(n + 1, 1 - par)
                copy_turned(n - 1, 1, 1 - par)
                exponential(n, par, 0)
                copy_u(n - 1)
                copy_turned(n, 0, par)
                exponential(n, par, 1)

            def last(b):
                n = b * heads + heads - 1
                copy_turned(n, 1, (heads - 1) % 2)
                copy_u(n)

            drive(act, first, step, last)


def grouped_attention_phase(nc, st, io, name, heads, width):
    HG = P // width
    NJ = heads // HG
    J_ALL = B * NJ
    NG = len(TURN_GROUPS)
    UNITS = 5
    assert HG == 2 and NG == 4 and NJ % 2 == 0
    PV_TILES = [range(0, 4), range(4, 8), range(8, KT)]
    with Phase(nc, name) as ph:
        ctx_in = ph.sb("ctx_in", [P, S_EVEN])
        ctx_hi = ph.sb("ctx_hi", [P, S_EVEN], F32R)
        ctx_lo = ph.sb("ctx_lo", [P, S_EVEN], F32R)
        mask_in = ph.sb("mask_in", [P, MASK_WORDS], I32)
        mask_bytes = mask_in[:, :].bitcast(U8)[:, 0:S]
        bias = ph.sb("bias", [P, S])
        x_hi = ph.sb("x_hi", [P, 2, Q], F32R)
        x_lo = ph.sb("x_lo", [P, 2, Q], F32R)
        a_hi = [ph.sb(f"a_hi{i}", [P, 2, C], F32R) for i in range(2)]
        a_lo = [ph.sb(f"a_lo{i}", [P, 2, C], F32R) for i in range(2)]
        wv_hi = [ph.sb(f"wv_hi{i}", [P, P], F32R) for i in range(2)]
        wv_lo = [ph.sb(f"wv_lo{i}", [P, P], F32R) for i in range(2)]
        g_hi = [ph.sb(f"g_hi{i}", [P, Q], F32R) for i in range(2)]
        g_lo = [ph.sb(f"g_lo{i}", [P, Q], F32R) for i in range(2)]
        probs = [ph.sb(f"probs{i}", [P, S]) for i in range(2)]
        negmax = ph.sb("negmax", [P, 2])
        rowsum = ph.sb("rowsum", [P, 2, HG, 2])
        inv = ph.sb("inv", [P, HG, 2])
        pT = [[ph.sb(f"pT{i}{k}", [P, KT, Q]) for k in range(HG)] for i in range(2)]
        v_sb = [ph.sb(f"v_sb{i}", [P, KT, P]) for i in range(2)]
        inv_rows = ph.sb("inv_rows", [P, Q])
        u_sb = ph.sb("u_sb", [P, Q])
        ps_s = ph.ps("ps_s", [P, 4 * BANK])
        ps_t = [ph.ps(f"ps_t{i}", [P, BANK]) for i in range(2)]
        ps_u = ph.ps("ps_u", [P, BANK])
        ps_m = ph.ps("ps_m", [P, BANK])

        ctx_loaded = ph.sem("ctx_loaded")
        mask_loaded = ph.sem("mask_loaded")
        staged_out = ph.sem("staged_out")
        halves = ph.sem("halves")
        x_ready = ph.sem("x_ready")
        ctx_ready = ph.sem("ctx_ready")
        bias_ready = ph.sem("bias_ready")
        a_ready = ph.sem("a_ready")
        wv_ready = ph.sem("wv_ready")
        g_made = ph.sem("g_made")
        g_hi_ready = ph.sem("g_hi_ready")
        g_ready = ph.sem("g_ready")
        scored = ph.sem("scored")
        maxed = ph.sem("maxed")
        exped = ph.sem("exped")
        turned = ph.sem("turned")
        turn_act = ph.sem("turn_act")
        turn_dve = ph.sem("turn_dve")
        inverted = ph.sem("inverted")
        inv_spread = ph.sem("inv_spread")
        inv_copied = ph.sem("inv_copied")
        pv_done = ph.sem("pv_done")
        u_ready = ph.sem("u_ready")
        out_made = ph.sem("out_made")
        x_added = ph.sem("x_added")
        dve_passed = ph.sem("dve_passed")
        pool_passed = ph.sem("pool_passed")
        block = ph.block()

        def drive(eng, start, body, finish):
            start()
            with eng.Fori(0, B - 1) as b:
                with eng.Fori(0, NJ // 2) as p:
                    body(NJ * b + 2 * p + 1, 1, b, 2 * p)
                    body(NJ * b + 2 * p + 2, 0, b, 2 * p + 1)
            b = B - 1
            with eng.Fori(0, NJ // 2 - 1) as p:
                body(NJ * b + 2 * p + 1, 1, b, 2 * p)
                body(NJ * b + 2 * p + 2, 0, b, 2 * p + 1)
            body(J_ALL - 1, 1, b, NJ - 2, last=True)
            finish(J_ALL, 0, b, NJ - 1)

        @block.sync
        def _(sp):
            with sp.Fori(0, B) as b:
                sp.wait_ge(staged_out, 2 * b + 2)
                sp.dma_start(ctx_in[:, :], io["ctxT"][bass.ds(b, 1), :, :].rearrange("a c s -> (a c) s")).then_inc(ctx_loaded, 16)
                sp.dma_start(mask_in[:, :], io["mask"][bass.ds(b, 1), :].to_broadcast([P, MASK_WORDS])).then_inc(mask_loaded, 16)

        @block.gpsimd
        def _(pool):
            pool.sem_inc(staged_out, 2)
            PER_BATCH = 2 + 3 * NJ

            def split(hi, lo, src, nth, ready):
                pool.sem_inc(pool_passed, 1)
                pool.tensor_copy(hi, src).then_inc(halves, 1)
                pool.wait_ge(halves, nth)
                pool.sem_inc(pool_passed, 1)
                pool.tensor_tensor(lo, src, hi.bitcast(F32), ALU.subtract).then_inc(ready, 1)

            def a_slot(n, h, par, nth):
                pool.wait_ge(g_made, n + 1)
                split(a_hi[par][:, :, :], a_lo[par][:, :, :], st.A[:, :, bass.ts(h, C)], nth, a_ready)

            def wv_slot(J, j, par, nth):
                pool.wait_ge(g_made, HG * J + 1)
                split(wv_hi[par][:, :], wv_lo[par][:, :], st.Wv[:, bass.ts(j, P)], nth, wv_ready)

            with pool.Fori(0, B) as b:
                s0 = PER_BATCH * b
                n0 = heads * b
                pool.wait_ge(g_made, n0 + 2)
                split(x_hi[:, :, :], x_lo[:, :, :], st.XT[:, :, bass.ts(b, Q)], s0 + 1, x_ready)
                a_slot(n0, 0, 0, s0 + 2)
                pool.wait_ge(ctx_loaded, 16 * b + 16)
                pool.wait_ge(scored, 2 * n0 + 1)
                split(ctx_hi[:, :], ctx_lo[:, :], ctx_in[:, :], s0 + 3, ctx_ready)
                pool.wait_ge(mask_loaded, 16 * b + 16)
                pool.wait_ge(maxed, 2 * n0 + 1)
                pool.sem_inc(pool_passed, 1)
                pool.tensor_scalar(bias[:, :], mask_bytes, NEG, -NEG, ALU.mult, ALU.add).then_inc(bias_ready, 1)
                wv_slot(NJ * b, 0, 0, s0 + 4)
                a_slot(n0 + 1, 1, 1, s0 + 5)
                pool.wait_ge(ctx_ready, b + 1)
                pool.wait_ge(bias_ready, b + 1)
                pool.sem_inc(staged_out, 2)

                def group(j, par, nth):
                    a_slot(n0 + HG * j, HG * j, 0, nth)
                    wv_slot(NJ * b + j, j, par, nth + 1)
                    a_slot(n0 + HG * j + 1, HG * j + 1, 1, nth + 2)

                with pool.Fori(0, NJ // 2 - 1) as p:
                    group(2 * p + 1, 1, s0 + 6 + 6 * p)
                    group(2 * p + 2, 0, s0 + 9 + 6 * p)
                group(NJ - 1, 1, s0 + 6 + 3 * (NJ - 2))

        @block.tensor
        def _(pe):
            pe.sem_inc(g_made, 2)
            pe.sem_inc(scored, 1)

            def scores(n, par, qt):
                pe.wait_ge(g_ready, n + 1)
                pe.wait_ge(maxed, 2 * n + qt + 1)
                hi, lo = (g[par][:, qt * P:(qt + 1) * P] for g in (g_hi, g_lo))
                for g, c_part, first, final in ((hi, ctx_hi, True, False), (hi, ctx_lo, False, False),
                                                (lo, ctx_hi, False, True)):
                    for c, w in EVEN_CHUNKS:
                        ins = pe.matmul(ps_s[:, c:c + w], g, c_part[:, c:c + w], start=first, stop=final)
                ins.then_inc(scored, 1)

            def make_g(n, par):
                pe.wait_ge(a_ready, n + 1)
                steps = [(a[par], x, f) for a, x in ((a_hi, x_hi), (a_hi, x_lo), (a_lo, x_hi)) for f in range(2)]
                for i, (a, x, f) in enumerate(steps):
                    ins = pe.matmul(ps_m[:, 0:Q], a[:, f, :], x[:, f, :], start=(i == 0), stop=(i == len(steps) - 1))
                ins.then_inc(g_made, 1)

            def bank_free(u, g):
                if g == 1:
                    pe.wait_ge(turn_dve, u + 1)
                else:
                    pe.wait_ge(turn_act, 3 * u + (0, 0, 1, 2)[g] + 1)

            def turn(u, tile, qt, groups):
                pe.wait_ge(exped, tile + 1)
                for g in groups:
                    bank_free(u, g)
                    for k in TURN_GROUPS[g]:
                        w = min(P, S - k * P)
                        ins = pe.transpose(ps_t[g == 1][0:w, (k % 4) * P:(k % 4 + 1) * P],
                                           probs[qt][:, k * P:k * P + w], st.ident[:, :])
                    ins.then_inc(turned, 1)

            def make_v(J, u, par):
                pe.wait_ge(wv_ready, J + 1)
                for g, tiles in enumerate(TURN_GROUPS):
                    bank_free(u, g)
                    for k in tiles:
                        w = min(P, S_EVEN - k * P)
                        out = ps_t[g == 1][0:w, (k % 4) * P:(k % 4 + 1) * P]
                        c = slice(k * P, k * P + w)
                        pe.matmul(out, ctx_hi[:, c], wv_hi[par][:, :], start=True, stop=False)
                        pe.matmul(out, ctx_hi[:, c], wv_lo[par][:, :], start=False, stop=False)
                        ins = pe.matmul(out, ctx_lo[:, c], wv_hi[par][:, :], start=False, stop=True)
                    ins.then_inc(turned, 1)

            def pv(par, part):
                for k in PV_TILES[part]:
                    w = min(P, S - k * P)
                    for i in range(HG):
                        ins = pe.matmul(ps_u[i * width:(i + 1) * width, 0:Q],
                                        v_sb[par][0:w, k, i * width:(i + 1) * width], pT[par][i][0:w, k, :],
                                        start=(k == 0), stop=(k == KT - 1))
                if part == len(PV_TILES) - 1:
                    ins.then_inc(pv_done, 1)

            def spread_inverse(J):
                pe.wait_ge(inverted, J)
                for qt in range(2):
                    for i in range(HG):
                        ins = pe.matmul(ps_m[i * width:(i + 1) * width, Q + qt * P:Q + (qt + 1) * P],
                                        inv[:, i, qt:qt + 1].to_broadcast([P, width]), st.ident[:, :],
                                        start=True, stop=True)
                ins.then_inc(inv_spread, 1)

            def output(J, jf):
                pe.wait_ge(u_ready, J)
                pe.wait_ge(inv_copied, J)
                for qt in range(2):
                    ins = pe.matmul(ps_m[:, qt * D:(qt + 1) * D], u_sb[:, qt * P:(qt + 1) * P],
                                    st.Wo[:, bass.ts(jf, D)], start=True, stop=True)
                ins.then_inc(out_made, 1)

            def start():
                make_g(0, 0)
                make_v(0, 0, 0)
                scores(0, 0, 0)
                make_g(1, 1)
                scores(0, 0, 1)
                turn(1, 0, 0, range(NG))
                scores(1, 1, 0)
                turn(2, 1, 1, range(NG))
                scores(1, 1, 1)
                turn(3, 2, 0, range(NG))
                pe.wait_ge(g_ready, 2)
                make_g(2, 0)
                make_v(1, 4, 1)

            def body(J, par, bf, jf, last=False):
                n, u = HG * J, UNITS * J
                scores(n, 0, 0)
                turn(u, 2 * n - 1, 1, (0, 1, 2))
                make_g(n + 1, 1)
                turn(u, 2 * n - 1, 1, (3,))
                pe.wait_ge(turn_act, 3 * u + 4)
                pe.wait_ge(turn_dve, u + 2)
                pv(1 - par, 0)
                scores(n, 0, 1)
                turn(u + 1, 2 * n, 0, (0, 1, 2))
                pe.wait_ge(g_ready, n + 2)
                spread_inverse(J)
                turn(u + 1, 2 * n, 0, (3,))
                pv(1 - par, 1)
                scores(n + 1, 1, 0)
                turn(u + 2, 2 * n + 1, 1, (0, 1, 2))
                pv(1 - par, 2)
                turn(u + 2, 2 * n + 1, 1, (3,))
                scores(n + 1, 1, 1)
                output(J, jf)
                turn(u + 3, 2 * n + 2, 0, (0, 1, 2))
                pe.wait_ge(x_added, J)
                if not last:
                    make_g(n + 2, 0)
                turn(u + 3, 2 * n + 2, 0, (3,))
                if not last:
                    make_v(J + 1, u + 4, 1 - par)

            def finish(J, par, bf, jf):
                u = UNITS * J - 1
                turn(u, 2 * HG * J - 1, 1, range(NG))
                pe.wait_ge(turn_act, 3 * u + 4)
                pe.wait_ge(turn_dve, u + 2)
                for part in range(len(PV_TILES)):
                    pv(1 - par, part)
                spread_inverse(J)
                output(J, jf)

            drive(pe, start, body, finish)

        @block.vector
        def _(dve):
            dve.sem_inc(maxed, 1)
            dve.sem_inc(turn_dve, 1)

            def rowmax(tile, qt, turned_groups):
                dve.wait_ge(scored, tile + 2)
                if turned_groups is not None:
                    dve.wait_ge(turned, turned_groups)
                dve.sem_inc(dve_passed, 1)
                dve.tensor_tensor_reduce(out=probs[qt][:, :], in0=ps_s[:, 0:S], in1=bias[:, :], scale=-1.0, scalar=BIG,
                                         op0=ALU.add, op1=ALU.min, accum_out=negmax[:, qt:qt + 1]).then_inc(maxed, 1)

            def take(u, to):
                dve.wait_ge(turned, NG * u + 2)
                dve.tensor_copy(to, ps_t[1][:, :].rearrange("p (k q) -> p k q", q=P)).then_inc(turn_dve, 1)

            def take_probs(u, par, i, qt):
                take(u, pT[par][i][:, 4:8, qt * P:(qt + 1) * P])

            def take_v(u, par):
                take(u, v_sb[par][:, 4:8, :])

            def g_low(n, par):
                dve.wait_ge(g_hi_ready, n + 1)
                dve.tensor_tensor(g_lo[par][:, :], ps_m[:, 0:Q], g_hi[par][:, :].bitcast(F32), ALU.subtract).then_inc(g_ready, 1)

            def invert(J, par):
                dve.wait_ge(exped, 2 * HG * J)
                dve.reciprocal(inv[:, :, :], rowsum[:, par, :, :]).then_inc(inverted, 1)

            def normalise(J):
                dve.wait_ge(inv_copied, J)
                dve.wait_ge(pv_done, J)
                dve.tensor_tensor(u_sb[:, :], ps_u[:, 0:Q], inv_rows[:, :], ALU.mult).then_inc(u_ready, 1)

            def add(J, bf):
                dve.wait_ge(out_made, J)
                x = st.X[:, bass.ds(2 * bf, 2), :]
                dve.tensor_tensor(x, ps_m[:, :].rearrange("p (t d) -> p t d", t=2), x, ALU.add).then_inc(x_added, 1)

            def start():
                g_low(0, 0)
                take_v(0, 0)
                rowmax(0, 0, None)
                g_low(1, 1)
                rowmax(1, 1, None)
                take_probs(1, 0, 0, 0)
                rowmax(2, 0, NG * 2)
                take_probs(2, 0, 0, 1)
                rowmax(3, 1, NG * 3)
                take_probs(3, 0, 1, 0)
                g_low(2, 0)
                take_v(4, 1)

            def body(J, par, bf, jf, last=False):
                n, u = HG * J, UNITS * J
                rowmax(2 * n, 0, NG * (u - 1))
                take_probs(u, 1 - par, 1, 1)
                g_low(n + 1, 1)
                invert(J, 1 - par)
                rowmax(2 * n + 1, 1, NG * (u + 1))
                take_probs(u + 1, par, 0, 0)
                rowmax(2 * n + 2, 0, NG * (u + 2))
                take_probs(u + 2, par, 0, 1)
                normalise(J)
                rowmax(2 * n + 3, 1, NG * (u + 3))
                add(J, bf)
                take_probs(u + 3, par, 1, 0)
                if not last:
                    g_low(n + 2, 0)
                    take_v(u + 4, 1 - par)

            def finish(J, par, bf, jf):
                take_probs(UNITS * J - 1, 1 - par, 1, 1)
                invert(J, 1 - par)
                normalise(J)
                add(J, bf)

            drive(dve, start, body, finish)

        @block.scalar
        def _(act):
            act.sem_inc(turn_act, 1)

            def take(u, groups, to):
                for g in groups:
                    tiles = TURN_GROUPS[g]
                    w = min(P, S - tiles[0] * P)
                    act.wait_ge(turned, NG * u + g + 1)
                    act.activation(to(slice(0, w), slice(tiles[0], tiles[-1] + 1)),
                                   ps_t[0][0:w, 0:P * len(tiles)].rearrange("p (k q) -> p k q", q=P),
                                   ACT.Copy).then_inc(turn_act, 1)

            def take_probs(u, par, i, qt, groups):
                take(u, groups, lambda p, k: pT[par][i][p, k, qt * P:(qt + 1) * P])

            def take_v(u, par):
                take(u, (0, 2, 3), lambda p, k: v_sb[par][p, k, :])

            def g_high(n, par):
                act.wait_ge(g_made, n + 3)
                act.activation(g_hi[par][:, :], ps_m[:, 0:Q], ACT.Copy).then_inc(g_hi_ready, 1)

            def exponential(tile, par, i, qt):
                act.wait_ge(maxed, tile + 2)
                act.activation(probs[qt][:, :], probs[qt][:, :], ACT.Exp, scale=-1.0, bias=negmax[:, qt:qt + 1],
                               accum_out=rowsum[:, par, i, qt:qt + 1]).then_inc(exped, 1)

            def copy_inverse(J):
                act.wait_ge(inv_spread, J)
                act.activation(inv_rows[:, :], ps_m[:, Q:2 * Q], ACT.Copy).then_inc(inv_copied, 1)

            def start():
                g_high(0, 0)
                take_v(0, 0)
                g_high(1, 1)
                exponential(0, 0, 0, 0)
                take_probs(1, 0, 0, 0, (0, 2, 3))
                exponential(1, 0, 0, 1)
                take_probs(2, 0, 0, 1, (0, 2, 3))
                exponential(2, 0, 1, 0)
                take_probs(3, 0, 1, 0, (0, 2, 3))
                g_high(2, 0)
                take_v(4, 1)
                exponential(3, 0, 1, 1)

            def body(J, par, bf, jf, last=False):
                n, u = HG * J, UNITS * J
                take_probs(u, 1 - par, 1, 1, (0, 2))
                g_high(n + 1, 1)
                take_probs(u, 1 - par, 1, 1, (3,))
                exponential(2 * n, par, 0, 0)
                take_probs(u + 1, par, 0, 0, (0, 2))
                copy_inverse(J)
                take_probs(u + 1, par, 0, 0, (3,))
                exponential(2 * n + 1, par, 0, 1)
                take_probs(u + 2, par, 0, 1, (0, 2, 3))
                exponential(2 * n + 2, par, 1, 0)
                take_probs(u + 3, par, 1, 0, (0, 2))
                if not last:
                    g_high(n + 2, 0)
                take_probs(u + 3, par, 1, 0, (3,))
                if not last:
                    take_v(u + 4, 1 - par)
                exponential(2 * n + 3, par, 1, 1)

            def finish(J, par, bf, jf):
                take_probs(UNITS * J - 1, 1 - par, 1, 1, (0, 2, 3))
                copy_inverse(J)

            drive(act, start, body, finish)


def narrow_attention_phase(nc, st, io, name, heads, width):
    HG = 4
    NJ = heads // HG
    J_ALL = B * NJ
    TILES = 2 * HG
    PAD = P // HG
    SCALE = width ** -0.5
    assert PAD == 4 * width and NJ == 4 and len(TURN_GROUPS) == 4 and len(EVEN_CHUNKS) == 4
    PV_TILES = [range(0, 4), range(4, 7), range(7, 10), range(10, KT)]

    FILL0, FILL1 = {}, {}
    for s in range(TILES):
        for g in (3, 0, 2):
            FILL0[g, s] = len(FILL0) + 1
        FILL1[s] = len(FILL1) + 1
        if s >= 5:
            FILL0["V", (0, 2, 3)[s - 5]] = len(FILL0) + 1
        if s == 5:
            FILL1["V"] = len(FILL1) + 1
    FILLS0, FILLS1 = len(FILL0), len(FILL1)
    START0, START1 = FILL0[3, 2] - 3, FILL1[1] - 1

    with Phase(nc, name) as ph:
        ctx_in = ph.sb("ctx_in", [P, S_EVEN])
        ctx = ph.sb("ctx", [P, S_EVEN])
        wq = ph.sb("wq", [P, 2, NJ, P])
        wk = ph.sb("wk", [P, NJ, P])
        wv = ph.sb("wv", [P, NJ, P])
        wo = ph.sb("wo", [P, NJ, D])
        picks = ph.sb("picks", [P, 2 + HG])
        zeros = ph.sb("zeros", [P, S])
        q_sb = ph.sb("q_sb", [P, Q])
        q_hi = ph.sb("q_hi", [P, Q], F32R)
        q_off = ph.sb("q_off", [P, Q])
        q_mixed = ph.sb("q_mixed", [P, Q])
        q_head = [[ph.sb(f"q_head{i}{k}", [P, Q], F32R) for k in range(HG)] for i in range(2)]
        k_sb = ph.sb("k_sb", [P, S_EVEN])
        k_hi = ph.sb("k_hi", [P, BANK], F32R)
        k_off = ph.sb("k_off", [P, BANK])
        k_mixed = [ph.sb(f"k_mixed{i}", [P, S_EVEN], F32R) for i in range(2)]
        probs = [ph.sb(f"probs{i}", [P, S]) for i in range(HG)]
        negmax = ph.sb("negmax", [P, HG])
        rowsum = ph.sb("rowsum", [P, 2, HG])
        inv = ph.sb("inv", [P, 2, HG])
        turned_size = KT * P
        spare = [st.A[:, :, :].rearrange("p a c -> p (a c)"), st.Bw[:, :]]
        pT = [[spare[i // 2][:, (i % 2) * turned_size:(i % 2 + 1) * turned_size].rearrange("p (k q) -> p k q", q=P)
               for i in range(HG)],
              [ph.sb(f"pT{i}", [P, KT, P])[:, :, :] for i in range(HG)]]
        v_sb = [ph.sb(f"v_sb{i}", [P, KT, P]) for i in range(2)]
        inv_rows = ph.sb("inv_rows", [P, P])
        u_sb = ph.sb("u_sb", [P, P])
        ps_s = ph.ps("ps_s", [P, 4 * BANK])
        ps_t = [ph.ps(f"ps_t{i}", [P, BANK]) for i in range(2)]
        ps_u = ph.ps("ps_u", [P, BANK])
        ps_m = ph.ps("ps_m", [P, BANK])

        weights_loaded = ph.sem("weights_loaded")
        ctx_loaded = ph.sem("ctx_loaded")
        ctx_ready = ph.sem("ctx_ready")
        zeros_ready = ph.sem("zeros_ready")
        q_made = ph.sem("q_made")
        q_taken = ph.sem("q_taken")
        q_ready = ph.sem("q_ready")
        k_made = ph.sem("k_made")
        k_taken = ph.sem("k_taken")
        k_ready = ph.sem("k_ready")
        steps = ph.sem("steps")
        scored = ph.sem("scored")
        maxed = ph.sem("maxed")
        exped = ph.sem("exped")
        turned = [ph.sem(f"turned{i}") for i in range(2)]
        taken = [ph.sem(f"taken{i}") for i in range(2)]
        inverted = ph.sem("inverted")
        inv_spread = ph.sem("inv_spread")
        inv_taken = ph.sem("inv_taken")
        pv_done = ph.sem("pv_done")
        u_ready = ph.sem("u_ready")
        out_made = ph.sem("out_made")
        x_added = ph.sem("x_added")
        dve_passed = ph.sem("dve_passed")
        pool_passed = ph.sem("pool_passed")
        block = ph.block()

        def drive(eng, group, finish):
            for j in range(NJ):
                group(0, j, j == 0, False)
            with eng.Fori(1, B - 1) as b:
                for j in range(NJ):
                    group(b, j, False, False)
            for j in range(NJ):
                group(B - 1, j, False, j == NJ - 1)
            finish()

        END0 = FILLS0 * J_ALL - 3
        END1 = FILLS1 * J_ALL - 1

        def fill0(J, key, last):
            skipped = sum(FILL0["V", g] < FILL0[key] for g in (0, 2, 3)) if last else 0
            return FILLS0 * J + FILL0[key] - skipped

        def fill1(J, key, last):
            skipped = 1 if last and FILL1["V"] < FILL1[key] else 0
            return FILLS1 * J + FILL1[key] - skipped

        @block.sync
        def _(sp):
            sp.dma_start(wq[:, :, :, :], io[f"{name}_wq"]).then_inc(weights_loaded, 16)
            sp.dma_start(wk[:, :, :], io[f"{name}_wk"]).then_inc(weights_loaded, 16)
            sp.dma_start(wv[:, :, :], io[f"{name}_wv"]).then_inc(weights_loaded, 16)
            sp.dma_start(wo[:, :, :], io[f"{name}_wo"]).then_inc(weights_loaded, 16)
            sp.dma_start(picks[:, :], io["copy_picks"]).then_inc(weights_loaded, 16)
            sp.dma_start(ctx_in[:, :], io["ctxT"][0, :, :]).then_inc(ctx_loaded, 16)
            with sp.Fori(1, B) as b:
                sp.wait_ge(ctx_ready, b)
                sp.dma_start(ctx_in[:, :], io["ctxT"][bass.ds(b, 1), :, :].rearrange("a c s -> (a c) s")).then_inc(ctx_loaded, 16)

        @block.gpsimd
        def _(pool):
            STEPS = 3 + 2 * 4

            def split_q(J, par):
                pool.wait_ge(q_taken, J + 1)
                pool.sem_inc(pool_passed, 1)
                pool.tensor_copy(q_hi[:, :], q_sb[:, :]).then_inc(steps, 1)
                pool.wait_ge(steps, STEPS * J + 1)
                pool.sem_inc(pool_passed, 1)
                pool.tensor_scalar(q_off[:, :], q_hi[:, :].bitcast(F32), picks[:, 0:1], None, ALU.mult).then_inc(steps, 1)
                pool.wait_ge(steps, STEPS * J + 2)
                pool.sem_inc(pool_passed, 1)
                pool.tensor_tensor(q_mixed[:, :], q_sb[:, :], q_off[:, :], ALU.subtract).then_inc(steps, 1)
                pool.wait_ge(steps, STEPS * J + 3)
                pool.sem_inc(pool_passed, 1)
                for i in range(HG):
                    pool.tensor_scalar(q_head[par][i][:, :], q_mixed[:, :], picks[:, 2 + i:3 + i], None,
                                       ALU.mult).then_inc(q_ready, 1)

            def split_k(J, par):
                for i, (c, w) in enumerate(EVEN_CHUNKS):
                    pool.wait_ge(k_taken, 4 * J + i + 1)
                    if i:
                        pool.wait_ge(k_ready, 4 * J + i)
                    pool.sem_inc(pool_passed, 1)
                    pool.tensor_copy(k_hi[:, 0:w], k_sb[:, c:c + w]).then_inc(steps, 1)
                    pool.wait_ge(steps, STEPS * J + 3 + 2 * i + 1)
                    pool.sem_inc(pool_passed, 1)
                    pool.tensor_scalar(k_off[:, 0:w], k_hi[:, 0:w].bitcast(F32), picks[:, 1:2], None,
                                       ALU.mult).then_inc(steps, 1)
                    pool.wait_ge(steps, STEPS * J + 3 + 2 * i + 2)
                    pool.sem_inc(pool_passed, 1)
                    pool.tensor_tensor(k_mixed[par][:, c:c + w], k_sb[:, c:c + w], k_off[:, 0:w],
                                       ALU.subtract).then_inc(k_ready, 1)

            def take_context(b):
                pool.wait_ge(ctx_loaded, 16 * b + 16)
                pool.sem_inc(pool_passed, 1)
                pool.tensor_copy(ctx[:, :], ctx_in[:, :]).then_inc(ctx_ready, 1)

            def group(b, j, first, last):
                J = NJ * b + j
                if last:
                    return
                if j == NJ - 1:
                    pool.wait_ge(turned[0], FILLS0 * J)
                    take_context(b + 1)
                split_q(J + 1, (j + 1) % 2)
                split_k(J + 1, (j + 1) % 2)

            take_context(0)
            pool.memset(zeros[:, :], 0.0).then_inc(zeros_ready, 1)
            pool.wait_ge(weights_loaded, 80)
            split_q(0, 0)
            split_k(0, 0)
            drive(pool, group, lambda: None)

        @block.tensor
        def _(pe):
            pe.sem_inc(turned[0], START0)
            pe.sem_inc(turned[1], START1)

            def make_q(b, j):
                for f in range(2):
                    ins = pe.matmul(ps_m[:, 0:Q], wq[:, f, j, :], st.XT[:, f, bass.ts(b, Q)], start=(f == 0), stop=(f == 1))
                ins.then_inc(q_made, 1)

            def make_k(j, i):
                c, w = EVEN_CHUNKS[i]
                pe.matmul(ps_m[:, 0:w], wk[:, j, :], ctx[:, c:c + w], start=True, stop=True).then_inc(k_made, 1)

            def fill(g, number, put):
                bank = int(g == 1)
                pe.wait_ge(taken[bank], number - 1)
                for k in TURN_GROUPS[g]:
                    ins = put(k, ps_t[bank][0:min(P, S - k * P), (k % 4) * P:(k % 4 + 1) * P])
                ins.then_inc(turned[bank], 1)

            def make_v(j, g, number):
                fill(g, number, lambda k, out: pe.matmul(out, ctx[:, k * P:min(k * P + P, S)], wv[:, j, :],
                                                         start=True, stop=True))

            def turn(s, g, number):
                fill(g, number, lambda k, out: pe.transpose(out, probs[s % HG][:, k * P:min(k * P + P, S)], st.ident[:, :]))

            def scores(t, s, par):
                qt, i = s // HG, s % HG
                for c, w in EVEN_CHUNKS:
                    ins = pe.matmul(ps_s[:, c:c + w], q_head[par][i][:, qt * P:(qt + 1) * P], k_mixed[par][:, c:c + w],
                                    start=True, stop=True)
                ins.then_inc(scored, 1)

            def pv(qt, par, part):
                for k in PV_TILES[part]:
                    w = min(P, S - k * P)
                    for i in range(HG):
                        ins = pe.matmul(ps_u[i * PAD:(i + 1) * PAD, 0:P], v_sb[par][0:w, k, i * PAD:(i + 1) * PAD],
                                        pT[qt][i][0:w, k, :], start=(k == 0), stop=(k == KT - 1))
                if part == len(PV_TILES) - 1:
                    ins.then_inc(pv_done, 1)

            def wait_turned(J, s, part, last):
                if part == 1:
                    pe.wait_ge(taken[1], fill1(J, s, last))
                else:
                    key = {0: (0, s), 2: (2, s), 3: (3, s + 1)}[part]
                    pe.wait_ge(taken[0], fill0(J, key, last))

            def spread_inverse(m, qt):
                pe.wait_ge(inverted, m + 1)
                for i in range(HG):
                    ins = pe.matmul(ps_m[i * PAD:(i + 1) * PAD, Q:Q + P], inv[:, qt, i:i + 1].to_broadcast([P, PAD]),
                                    st.ident[:, :], start=True, stop=True)
                ins.then_inc(inv_spread, 1)

            def output(m, j):
                pe.wait_ge(u_ready, m + 1)
                pe.matmul(ps_m[:, 0:D], u_sb[:, :], wo[:, j, :], start=True, stop=True).then_inc(out_made, 1)

            def group(b, j, first, last):
                J, par = NJ * b + j, j % 2
                before = (j - 1) % NJ
                b_next = b + 1 if j == NJ - 1 else b
                for s in range(TILES):
                    t = TILES * J + s
                    if s == 0:
                        pe.wait_ge(q_ready, HG * (J + 1))
                        pe.wait_ge(k_ready, 4 * (J + 1))
                    if not (first and s == 0):
                        pe.wait_ge(maxed, t)
                    scores(t, s, par)
                    if not first or s >= 3:
                        turn((s - 3) % TILES, 3, fill0(J, (3, s), last))
                    if not first or s >= 2:
                        pe.wait_ge(exped, t - 1)
                        turn((s - 2) % TILES, 1, fill1(J, s, last))
                        turn((s - 2) % TILES, 0, fill0(J, (0, s), last))
                    if s == 2 and not first:
                        if last:
                            pe.wait_ge(inv_taken, 2 * J - 1)
                        else:
                            pe.wait_ge(k_taken, 4 * (J + 1) + 1)
                        output(2 * J - 2, before)
                    if s == 4 and not first:
                        if last:
                            pe.wait_ge(x_added, 2 * J - 1)
                        else:
                            pe.wait_ge(k_taken, 4 * (J + 1) + 3)
                        spread_inverse(2 * J - 1, 1)
                    if s == 6 and not first:
                        if last:
                            pe.wait_ge(inv_taken, 2 * J)
                        else:
                            pe.wait_ge(k_taken, 4 * (J + 1) + 4)
                        output(2 * J - 1, before)
                    if s < 2 and not first:
                        wait_turned(J - 1, 5, s + 2, False)
                        pv(0, 1 - par, s + 2)
                    if 2 <= s < 6 and not first:
                        if s == 2:
                            pe.wait_ge(u_ready, 2 * J - 1)
                        wait_turned(J, 1, s - 2, last)
                        pv(1, 1 - par, s - 2)
                    if s >= 6:
                        if s == 6 and not first:
                            pe.wait_ge(u_ready, 2 * J)
                        wait_turned(J, 5, s - 6, last)
                        pv(0, par, s - 6)
                    if not first or s >= 2:
                        turn((s - 2) % TILES, 2, fill0(J, (2, s), last))
                    if s == 0:
                        if isinstance(b, int) and b == 0 and j < 2:
                            pe.wait_ge(k_taken, 4 * J + 4)
                        else:
                            pe.wait_ge(x_added, 2 * J - 2)
                        if not first:
                            spread_inverse(2 * J - 2, 0)
                        if not last:
                            make_q(b_next, (j + 1) % NJ)
                    if s == 1 and not last:
                        pe.wait_ge(q_taken, J + 2)
                        if not first:
                            pe.wait_ge(inv_taken, 2 * J - 1)
                        if j == NJ - 1:
                            pe.wait_ge(ctx_ready, b + 2)
                        make_k((j + 1) % NJ, 0)
                    if s == 2 and not last:
                        if first:
                            pe.wait_ge(k_taken, 4 * (J + 1) + 1)
                        else:
                            pe.wait_ge(x_added, 2 * J - 1)
                        make_k((j + 1) % NJ, 1)
                    if s == 3 and not last:
                        pe.wait_ge(k_taken, 4 * (J + 1) + 2)
                        make_k((j + 1) % NJ, 2)
                    if s == 4 and not last:
                        if first:
                            pe.wait_ge(k_taken, 4 * (J + 1) + 3)
                        else:
                            pe.wait_ge(inv_taken, 2 * J)
                        make_k((j + 1) % NJ, 3)
                    if s >= 5 and not last:
                        make_v((j + 1) % NJ, (0, 2, 3)[s - 5], fill0(J, ("V", (0, 2, 3)[s - 5]), False))
                    if s == 5 and not last:
                        make_v((j + 1) % NJ, 1, fill1(J, "V", False))

            def finish():
                J, par, j = J_ALL, 0, NJ - 1
                for s in range(3):
                    turn((s - 3) % TILES, 3, END0 + FILL0[3, s])
                    if s < 2:
                        pe.wait_ge(exped, TILES * J + s - 1)
                        turn((s - 2) % TILES, 1, END1 + FILL1[s])
                        turn((s - 2) % TILES, 0, END0 + FILL0[0, s])
                        wait_turned(J - 1, 5, s + 2, True)
                        pv(0, 1 - par, s + 2)
                        turn((s - 2) % TILES, 2, END0 + FILL0[2, s])
                pe.wait_ge(x_added, 2 * J - 2)
                spread_inverse(2 * J - 2, 0)
                pe.wait_ge(inv_taken, 2 * J - 1)
                output(2 * J - 2, j)
                pe.wait_ge(u_ready, 2 * J - 1)
                pe.wait_ge(taken[0], END0 + FILL0[3, 2])
                pe.wait_ge(taken[1], END1 + FILL1[1])
                for part in range(4):
                    pv(1, 1 - par, part)
                pe.wait_ge(x_added, 2 * J - 1)
                spread_inverse(2 * J - 1, 1)
                pe.wait_ge(inv_taken, 2 * J)
                output(2 * J - 1, j)

            pe.wait_ge(weights_loaded, 80)
            make_q(0, 0)
            pe.wait_ge(ctx_ready, 1)
            pe.wait_ge(q_taken, 1)
            make_k(0, 0)
            make_v(0, 0, START0 + 1)
            pe.wait_ge(k_taken, 1)
            make_k(0, 1)
            make_v(0, 1, START1 + 1)
            pe.wait_ge(k_taken, 2)
            make_k(0, 2)
            make_v(0, 2, START0 + 2)
            pe.wait_ge(k_taken, 3)
            make_k(0, 3)
            make_v(0, 3, START0 + 3)
            drive(pe, group, finish)

        @block.vector
        def _(dve):
            dve.sem_inc(taken[1], START1)

            def rowmax(t, s):
                dve.wait_ge(scored, t + 1)
                dve.sem_inc(dve_passed, 1)
                i = s % HG
                dve.tensor_tensor_reduce(out=probs[i][:, :], in0=ps_s[:, 0:S], in1=zeros[:, :], scale=-SCALE, scalar=BIG,
                                         op0=ALU.add, op1=ALU.min, accum_out=negmax[:, i:i + 1]).then_inc(maxed, 1)

            def take(number, to):
                dve.wait_ge(turned[1], number)
                dve.tensor_copy(to[:, 4:8, :], ps_t[1][:, :].rearrange("p (k q) -> p k q", q=P)).then_inc(taken[1], 1)

            def take_probs(s, number):
                take(number, pT[s // HG][s % HG])

            def take_k(J, i):
                c, w = EVEN_CHUNKS[i]
                dve.wait_ge(k_made, 4 * J + i + 1)
                dve.tensor_copy(k_sb[:, c:c + w], ps_m[:, 0:w]).then_inc(k_taken, 1)

            def invert(m, qt):
                dve.wait_ge(exped, HG * (m + 1))
                dve.reciprocal(inv[:, qt, :], rowsum[:, qt, :]).then_inc(inverted, 1)

            def normalise(m):
                dve.wait_ge(inv_taken, m + 1)
                dve.wait_ge(pv_done, m + 1)
                dve.tensor_tensor(u_sb[:, :], ps_u[:, 0:P], inv_rows[:, :], ALU.mult).then_inc(u_ready, 1)

            def add(m, row):
                dve.wait_ge(out_made, m + 1)
                x = st.X[:, bass.ds(row, 1), :].rearrange("p a d -> p (a d)")
                dve.tensor_tensor(x, ps_m[:, 0:D], x, ALU.add).then_inc(x_added, 1)

            def group(b, j, first, last):
                J, par = NJ * b + j, j % 2
                b_before = b - 1 if j == 0 else b
                for s in range(TILES):
                    rowmax(TILES * J + s, s)
                    if not first or s >= 2:
                        take_probs((s - 2) % TILES, fill1(J, s, last))
                    if s == 2 and not first:
                        add(2 * J - 2, 2 * b_before)
                        invert(2 * J - 1, 1)
                    if s == 6:
                        if not first:
                            add(2 * J - 1, 2 * b_before + 1)
                        invert(2 * J, 0)
                    if s in (1, 5) and not first:
                        normalise(2 * J - 2 + s // 4)
                    if s in (1, 2, 3, 4) and not last:
                        take_k(J + 1, s - 1)
                    if s == 5 and not last:
                        take(fill1(J, "V", False), v_sb[1 - par])

            def finish():
                J = J_ALL
                take_probs(TILES - 2, END1 + FILL1[0])
                take_probs(TILES - 1, END1 + FILL1[1])
                invert(2 * J - 1, 1)
                normalise(2 * J - 2)
                add(2 * J - 2, 2 * B - 2)
                normalise(2 * J - 1)
                add(2 * J - 1, 2 * B - 1)

            take_k(0, 0)
            take_k(0, 1)
            take(START1 + 1, v_sb[0])
            take_k(0, 2)
            take_k(0, 3)
            dve.wait_ge(zeros_ready, 1)
            drive(dve, group, finish)

        @block.scalar
        def _(act):
            act.sem_inc(taken[0], START0)

            def take(g, number, to):
                tiles = TURN_GROUPS[g]
                w = min(P, S - tiles[0] * P)
                act.wait_ge(turned[0], number)
                act.activation(to[0:w, tiles[0]:tiles[-1] + 1, :],
                               ps_t[0][0:w, 0:P * len(tiles)].rearrange("p (k q) -> p k q", q=P), ACT.Copy).then_inc(taken[0], 1)

            def take_probs(s, g, number):
                take(g, number, pT[s // HG][s % HG])

            def take_q(J):
                act.wait_ge(q_made, J + 1)
                act.activation(q_sb[:, :], ps_m[:, 0:Q], ACT.Copy).then_inc(q_taken, 1)

            def take_inverse(m):
                act.wait_ge(inv_spread, m + 1)
                act.activation(inv_rows[:, :], ps_m[:, Q:Q + P], ACT.Copy).then_inc(inv_taken, 1)

            def exponential(t, s):
                qt, i = s // HG, s % HG
                act.wait_ge(maxed, t + 1)
                act.activation(probs[i][:, :], probs[i][:, :], ACT.Exp, scale=-1.0, bias=negmax[:, i:i + 1],
                               accum_out=rowsum[:, qt, i:i + 1]).then_inc(exped, 1)

            def group(b, j, first, last):
                J, par = NJ * b + j, j % 2
                for s in range(TILES):
                    if not first or s >= 3:
                        take_probs((s - 3) % TILES, 3, fill0(J, (3, s), last))
                    if not first or s >= 2:
                        take_probs((s - 2) % TILES, 0, fill0(J, (0, s), last))
                    if s == 4 and not first:
                        take_inverse(2 * J - 1)
                    if not first or s >= 2:
                        take_probs((s - 2) % TILES, 2, fill0(J, (2, s), last))
                    exponential(TILES * J + s, s)
                    if s == 0:
                        if not last:
                            take_q(J + 1)
                        if not first:
                            take_inverse(2 * J - 2)
                    if s >= 5 and not last:
                        g = (0, 2, 3)[s - 5]
                        take(g, fill0(J, ("V", g), False), v_sb[1 - par])

            def finish():
                for s in range(3):
                    take_probs((s - 3) % TILES, 3, END0 + FILL0[3, s])
                    if s < 2:
                        take_probs((s - 2) % TILES, 0, END0 + FILL0[0, s])
                        take_probs((s - 2) % TILES, 2, END0 + FILL0[2, s])
                take_inverse(2 * J_ALL - 2)
                take_inverse(2 * J_ALL - 1)

            take_q(0)
            for n, g in enumerate((0, 2, 3)):
                take(g, START0 + 1 + n, v_sb[0])
            drive(act, group, finish)


def mlp_phase(nc, st, io, name, gate):
    F = 4 * D
    FT = F // P
    TC = BANK
    NC = B * Q // TC
    with Phase(nc, name) as ph:
        w1 = ph.sb("w1", [P, 2, F])
        w2 = ph.sb("w2", [P, FT, D])
        g = ph.sb("g", [P, 2])
        hid = [ph.sb(f"hid{i}", [P, FT, TC]) for i in range(2)]
        ps_h = [ph.ps(f"ps_h{i}", [P, TC]) for i in range(2)]
        ps_y = [ph.ps(f"ps_y{i}", [P, D]) for i in range(2)]
        loaded = ph.sem("loaded")
        gate_ready = ph.sem("gate_ready")
        hid_made = ph.sem("hid_made")
        hid_ready = ph.sem("hid_ready")
        y_made = ph.sem("y_made")
        y_added = ph.sem("y_added")
        block = ph.block()

        @block.sync
        def _(sp):
            sp.dma_start(w1[:, :, :], io[f"{name}_w1"]).then_inc(loaded, 16)
            sp.dma_start(w2[:, :, :], io[f"{name}_w2"]).then_inc(loaded, 16)
            sp.dma_start(g[:, 0:1], io[gate].to_broadcast([P, 1])).then_inc(loaded, 16)

        @block.tensor
        def _(pe):
            pe.wait_ge(loaded, 48)
            with pe.Fori(0, NC // 2) as i:
                for par in range(2):
                    c = 2 * i + par
                    for t in range(FT):
                        m = c * FT + t
                        pe.wait_ge(hid_ready, m + 1)
                        for f in range(2):
                            ins = pe.matmul(ps_h[t % 2][:, :], w1[:, f, t * P:(t + 1) * P], st.XT[:, f, bass.ts(c, TC)],
                                            start=(f == 0), stop=(f == 1))
                        ins.then_inc(hid_made, 1)
                for par in range(2):
                    c = 2 * i + par
                    pe.wait_ge(hid_ready, FT * (c + 1) + 2)
                    for r in range(TC // P):
                        pe.wait_ge(y_added, 4 * c + r + 1)
                        for t in range(FT):
                            ins = pe.matmul(ps_y[r % 2][:, :], hid[par][:, t, r * P:(r + 1) * P], w2[:, t, :],
                                            start=(t == 0), stop=(t == FT - 1))
                        ins.then_inc(y_made, 1)

        @block.scalar
        def _(act):
            act.sem_inc(hid_ready, 2)
            act.wait_ge(loaded, 48)
            act.activation(g[:, 1:2], g[:, 0:1], ACT.Tanh).then_inc(gate_ready, 1)
            with act.Fori(0, NC // 2) as i:
                for par in range(2):
                    for t in range(FT):
                        act.wait_ge(hid_made, (2 * i + par) * FT + t + 1)
                        act.activation(hid[par][:, t, :], ps_h[t % 2][:, :], ACT.Gelu).then_inc(hid_ready, 1)

        @block.vector
        def _(dve):
            dve.sem_inc(y_added, 2)
            dve.wait_ge(gate_ready, 1)
            with dve.Fori(0, NC) as c:
                for r in range(TC // P):
                    j = 4 * c + r
                    dve.wait_ge(y_made, j + 1)
                    dve.scalar_tensor_tensor(out=st.X[:, j, :], in0=ps_y[r % 2][:, :], scalar=g[:, 1:2],
                                             in1=st.X[:, j, :], op0=ALU.mult, op1=ALU.add).then_inc(y_added, 1)


def expert_masks_phase(nc, st, io):
    with Phase(nc, "masks") as ph:
        types = ph.sb("types", [P, B, Q], I32)
        is_one = ph.sb("is_one", [P, B, Q])
        pos_in = ph.sb("pos_in", [P, Q], I32)
        pos = ph.sb("pos", [P, 2, Q])
        rows = ph.sb("rows", [P, 2])
        onehot = ph.sb("onehot", [P, 2, Q])
        table = ph.sb("table", [P, 2, 24])
        picked = ph.ps("picked", [P, 2, 24])
        loaded = ph.sem("loaded")
        chain_sem = ph.sem("chain")
        onehot_ready = ph.sem("onehot_ready")
        picks_done = ph.sem("picks_done")
        block = ph.block()

        @block.sync
        def _(sp):
            sp.dma_start(types[:, :, :], io["types"].rearrange("b q -> (b q)").unsqueeze(0).to_broadcast([P, B * Q]).rearrange("p (b q) -> p b q", b=B)).then_inc(loaded, 16)
            sp.dma_start(pos_in[:, :], io["positions"].to_broadcast([P, Q])).then_inc(loaded, 16)
            sp.dma_start(rows[:, :], io["row_numbers"]).then_inc(loaded, 16)
            sp.dma_start(table[:, :, :], io["rope_table"]).then_inc(loaded, 16)
            sp.dma_start(st.head_rows[:, :], io["head_rows"]).then_inc(loaded, 16)

        @block.vector
        def _(dve):
            chain = Chain(dve, chain_sem)
            dve.wait_ge(loaded, 80)
            chain(dve.tensor_scalar(pos[:, 0, :], pos_in[:, :], 0.0, float(Q), ALU.is_lt, ALU.mult))
            chain(dve.tensor_tensor(pos[:, 1, :], pos_in[:, :], pos[:, 0, :], ALU.add))
            chain(dve.tensor_scalar(pos[:, 0, :], pos[:, 1, :], 0.0, float(Q - 1), ALU.max, ALU.min))
            for k in range(2):
                ins = dve.tensor_scalar(onehot[:, k, :], pos[:, 0, :], rows[:, k:k + 1], None, ALU.is_equal)
            ins.then_inc(onehot_ready, 1)
            chain(dve.tensor_scalar(is_one[:, :, :], types[:, :, :], 1.0, None, ALU.is_equal))
            dve.tensor_tensor(st.vm[:, :, 0:Q - 1], is_one[:, :, 0:Q - 1], is_one[:, :, 1:Q], ALU.mult)
            dve.memset(st.vm[:, :, Q - 1:Q], 0.0)
            dve.wait_ge(picks_done, 1)
            dve.tensor_copy(st.rope[:, :, :], picked[:, :, :])

        @block.tensor
        def _(pe):
            pe.wait_ge(onehot_ready, 1)
            for t in range(2):
                for k in range(2):
                    ins = pe.matmul(picked[:, t, :], onehot[:, k, t * P:(t + 1) * P], table[:, k, :],
                                    start=(k == 0), stop=(k == 1))
            ins.then_inc(picks_done, 1)


def self_attention_phase(nc, st, io):
    H, W = 16, 16
    with Phase(nc, "self") as ph:
        wqkv = ph.sb("wqkv", [P, 2, 2, 3 * D])
        wd = ph.sb("wd", [P, 2, 2, D])
        causal = ph.sb("causal", [P, Q])
        z = ph.sb("z", [P, 2, 2, Q])
        rot_a = ph.sb("rot_a", [P, 2, 2 * D])
        rot_b = ph.sb("rot_b", [P, 2, 2 * D])
        v_sb = ph.sb("v_sb", [P, 2, D])
        kT = ph.sb("kT", [P, 2, Q])
        qT = ph.sb("qT", [P, 2, Q])
        qm = ph.sb("qm", [P, H, Q])
        neg = ph.sb("neg", [P, 2, 3 * P])
        probs = ph.sb("probs", [P, 2, 3 * P])
        negmax = ph.sb("negmax", [P, 2, 2])
        rowsum = ph.sb("rowsum", [P, 2, H])
        inv = ph.sb("inv", [P, 2, H])
        pT = ph.sb("pT", [P, 2, 3 * P])
        o_sb = ph.sb("o_sb", [P, 2, D])
        oT = ph.sb("oT", [P, 2, 2, Q])
        ps_qk = [ph.ps(f"ps_qk{i}", [P, BANK]) for i in range(2)]
        ps_v = ph.ps("ps_v", [P, 2, D])
        ps_t = [ph.ps(f"ps_t{i}", [P, BANK]) for i in range(2)]
        ps_oT = ph.ps("ps_oT", [P, 2, Q])
        ps_y = ph.ps("ps_y", [P, 2, D])
        loaded = ph.sem("loaded")
        z_ready = ph.sem("z_ready")
        qk_made = ph.sem("qk_made")
        v_made = ph.sem("v_made")
        v_ready = ph.sem("v_ready")
        chain = ph.sem("chain")
        rot_ready = ph.sem("rot_ready")
        qkT_made = ph.sem("qkT_made")
        qkT_ready = ph.sem("qkT_ready")
        qm_ready = ph.sem("qm_ready")
        scored = ph.sem("scored")
        maxed = ph.sem("maxed")
        exped = ph.sem("exped")
        turned = ph.sem("turned")
        pT_ready = ph.sem("pT_ready")
        pv_done = ph.sem("pv_done")
        inverted = ph.sem("inverted")
        o_ready = ph.sem("o_ready")
        oT_made = ph.sem("oT_made")
        oT_ready = ph.sem("oT_ready")
        y_made = ph.sem("y_made")
        y_added = ph.sem("y_added")
        dve_passed = ph.sem("dve_passed")
        pool_passed = ph.sem("pool_passed")
        block = ph.block()

        @block.sync
        def _(sp):
            for e, n in enumerate("vl"):
                sp.dma_start(wqkv[:, e, :, :], io[f"L1_{n}_qkv"]).then_inc(loaded, 16)
                sp.dma_start(wd[:, e, :, :], io[f"L1_{n}_dense"]).then_inc(loaded, 16)
            sp.dma_start(causal[:, :], io["causal"]).then_inc(loaded, 16)

        @block.tensor
        def _(pe):
            pe.sem_inc(turned, 2)
            pe.sem_inc(pv_done, 2)
            pe.wait_ge(loaded, 80)
            with pe.Fori(0, B) as b:
                n0 = b * H
                pe.wait_ge(z_ready, b + 1)
                pe.wait_ge(y_added, b + 1)
                for t in range(2):
                    for i in range(4):
                        e, f = divmod(i, 2)
                        ins = pe.matmul(ps_qk[t][:, :], z[:, e, f, t * P:(t + 1) * P], wqkv[:, e, f, 0:2 * D],
                                        start=(i == 0), stop=(i == 3))
                    ins.then_inc(qk_made, 1)
                for t in range(2):
                    for i in range(4):
                        e, f = divmod(i, 2)
                        ins = pe.matmul(ps_v[:, t, :], z[:, e, f, t * P:(t + 1) * P], wqkv[:, e, f, 2 * D:3 * D],
                                        start=(i == 0), stop=(i == 3))
                ins.then_inc(v_made, 1)
                for t in range(2):
                    pe.wait_ge(rot_ready, 2 * b + t + 1)
                    for i in range(4):
                        ins = pe.transpose(ps_t[t][:, i * P:(i + 1) * P], rot_a[:, t, i * P:(i + 1) * P],
                                           st.ident[:, :])
                    ins.then_inc(qkT_made, 1)
                for h in range(H + 2):
                    if h < H:
                        n = n0 + h
                        f = h // 8
                        if h == 0:
                            pe.wait_ge(qkT_ready, 2 * b + 2)
                        pe.wait_ge(qm_ready, n + 1)
                        pe.wait_ge(maxed, 2 * n + 2)
                        s = ps_qk[h % 2]
                        pe.matmul(s[:, 0:P], qm[:, h, 0:P], kT[:, f, 0:P], start=True, stop=True)
                        pe.matmul(s[:, P:3 * P], qm[:, h, P:2 * P], kT[:, f, :], start=True, stop=True)\
                            .then_inc(scored, 1)
                    if 1 <= h <= H:
                        n = n0 + h - 1
                        p = (h - 1) % 2
                        pe.wait_ge(exped, 2 * n + 6)
                        pe.wait_ge(pT_ready, n + 1)
                        for i in range(3):
                            ins = pe.transpose(ps_t[p][:, i * P:(i + 1) * P], probs[:, p, i * P:(i + 1) * P],
                                               st.ident[:, :])
                        ins.then_inc(turned, 1)
                    if h >= 2:
                        n = n0 + h - 2
                        p = (h - 2) % 2
                        c = slice((h - 2) * W, (h - 1) * W)
                        pe.wait_ge(pT_ready, n + 3)
                        if h == 2:
                            pe.wait_ge(v_ready, b + 1)
                        pe.matmul(ps_v[:, 0, c], pT[:, p, 0:P], v_sb[:, 0, c], start=True, stop=True)
                        pe.matmul(ps_v[:, 1, c], pT[:, p, P:2 * P], v_sb[:, 0, c], start=True, stop=False)
                        pe.matmul(ps_v[:, 1, c], pT[:, p, 2 * P:3 * P], v_sb[:, 1, c], start=False, stop=True)\
                            .then_inc(pv_done, 1)
                pe.wait_ge(o_ready, b + 1)
                for f in range(2):
                    for t in range(2):
                        ins = pe.transpose(ps_oT[:, f, t * P:(t + 1) * P], o_sb[:, t, f * P:(f + 1) * P],
                                           st.ident[:, :])
                ins.then_inc(oT_made, 1)
                pe.wait_ge(oT_ready, b + 1)
                for t in range(2):
                    for i in range(4):
                        e, f = divmod(i, 2)
                        ins = pe.matmul(ps_y[:, t, :], oT[:, e, f, t * P:(t + 1) * P], wd[:, e, f, :],
                                        start=(i == 0), stop=(i == 3))
                ins.then_inc(y_made, 1)

        @block.vector
        def _(dve):
            dve.sem_inc(maxed, 4)
            dve.sem_inc(y_added, 1)
            dve.wait_ge(loaded, 80)

            def pick(to, src, b, sem, seen):
                for f in range(2):
                    ins = dve.tensor_tensor(to[:, 0, f, :], src[:, f, :], st.vm[:, bass.ds(b, 1), :].squeeze(1), ALU.mult)
                ins.then_inc(chain, 1)
                dve.wait_ge(chain, seen)
                dve.tensor_tensor(to[:, 1, :, :], src, to[:, 0, :, :], ALU.subtract).then_inc(sem, 1)

            with dve.Fori(0, B) as b:
                n0 = b * H
                k0 = 8 * b
                pick(z, st.XT[:, :, bass.ts(b, Q)], b, z_ready, k0 + 1)
                for t in range(2):
                    k = k0 + 1 + 3 * t
                    cos = st.rope[:, t, 0:8].unsqueeze(1).to_broadcast([P, 64, 8])
                    msin = st.rope[:, t, 8:16].unsqueeze(1).to_broadcast([P, 32, 8])
                    sin = st.rope[:, t, 16:24].unsqueeze(1).to_broadcast([P, 32, 8])
                    pairs = ps_qk[t][:, :].rearrange("p (g h e) -> p g h e", h=2, e=8)
                    rb = rot_b[:, t, :].rearrange("p (g h e) -> p g h e", h=2, e=8)
                    dve.wait_ge(qk_made, 2 * b + t + 1)
                    dve.tensor_tensor(rot_a[:, t, :].rearrange("p (g e) -> p g e", e=8),
                                      ps_qk[t][:, :].rearrange("p (g e) -> p g e", e=8), cos, ALU.mult).then_inc(chain, 1)
                    dve.tensor_tensor(rb[:, :, 0, :], pairs[:, :, 1, :], msin, ALU.mult).then_inc(chain, 1)
                    dve.tensor_tensor(rb[:, :, 1, :], pairs[:, :, 0, :], sin, ALU.mult).then_inc(chain, 1)
                    dve.wait_ge(chain, k + 3)
                    dve.tensor_tensor(rot_a[:, t, :], rot_a[:, t, :], rot_b[:, t, :], ALU.add).then_inc(rot_ready, 1)
                for h in range(H):
                    n = n0 + h
                    p = h % 2
                    dve.wait_ge(exped, 2 * n + 2)
                    dve.wait_ge(scored, n + 1)
                    dve.sem_inc(dve_passed, 1)
                    dve.tensor_tensor_reduce(out=neg[:, p, 0:P], in0=ps_qk[p][:, 0:P], in1=causal[:, P:2 * P],
                                             scale=-1.0, scalar=BIG, op0=ALU.add, op1=ALU.min,
                                             accum_out=negmax[:, p, 0:1]).then_inc(maxed, 1)
                    dve.tensor_tensor_reduce(out=neg[:, p, P:3 * P], in0=ps_qk[p][:, P:3 * P], in1=causal[:, :],
                                             scale=-1.0, scalar=BIG, op0=ALU.add, op1=ALU.min,
                                             accum_out=negmax[:, p, 1:2]).then_inc(maxed, 1)
                dve.wait_ge(exped, 2 * n0 + 2 * H + 4)
                dve.reciprocal(inv[:, :, :], rowsum[:, :, :]).then_inc(inverted, 1)
                dve.wait_ge(inverted, b + 1)
                dve.wait_ge(pv_done, n0 + H + 2)
                dve.tensor_tensor(o_sb[:, :, :].rearrange("p t (h w) -> p (t h) w", w=W),
                                  ps_v[:, :, :].rearrange("p t (h w) -> p (t h) w", w=W),
                                  inv[:, :, :].rearrange("p t h -> p (t h)").unsqueeze(2).to_broadcast([P, 2 * H, W]),
                                  ALU.mult).then_inc(o_ready, 1)
                dve.wait_ge(oT_made, b + 1)
                pick(oT, ps_oT[:, :, :], b, oT_ready, k0 + 8)
                dve.wait_ge(y_made, b + 1)
                dve.tensor_tensor(st.X[:, bass.ds(2 * b, 2), :], ps_y[:, :, :], st.X[:, bass.ds(2 * b, 2), :],
                                  ALU.add).then_inc(y_added, 1)

        @block.scalar
        def _(act):
            act.sem_inc(exped, 4)
            act.sem_inc(pT_ready, 2)
            with act.Fori(0, B) as b:
                n0 = b * H
                act.wait_ge(v_made, b + 1)
                act.activation(v_sb[:, :, :], ps_v[:, :, :], ACT.Copy).then_inc(v_ready, 1)
                for t in range(2):
                    act.wait_ge(qkT_made, 2 * b + t + 1)
                    act.activation(qT[:, :, t * P:(t + 1) * P],
                                   ps_t[t][:, 0:2 * P].rearrange("p (f q) -> p f q", f=2), ACT.Copy)
                    act.activation(kT[:, :, t * P:(t + 1) * P],
                                   ps_t[t][:, 2 * P:4 * P].rearrange("p (f q) -> p f q", f=2),
                                   ACT.Copy).then_inc(qkT_ready, 1)
                for h in range(H + 1):
                    if h < H:
                        n = n0 + h
                        p = h % 2
                        for t in range(2):
                            act.wait_ge(maxed, 2 * n + t + 5)
                            act.wait_ge(turned, n + 1)
                            cols = slice(0, P) if t == 0 else slice(P, 3 * P)
                            act.activation(probs[:, p, cols], neg[:, p, cols], ACT.Exp, scale=-1.0,
                                           bias=negmax[:, p, t:t + 1],
                                           accum_out=rowsum[:, t, h:h + 1]).then_inc(exped, 1)
                    if h >= 1:
                        n = n0 + h - 1
                        p = (h - 1) % 2
                        act.wait_ge(turned, n + 3)
                        act.wait_ge(pv_done, n + 1)
                        act.activation(pT[:, p, :], ps_t[p][:, 0:3 * P], ACT.Copy).then_inc(pT_ready, 1)

        @block.gpsimd
        def _(pool):
            with pool.Fori(0, B) as b:
                pool.wait_ge(qkT_ready, 2 * b + 2)
                pool.sem_inc(pool_passed, 1)
                for h in range(H):
                    pool.tensor_scalar(qm[:, h, :], qT[:, h // 8, :], st.head_rows[:, h % 8:h % 8 + 1], None,
                                       ALU.mult).then_inc(qm_ready, 1)


def expert_mlp_phase(nc, st, io):
    F = 688
    FT = (F + P - 1) // P
    TC = BANK
    NC = B * Q // TC
    with Phase(nc, "experts") as ph:
        wg = ph.sb("wg", [P, 2, 2, F])
        wu = ph.sb("wu", [P, 2, 2, F])
        wd = ph.sb("wd", [P, 2, FT, D])
        zv = ph.sb("zv", [P, 2, TC])
        zl = ph.sb("zl", [P, 2, TC])
        act_g = [ph.sb(f"act_g{i}", [P, TC]) for i in range(2)]
        hid = [ph.sb(f"hid{i}", [P, TC]) for i in range(2)]
        hx = ph.sb("hx", [P, 2, FT, TC])
        ps_g = [ph.ps(f"ps_g{i}", [P, TC]) for i in range(2)]
        ps_u = [ph.ps(f"ps_u{i}", [P, TC]) for i in range(2)]
        ps_y = [ph.ps(f"ps_y{i}", [P, D]) for i in range(2)]
        loaded = ph.sem("loaded")
        split = ph.sem("split")
        z_ready = ph.sem("z_ready")
        g_made = ph.sem("g_made")
        silu_done = ph.sem("silu_done")
        hid_ready = ph.sem("hid_ready")
        v_done = ph.sem("v_done")
        h_split = ph.sem("h_split")
        y_made = ph.sem("y_made")
        y_added = ph.sem("y_added")
        pool_passed = ph.sem("pool_passed")
        block = ph.block()

        @block.sync
        def _(sp):
            for e, n in enumerate("vl"):
                sp.dma_start(wg[:, e, :, :], io[f"L1_{n}_gate"]).then_inc(loaded, 16)
                sp.dma_start(wu[:, e, :, :], io[f"L1_{n}_up"]).then_inc(loaded, 16)
                sp.dma_start(wd[:, e, :, :], io[f"L1_{n}_down"]).then_inc(loaded, 16)

        vm_flat = st.vm[:, :, :].rearrange("p b q -> p (b q)")

        @block.tensor
        def _(pe):
            pe.sem_inc(g_made, 2)
            pe.wait_ge(loaded, 96)
            with pe.Fori(0, NC) as c:
                pe.wait_ge(z_ready, c + 1)
                for t in range(FT):
                    w = min(P, F - t * P)
                    m = c * FT + t
                    pe.wait_ge(hid_ready, m + 1)
                    for out, weights in ((ps_g, wg), (ps_u, wu)):
                        for i in range(4):
                            e, f = divmod(i, 2)
                            ins = pe.matmul(out[t % 2][0:w, :], weights[:, e, f, t * P:t * P + w],
                                            (zl if e else zv)[:, f, :], start=(i == 0), stop=(i == 3))
                    ins.then_inc(g_made, 1)
                pe.wait_ge(h_split, FT * (c + 1) + 2)
                for r in range(TC // P):
                    pe.wait_ge(y_added, 4 * c + r + 1)
                    for t in range(FT):
                        w = min(P, F - t * P)
                        for e in range(2):
                            ins = pe.matmul(ps_y[r % 2][:, :], hx[0:w, e, t, r * P:(r + 1) * P], wd[0:w, e, t, :],
                                            start=(t == 0 and e == 0), stop=(t == FT - 1 and e == 1))
                    ins.then_inc(y_made, 1)

        @block.scalar
        def _(act):
            with act.Fori(0, NC) as c:
                for t in range(FT):
                    w = min(P, F - t * P)
                    m = c * FT + t
                    act.wait_ge(hid_ready, m + 1)
                    act.wait_ge(g_made, m + 3)
                    act.activation(act_g[t % 2][0:w, :], ps_g[t % 2][0:w, :], ACT.Silu).then_inc(silu_done, 1)

        @block.vector
        def _(dve):
            dve.sem_inc(hid_ready, 2)
            dve.sem_inc(y_added, 2)
            with dve.Fori(0, NC) as c:
                dve.wait_ge(g_made, FT * c + 2)
                for f in range(2):
                    ins = dve.tensor_tensor(zv[:, f, :], st.XT[:, f, bass.ts(c, TC)], vm_flat[:, bass.ts(c, TC)],
                                            ALU.mult)
                ins.then_inc(split, 1)
                dve.wait_ge(split, c + 1)
                dve.tensor_tensor(zl[:, :, :], st.XT[:, :, bass.ts(c, TC)], zv[:, :, :],
                                  ALU.subtract).then_inc(z_ready, 1)
                for t in range(FT):
                    w = min(P, F - t * P)
                    m = c * FT + t
                    dve.wait_ge(h_split, m + 1)
                    dve.wait_ge(silu_done, m + 1)
                    dve.tensor_tensor(hid[t % 2][0:w, :], act_g[t % 2][0:w, :], ps_u[t % 2][0:w, :],
                                      ALU.mult).then_inc(hid_ready, 1)
                for r in range(TC // P):
                    j = 4 * c + r
                    dve.wait_ge(y_made, j + 1)
                    dve.tensor_tensor(st.X[:, bass.ds(j, 1), :].squeeze(1), ps_y[r % 2][:, :],
                                      st.X[:, bass.ds(j, 1), :].squeeze(1), ALU.add).then_inc(y_added, 1)

        @block.gpsimd
        def _(pool):
            pool.sem_inc(h_split, 2)
            with pool.Fori(0, NC) as c:
                pool.wait_ge(y_added, 4 * c + 2)
                for t in range(FT):
                    w = min(P, F - t * P)
                    m = c * FT + t
                    pool.wait_ge(hid_ready, m + 3)
                    pool.sem_inc(pool_passed, 1)
                    pool.tensor_tensor(hx[0:w, 0, t, :], hid[t % 2][0:w, :], vm_flat[0:w, bass.ts(c, TC)],
                                       ALU.mult).then_inc(v_done, 1)
                    pool.wait_ge(v_done, m + 1)
                    pool.tensor_tensor(hx[0:w, 1, t, :], hid[t % 2][0:w, :], hx[0:w, 0, t, :],
                                       ALU.subtract).then_inc(h_split, 1)


def memory_weights_phase(nc, st, io):
    with Phase(nc, "memw") as ph:
        w = ph.sb("w", [P, 2, C])
        loaded = ph.sem("loaded")
        block = ph.block()

        @block.sync
        def _(sp):
            sp.dma_start(w[:, :, :], io["L2_mem"]).then_inc(loaded, 16)
            sp.dma_start(st.Bw[:, 0:D], io["L2_memT"]).then_inc(loaded, 16)
            sp.wait_ge(loaded, 32)

        @block.vector
        def _(dve):
            dve.wait_ge(loaded, 32)
            dve.tensor_scalar(st.A[:, :, 0:C], w[:, :, :], D ** -0.5, None, ALU.mult)


def gate_phase(nc, st, io):
    with Phase(nc, "gate") as ph:
        wg = ph.sb("wg", [P, 4, D])
        bias = ph.sb("bias", [P, D])
        norm_w = ph.sb("norm_w", [P, D])
        mc = [ph.sb(f"mc{i}", [P, D]) for i in range(2)]
        zT = [ph.sb(f"zT{i}", [P, 4, P]) for i in range(2)]
        g = [ph.sb(f"g{i}", [P, D]) for i in range(2)]
        stats = ph.sb("stats", [P, NT, 6])
        rows = ph.sb("rows", [P, 4, NT])
        ps_t = [ph.ps(f"ps_t{i}", [P, BANK]) for i in range(2)]
        ps_z = [ph.ps(f"ps_z{i}", [P, D]) for i in range(2)]
        loaded = ph.sem("loaded")
        mc_ready = ph.sem("mc_ready")
        hs_ready = ph.sem("hs_ready")
        turned = ph.sem("turned")
        zT_ready = ph.sem("zT_ready")
        z_made = ph.sem("z_made")
        summed = ph.sem("summed")
        pool_passed = ph.sem("pool_passed")
        sig_done = ph.sem("sig_done")
        scaled = ph.sem("scaled")
        fused = ph.sem("fused")
        chain_sem = ph.sem("chain")
        root_asked = ph.sem("root_asked")
        root_taken = ph.sem("root_taken")
        block = ph.block()

        @block.sync
        def _(sp):
            sp.dma_start(wg[:, :, :], io["L2_gateT"]).then_inc(loaded, 16)
            sp.dma_start(bias[:, :], io["L2_gate_b"].to_broadcast([P, D])).then_inc(loaded, 16)
            sp.dma_start(norm_w[:, :], io["L2_norm_w"].to_broadcast([P, D])).then_inc(loaded, 16)

        @block.gpsimd
        def _(pool):
            pool.wait_ge(loaded, 48)
            with pool.Fori(0, NT // 2) as i:
                for par in range(2):
                    j = 2 * i + par
                    pool.wait_ge(turned, j + 1)
                    pool.sem_inc(pool_passed, 1)
                    pool.tensor_copy(mc[par][:, :], st.MC[:, bass.ds(j, 1), :].squeeze(1)).then_inc(mc_ready, 1)
                    pool.wait_ge(z_made, j + 1)
                    pool.sem_inc(pool_passed, 1)
                    pool.tensor_copy(zT[par][:, 0:2, :], st.XT[:, :, bass.ts(j, P)]).then_inc(hs_ready, 1)

        @block.tensor
        def _(pe):
            pe.sem_inc(turned, 2)
            pe.sem_inc(z_made, 2)
            pe.wait_ge(loaded, 48)
            with pe.Fori(0, NT // 2) as i:
                for par in range(2):
                    j = 2 * i + par
                    pe.wait_ge(mc_ready, j + 1)
                    pe.wait_ge(zT_ready, j + 1)
                    for f in range(2):
                        ins = pe.transpose(ps_t[par][:, f * P:(f + 1) * P], mc[par][:, f * P:(f + 1) * P],
                                           st.ident[:, :])
                    ins.then_inc(turned, 1)
                for par in range(2):
                    j = 2 * i + par
                    pe.wait_ge(hs_ready, j + 1)
                    pe.wait_ge(zT_ready, j + 3)
                    pe.wait_ge(summed, j + 1)
                    for f in range(4):
                        ins = pe.matmul(ps_z[par][:, :], zT[par][:, f, :], wg[:, f, :], start=(f == 0), stop=(f == 3))
                    ins.then_inc(z_made, 1)

        @block.scalar
        def _(act):
            act.sem_inc(zT_ready, 2)
            with act.Fori(0, NT // 2) as i:
                for par in range(2):
                    j = 2 * i + par
                    act.wait_ge(turned, j + 3)
                    act.wait_ge(z_made, j + 1)
                    act.activation(zT[par][:, 2:4, :], ps_t[par][:, 0:2 * P].rearrange("p (f q) -> p f q", f=2),
                                   ACT.Copy).then_inc(zT_ready, 1)
                for par in range(2):
                    j = 2 * i + par
                    act.wait_ge(summed, j + 3)
                    act.activation(g[par][:, :], g[par][:, :], ACT.Sigmoid).then_inc(sig_done, 1)
            act.wait_ge(root_asked, 1)
            act.activation(rows[:, 1, :], rows[:, 1, :], ACT.Sqrt).then_inc(root_taken, 1)

        @block.vector
        def _(dve):
            dve.sem_inc(summed, 2)
            dve.sem_inc(fused, 2)
            dve.wait_ge(loaded, 48)
            with dve.Fori(0, NT // 2) as i:
                for par in range(2):
                    dve.wait_ge(fused, 2 * i + par + 1)
                    dve.wait_ge(z_made, 2 * i + par + 3)
                    dve.tensor_tensor(g[par][:, :], ps_z[par][:, :], bias[:, :], ALU.add).then_inc(summed, 1)
                for par in range(2):
                    j = 2 * i + par
                    dve.wait_ge(sig_done, j + 1)
                    dve.tensor_tensor(g[par][:, :], g[par][:, :], st.MC[:, bass.ds(j, 1), :].squeeze(1),
                                      ALU.mult).then_inc(scaled, 1)
                    dve.wait_ge(scaled, j + 1)
                    dve.tensor_tensor(st.X[:, bass.ds(j, 1), :].squeeze(1), g[par][:, :],
                                      st.X[:, bass.ds(j, 1), :].squeeze(1), ALU.add).then_inc(fused, 1)
            dve.wait_ge(fused, NT + 2)
            chain = Chain(dve, chain_sem)
            row_statistics(dve, chain, st.X, stats, rows, 1e-6, True, root_asked, root_taken)
            with dve.Fori(0, NT) as j:
                x = st.X[:, bass.ds(j, 1), :].squeeze(1)
                dve.scalar_tensor_tensor(out=x, in0=x, scalar=rows[:, 1, bass.ds(j, 1)], in1=norm_w[:, :],
                                         op0=ALU.mult, op1=ALU.mult)


class State:
    pass


def expert_layer(nc, st, io, stages):
    with ExitStack() as ctx:
        def sb(name, shape):
            return ctx.enter_context(nc.sbuf_tensor(name, shape, F32))

        st.vm = sb("vm", [P, B, Q])
        st.rope = sb("rope", [P, 2, 24])
        st.head_rows = sb("head_rows", [P, 8])
        for stage, args in stages:
            stage(nc, st, io, *args)


def memory_layer(nc, st, io, stages):
    with nc.sbuf_tensor("MC", [P, NT, D], F32) as st.MC:
        for stage, args in stages:
            stage(nc, st, io, *args)


def build(nc, io, stages):
    with ExitStack() as ctx:
        def sb(name, shape):
            return ctx.enter_context(nc.sbuf_tensor(name, shape, F32))

        st = State()
        st.ident = sb("ident", [P, P])
        st.X = sb("X", [P, NT, D])
        st.XT = sb("XT", [P, 2, B * Q])
        st.A = sb("A", [P, 2, 16 * C])
        st.Bw = sb("Bw", [P, 16 * D])
        st.Wv, st.Wo = st.Bw[:, 0:8 * P], st.Bw[:, 8 * P:8 * P + 8 * D]
        for stage, args in stages:
            stage(nc, st, io, *args)


def perceiver_stages(n):
    return [
        (norm_phase, (f"{n}_norm1", "ln", f"{n}_ln_q_g", f"{n}_ln_q_b", 1e-5)),
        (gated_weights_phase, (f"{n}_w", 16, 64, 64 ** -0.5, f"{n}_attn_gate")),
        (grouped_attention_phase, (f"{n}_attn", 16, 64)),
        (norm_phase, (f"{n}_norm2", "ln", f"{n}_ln_ff_g", f"{n}_ln_ff_b", 1e-5)),
        (mlp_phase, (f"{n}_mlp", f"{n}_ff_gate")),
    ]


EXPERT_STAGES = [
    (expert_masks_phase, ()),
    (norm_phase, ("L1_norm1", "rms", "L1_ln_in_w", None, 1e-6)),
    (self_attention_phase, ()),
    (norm_phase, ("L1_norm2", "rms", "L1_ln_post_cross_w", None, 1e-6)),
    (narrow_attention_phase, ("L1_cross", 16, 8)),
    (norm_phase, ("L1_norm3", "rms", "L1_ln_post_attn_w", None, 1e-6)),
    (expert_mlp_phase, ()),
]

MEMORY_STAGES = [
    (norm_phase, ("L2_turn", "plain")),
    (memory_weights_phase, ()),
    (attention_phase, ("L2_attn", 1, False, True)),
    (gate_phase, ()),
]

STAGES = ([(load_phase, ())] + perceiver_stages("L0") + [(expert_layer, (EXPERT_STAGES,))]
          + [(memory_layer, (MEMORY_STAGES,))] + perceiver_stages("L3") + [(store_phase, ())])


def layout(inputs):
    import numpy as np

    def heads_first(w, width):
        w = np.asarray(w)
        return w.reshape(w.shape[0], -1, width).transpose(2, 1, 0)

    def row_heads(w, width):
        w = np.asarray(w)
        return w.reshape(-1, width, w.shape[1]).transpose(1, 0, 2)

    def tiled(w):
        w = np.asarray(w)
        return w.reshape(-1, P, w.shape[1]).transpose(1, 0, 2)

    def halves(v):
        return np.asarray(v).reshape(2, P).T

    ctx = np.asarray(inputs["ctx_1024"])
    padded = np.zeros((B, SP, C), ctx.dtype)
    padded[:, :S] = ctx
    mask = np.zeros((B, 4 * MASK_WORDS), np.bool_)
    mask[:, :S] = np.asarray(inputs["mask_BxS2_bk0"])
    a = {
        "ident": np.eye(P, dtype=np.float32),
        "x": np.asarray(inputs["x"]).reshape(B * Q, D),
        "ctxT": padded[:, :S_EVEN].transpose(0, 2, 1),
        "ctx": padded.reshape(B, KT, P, C).transpose(0, 2, 1, 3),
        "mask": mask.view(np.int32),
    }
    for n in ("L0", "L3"):
        def w(k):
            return np.asarray(inputs[f"{n}_xattn_{k}"])
        for k in ("ln_q_g", "ln_q_b", "ln_ff_g", "ln_ff_b"):
            a[f"{n}_{k}"] = halves(w(k))
        kv = w("Wkv")
        a[f"{n}_w_wq"] = heads_first(w("Wq"), 64)
        a[f"{n}_w_wk"] = heads_first(kv[:, :1024], 64)
        a[f"{n}_w_wv"] = kv[:, 1024:]
        a[f"{n}_w_wo"] = tiled(w("Wo"))
        a[f"{n}_attn_gate"] = w("attn_gate").reshape(1, 1)
        a[f"{n}_ff_gate"] = w("ff_gate").reshape(1, 1)
        a[f"{n}_mlp_w1"] = tiled(w("W1"))
        a[f"{n}_mlp_w2"] = tiled(w("W2"))
    def w(k):
        return np.asarray(inputs[f"L1_xattn_{k}"])
    for k in ("ln_in_w", "ln_post_attn_w", "ln_post_cross_w"):
        a[f"L1_{k}"] = halves(w(k))
    for e in "vl":
        a[f"L1_{e}_qkv"] = tiled(w(f"{e}_qkv"))
        a[f"L1_{e}_dense"] = tiled(w(f"{e}_dense"))
        a[f"L1_{e}_gate"] = tiled(w(f"{e}_gate"))
        a[f"L1_{e}_up"] = tiled(w(f"{e}_up"))
        down = np.zeros((768, D), np.float32)
        down[:688] = w(f"{e}_down")
        a[f"L1_{e}_down"] = tiled(down)
    ckv = w("ckv_w")
    a["L1_cross_wq"] = np.tile(w("cq_w").reshape(2, P, 4, 1, 32), (1, 1, 1, 4, 1)).reshape(2, P, 4, P).transpose(1, 0, 2, 3)
    a["L1_cross_wk"] = np.tile(ckv[:, :C].reshape(P, 4, 1, 32), (1, 1, 4, 1)).reshape(P, 4, P)
    a["L1_cross_wv"] = np.pad(ckv[:, C:].reshape(P, 4, 4, 8), ((0, 0), (0, 0), (0, 0), (0, 24))).reshape(P, 4, P)
    a["L1_cross_wo"] = np.pad(w("cdense_w").reshape(4, 4, 8, D), ((0, 0), (0, 0), (0, 24), (0, 0))).reshape(4, P, D).transpose(1, 0, 2)
    a["L2_mem"] = tiled(inputs["L2_xattn_W_mem"])
    a["L2_memT"] = np.asarray(inputs["L2_xattn_W_mem"]).T
    a["L2_gateT"] = tiled(np.asarray(inputs["L2_xattn_W_gate"]).T)
    a["L2_gate_b"] = np.asarray(inputs["L2_xattn_b_gate"]).reshape(1, D)
    a["L2_norm_w"] = np.asarray(inputs["L2_xattn_norm_w"]).reshape(1, D)
    a["types"] = np.asarray(inputs["mask_BxS_ik0"])
    a["positions"] = np.asarray(inputs["pos_1xS"])
    freqs = np.outer(np.arange(Q, dtype=np.float32),
                     (1.0 / 10000.0 ** (np.arange(0, 16, 2, dtype=np.float32) / np.float32(16))).astype(np.float32))
    cos, sin = np.cos(freqs).astype(np.float32), np.sin(freqs).astype(np.float32)
    a["rope_table"] = tiled(np.concatenate([cos, -sin, sin], axis=1))
    a["row_numbers"] = np.arange(Q, dtype=np.float32).reshape(2, P).T
    a["head_rows"] = np.kron(np.eye(8, dtype=np.float32), np.full((16, 1), 0.25, np.float32))
    copy, head = np.arange(P) // 32, np.arange(P) // 8 % 4
    a["copy_picks"] = np.stack([copy % 2 == 1, copy >= 2] + [head == i for i in range(4)], axis=1).astype(np.float32)
    a["causal"] = np.concatenate([np.zeros((P, P), np.float32),
                                  np.triu(np.full((P, P), -NEG, np.float32), 1)], axis=1)
    return a


def kernel(**inputs):
    import numpy as np
    import concourse.bacc as bacc
    from concourse.bass_utils import run_bass_kernel_spmd

    nc = bacc.Bacc("TRN2", target_bir_lowering=False, num_devices=1)
    arrays = {k: np.ascontiguousarray(v) for k, v in layout(inputs).items()}
    io = {k: nc.dram_tensor(f"in_{k}", v.shape, mybir.dt.from_np(v.dtype), kind="ExternalInput").ap()
          for k, v in arrays.items()}
    io["out"] = nc.dram_tensor("out", (B * Q, D), F32, kind="ExternalOutput").ap()
    build(nc, io, STAGES)
    r = run_bass_kernel_spmd(nc, [{f"in_{k}": v for k, v in arrays.items()}], core_ids=[0])
    return r.results[0]["out"].reshape(B, Q, D)
```

```python
from contextlib import ExitStack

import concourse.bass as bass
from concourse import mybir

ALU = mybir.AluOpType
ACT = mybir.ActivationFunctionType
AX_X = mybir.AxisListType.X
F32 = mybir.dt.float32
I32 = mybir.dt.int32
U8 = mybir.dt.uint8
F32R = mybir.dt.float32r

P = 128
B = 8
Q = 256
D = 256
C = 128
S = 1601
NT = B * Q // P
KT = (S + P - 1) // P
SP = KT * P
BANK = 512
MASK_WORDS = (S + 3) // 4
NEG = 1e30
BIG = 3e38
EXPERT_F = 688
CHUNK = (S + 7) // 8 * 2
S_EVEN = 4 * CHUNK

SCORE_CHUNKS = [(c, min(BANK, S - c)) for c in range(0, S, BANK)]
EVEN_CHUNKS = [(c, CHUNK) for c in range(0, S_EVEN, CHUNK)]
TURN_GROUPS = [range(k, min(k + 4, KT)) for k in range(0, KT, 4)]


def by_bank(ps):
    return ps[:, :].rearrange("p (c k) -> p c k", k=BANK)[:, :, 0:CHUNK]


def by_chunk(sb):
    return sb[:, :].rearrange("p (c k) -> p c k", k=CHUNK)


class Phase:

    def __init__(self, nc, name):
        self.nc, self.name, self.ctx, self.sems = nc, name, ExitStack(), []

    def __enter__(self):
        self.ctx.__enter__()
        return self

    def __exit__(self, *error):
        self.ctx.__exit__(*error)
        self.nc.clear_and_free_semaphores(self.sems)
        self.nc.all_engine_barrier()

    def sb(self, name, shape, dt=F32):
        return self.ctx.enter_context(self.nc.sbuf_tensor(f"{self.name}_{name}", shape, dt))

    def ps(self, name, shape, dt=F32):
        return self.ctx.enter_context(self.nc.psum_tensor(f"{self.name}_{name}", shape, dt))

    def sem(self, name):
        self.sems.append(self.nc.alloc_semaphore(f"{self.name}_{name}"))
        return self.sems[-1]

    def block(self):
        return self.ctx.enter_context(self.nc.Block())


def load_phase(nc, st, io):
    with Phase(nc, "load") as ph:
        loaded = ph.sem("loaded")
        block = ph.block()

        @block.sync
        def _(sp):
            sp.dma_start(st.ident[:, :], io["ident"]).then_inc(loaded, 16)
            sp.dma_start(st.X[:, :, :], io["x"].rearrange("(j p) d -> p j d", p=P)).then_inc(loaded, 16)
            sp.wait_ge(loaded, 32)


def store_phase(nc, st, io):
    with Phase(nc, "store") as ph:
        stored = ph.sem("stored")
        block = ph.block()

        @block.sync
        def _(sp):
            sp.dma_start(io["out"].rearrange("(j p) d -> p j d", p=P), st.X[:, :, :]).then_inc(stored, 16)
            sp.wait_ge(stored, 16)


def tile_statistics(dve, st, j):
    return dve.bn_stats(st.stats[:, bass.ds(j, 1), :].squeeze(1), st.X[:, bass.ds(j, 1), :].squeeze(1))


def row_statistics(dve, chain, stats, rows, eps, rms, root_asked, root_taken):
    even, odd = stats[:, :, 1], stats[:, :, 4]
    chain(dve.tensor_tensor(rows[:, 2, :], even, odd, ALU.add))
    chain(dve.tensor_tensor(rows[:, 3, :], even, odd, ALU.subtract))
    chain(dve.scalar_tensor_tensor(out=rows[:, 3, :], in0=rows[:, 3, :], scalar=0.25, in1=rows[:, 3, :],
                                   op0=ALU.mult, op1=ALU.mult))
    chain(dve.tensor_tensor(rows[:, 1, :], stats[:, :, 2], stats[:, :, 5], ALU.add))
    chain(dve.scalar_tensor_tensor(out=rows[:, 1, :], in0=rows[:, 1, :], scalar=1.0 / D, in1=rows[:, 3, :],
                                   op0=ALU.mult, op1=ALU.add))
    chain(dve.tensor_scalar(rows[:, 0, :], rows[:, 2, :], 0.5, None, ALU.mult))
    if rms:
        chain(dve.tensor_tensor(rows[:, 3, :], rows[:, 0, :], rows[:, 0, :], ALU.mult))
        chain(dve.tensor_tensor(rows[:, 1, :], rows[:, 1, :], rows[:, 3, :], ALU.add))
    dve.tensor_scalar(rows[:, 1, :], rows[:, 1, :], eps, None, ALU.add).then_inc(root_asked, 1)
    dve.wait_ge(root_taken, 1)
    chain(dve.reciprocal(rows[:, 1, :], rows[:, 1, :]))


class Chain:

    def __init__(self, eng, sem):
        self.eng, self.sem, self.count = eng, sem, 0

    def __call__(self, instruction):
        instruction.then_inc(self.sem, 1)
        self.count += 1
        self.wait()

    def add(self, n):
        self.count += n

    def wait(self):
        self.eng.wait_ge(self.sem, self.count)


class GatedWeights:

    def __init__(self, ph, st, io, name, heads, width, scale, gate):
        self.st, self.io, self.name, self.scale, self.gate = st, io, name, scale, gate
        self.wq = ph.sb("wq", [width, heads, D])
        self.wk = ph.sb("wk", [width, heads, C])
        self.g = ph.sb("g", [P, 2])
        self.prod = [ph.ps(f"prod{i}", [P, BANK]) for i in range(4)]
        self.loaded = ph.sem("wq_wk_loaded")
        self.wo_loaded = ph.sem("wo_loaded")
        self.gate_ready = ph.sem("gate_ready")
        self.made = ph.sem("products_made")
        self.copied = ph.sem("products_copied")
        self.groups = [(h, f) for h in range(0, heads, 4) for f in range(2)]

    def load(self, sp):
        st, io, name = self.st, self.io, self.name
        sp.dma_start(self.wq[:, :, :], io[f"{name}_wq"]).then_inc(self.loaded, 16)
        sp.dma_start(self.wk[:, :, :], io[f"{name}_wk"]).then_inc(self.loaded, 16)
        sp.dma_start(self.g[:, 0:1], io[self.gate].to_broadcast([P, 1])).then_inc(self.wo_loaded, 16)
        sp.dma_start(st.Wo[:, :], io[f"{name}_wo"].rearrange("p t d -> p (t d)")).then_inc(self.wo_loaded, 16)
        sp.dma_start(st.Wv[:, :], io[f"{name}_wv"]).then_inc(self.wo_loaded, 16)
        sp.wait_ge(self.wo_loaded, 48)

    def tensor(self, pe):
        pe.wait_ge(self.loaded, 32)
        for n, (h0, f) in enumerate(self.groups):
            if n >= 4:
                pe.wait_ge(self.copied, n - 3)
            for i in range(4):
                ins = pe.matmul(self.prod[n % 4][:, i * C:(i + 1) * C], self.wq[:, h0 + i, f * P:(f + 1) * P],
                                self.wk[:, h0 + i, :], start=True, stop=True)
            ins.then_inc(self.made, 1)

    def scalar(self, act):
        for n, (h, f) in enumerate(self.groups):
            act.wait_ge(self.made, n + 1)
            act.activation(self.st.A[:, f, h * C:(h + 4) * C], self.prod[n % 4][:, :], ACT.Copy,
                           scale=self.scale).then_inc(self.copied, 1)
        act.wait_ge(self.wo_loaded, 48)
        act.activation(self.g[:, 1:2], self.g[:, 0:1], ACT.Tanh).then_inc(self.gate_ready, 1)

    def gpsimd(self, pool):
        pass

    def vector(self, dve):
        dve.wait_ge(self.gate_ready, 1)
        dve.tensor_scalar(self.st.Wo[:, :], self.st.Wo[:, :], self.g[:, 1:2], None, ALU.mult)


class SplitWeights:

    def __init__(self, ph, st, io, make_pieces):
        self.io, self.pieces = io, make_pieces(ph, st)
        self.loaded = [ph.sem(f"piece{i}_loaded") for i in range(len(self.pieces))]
        self.hi_ready = ph.sem("hi_ready")

    def load(self, sp):
        for loaded, (inputs, staging, hi, lo) in zip(self.loaded, self.pieces):
            at = 0
            for name in inputs:
                source = self.io[name]
                source = source.rearrange("p a c -> p (a c)")
                sp.dma_start(staging[:, at:at + source.shape[1]], source).then_inc(loaded, 16)
                at += source.shape[1]

    def tensor(self, pe):
        pass

    def scalar(self, act):
        for loaded, (inputs, staging, hi, lo) in zip(self.loaded, self.pieces):
            act.wait_ge(loaded, 16 * len(inputs))
            act.activation(hi, staging, ACT.Copy).then_inc(self.hi_ready, 1)

    def gpsimd(self, pool):
        for i, (inputs, staging, hi, lo) in enumerate(self.pieces):
            pool.wait_ge(self.hi_ready, i + 1)
            pool.tensor_tensor(lo, staging, hi.bitcast(F32), ALU.subtract)

    def vector(self, dve):
        pass


def norm_phase(nc, st, io, name, kind, gain=None, shift=None, eps=0.0, beside=None, fresh=False):
    with Phase(nc, name) as ph:
        xn = [ph.sb(f"xn{i}", [P, D]) for i in range(2)]
        rows = ph.sb("rows", [P, 4, NT])
        gs = ph.sb("gs", [P, 2, 2])
        turned = [ph.ps(f"turned{i}", [P, BANK]) for i in range(2)]
        gain_loaded = ph.sem("gain_loaded")
        chain_sem = ph.sem("chain")
        root_asked = ph.sem("root_asked")
        root_taken = ph.sem("root_taken")
        xn_ready = ph.sem("xn_ready")
        turn_done = ph.sem("turn_done")
        copied = ph.sem("copied")
        if beside:
            beside = beside[0](ph, st, io, *beside[1:])
        block = ph.block()

        @block.sync
        def _(sp):
            if gain:
                sp.dma_start(gs[:, 0, :], io[gain]).then_inc(gain_loaded, 16)
            if shift:
                sp.dma_start(gs[:, 1, :], io[shift]).then_inc(gain_loaded, 16)
            if beside:
                beside.load(sp)

        @block.gpsimd
        def _(pool):
            if beside:
                beside.gpsimd(pool)

        @block.vector
        def _(dve):
            chain = Chain(dve, chain_sem)
            if fresh:
                with dve.Fori(0, NT) as j:
                    tile_statistics(dve, st, j).then_inc(chain_sem, 1)
                chain.add(NT)
                chain.wait()
            if kind != "plain":
                row_statistics(dve, chain, st.stats, rows, eps, kind == "rms", root_asked, root_taken)
            with dve.Fori(0, NT // 2) as i:
                for par in range(2):
                    j = 2 * i + par
                    dve.wait_ge(turn_done, j + 1)
                    if kind == "ln":
                        ins = dve.tensor_scalar(xn[par][:, :], st.X[:, j, :], rows[:, 0, bass.ds(j, 1)],
                                                rows[:, 1, bass.ds(j, 1)], ALU.subtract, ALU.mult)
                    elif kind == "rms":
                        ins = dve.tensor_scalar(xn[par][:, :], st.X[:, j, :], rows[:, 1, bass.ds(j, 1)], None,
                                                ALU.mult)
                    else:
                        ins = dve.tensor_copy(xn[par][:, :], st.X[:, j, :])
                    ins.then_inc(xn_ready, 1)
            if beside:
                beside.vector(dve)

        @block.tensor
        def _(pe):
            pe.sem_inc(turn_done, 2)
            if beside:
                beside.tensor(pe)
            with pe.Fori(0, NT // 2) as i:
                for par in range(2):
                    pe.wait_ge(xn_ready, 2 * i + par + 1)
                    pe.wait_ge(copied, 2 * i + par + 1)
                    for f in range(2):
                        ins = pe.transpose(turned[par][:, f * P:(f + 1) * P], xn[par][:, f * P:(f + 1) * P],
                                           st.ident[:, :])
                    ins.then_inc(turn_done, 1)

        @block.scalar
        def _(act):
            act.sem_inc(copied, 2)
            if beside and fresh:
                beside.scalar(act)
            if kind != "plain":
                act.wait_ge(root_asked, 1)
                act.activation(rows[:, 1, :], rows[:, 1, :], ACT.Sqrt).then_inc(root_taken, 1)
            if beside and not fresh:
                beside.scalar(act)
            if gain:
                act.wait_ge(gain_loaded, 32 if shift else 16)
            with act.Fori(0, NT // 2) as i:
                for par in range(2):
                    j = 2 * i + par
                    act.wait_ge(turn_done, j + 3)
                    for f in range(2):
                        to = st.XT[:, f, bass.ts(j, P)]
                        src = turned[par][:, f * P:(f + 1) * P]
                        if kind == "ln":
                            ins = act.activation(to, src, ACT.Identity, scale=gs[:, 0, f:f + 1],
                                                 bias=gs[:, 1, f:f + 1])
                        elif kind == "rms":
                            ins = act.activation(to, src, ACT.Copy, scale=gs[:, 0, f:f + 1])
                        else:
                            ins = act.activation(to, src, ACT.Copy)
                    ins.then_inc(copied, 1)


def memory_attention_phase(nc, st, io):
    with Phase(nc, "memory") as ph:
        ctxT = [ph.sb(f"ctxT{i}", [P, S_EVEN]) for i in range(2)]
        ctx = [ph.sb(f"ctx{i}", [P, KT, C]) for i in range(2)]
        zeros = ph.sb("zeros", [P, S])
        g_sb = [ph.sb(f"g_sb{i}", [P, Q]) for i in range(2)]
        probs = [ph.sb(f"probs{i}", [P, S]) for i in range(2)]
        negmax = ph.sb("negmax", [P, 2])
        rowsum = ph.sb("rowsum", [P, 2, 2])
        inv = ph.sb("inv", [P, 2])
        pT = [ph.sb(f"pT{i}", [P, KT, Q]) for i in range(2)]
        u_sb = ph.sb("u_sb", [P, Q])
        ps_s = ph.ps("ps_s", [P, 4 * BANK])
        ps_t = [ph.ps(f"ps_t{i}", [P, BANK]) for i in range(2)]
        ps_gu = ph.ps("ps_gu", [P, BANK])
        ps_g, ps_u = ps_gu[:, 0:Q], ps_gu[:, Q:2 * Q]
        ps_o = ph.ps("ps_o", [P, 2, D])

        ctx_loaded = [ph.sem(f"ctx_loaded{i}") for i in range(2)]
        zeros_ready = ph.sem("zeros_ready")
        g_made = ph.sem("g_made")
        g_copied = ph.sem("g_copied")
        scored = ph.sem("scored")
        maxed = ph.sem("maxed")
        exped = ph.sem("exped")
        turned = ph.sem("turned")
        turn_act = ph.sem("turn_act")
        turn_dve = ph.sem("turn_dve")
        pv_done = ph.sem("pv_done")
        u_copied = ph.sem("u_copied")
        out_made = ph.sem("out_made")
        inverted = ph.sem("inverted")
        summed = ph.sem("summed")
        dve_passed = ph.sem("dve_passed")
        sp_passed = ph.sem("sp_passed")
        block = ph.block()

        NG = len(TURN_GROUPS)

        def drive(eng, first, step, last):
            first()
            with eng.Fori(0, (B - 2) // 2) as k:
                step(2 * k + 1, 1, k, False)
                step(2 * k + 2, 0, k + 1, False)
            step(B - 1, 1, (B - 2) // 2, True)
            last()

        @block.sync
        def _(sp):
            def load(b, par):
                sp.dma_start(ctxT[par][:, :], io["ctxT"][bass.ds(b, 1), :, :].rearrange("a c s -> (a c) s")).then_inc(ctx_loaded[par], 16)
                sp.dma_start(ctx[par][:, :, :], io["ctx"][bass.ds(b, 1), :, :, :].rearrange("a p k c -> (a p) k c")).then_inc(ctx_loaded[par], 16)

            load(0, 0)
            load(1, 1)
            with sp.Fori(0, (B - 2) // 2) as k:
                for par in range(2):
                    sp.wait_ge(pv_done, 2 * k + par + 1)
                    sp.sem_inc(sp_passed, 1)
                    load(2 * k + 2 + par, par)

        @block.gpsimd
        def _(pool):
            pool.memset(zeros[:, :], 0.0).then_inc(zeros_ready, 1)

        @block.tensor
        def _(pe):
            pe.sem_inc(turned, 2 * NG)

            def scores(b, par, qt):
                pe.wait_ge(g_copied, b + 2)
                pe.wait_ge(maxed, 2 * b + qt + 1)
                for c, w in SCORE_CHUNKS:
                    ins = pe.matmul(ps_s[:, c:c + w], g_sb[par][:, qt * P:(qt + 1) * P], ctxT[par][:, c:c + w],
                                    start=True, stop=True)
                ins.then_inc(scored, 1)

            def make_g(b):
                pe.wait_ge(g_copied, b + 1)
                for f in range(2):
                    ins = pe.matmul(ps_g, st.A[:, f, 0:C], st.XT[:, f, bass.ts(b, Q)], start=(f == 0), stop=(f == 1))
                ins.then_inc(g_made, 1)

            def turn(b, qt, groups):
                pe.wait_ge(exped, 2 * b + qt + 1)
                for g in groups:
                    pe.wait_ge(turn_dve if g % 2 else turn_act, 4 * b + 2 * qt + g // 2 + 1)
                    for k in TURN_GROUPS[g]:
                        w = min(P, S - k * P)
                        ins = pe.transpose(ps_t[g % 2][0:w, (k % 4) * P:(k % 4 + 1) * P],
                                           probs[qt][:, k * P:k * P + w], st.ident[:, :])
                    ins.then_inc(turned, 1)

            def pv(b, par):
                pe.wait_ge(turn_act, 4 * b + 5)
                pe.wait_ge(turn_dve, 4 * b + 5)
                for k in range(KT):
                    w = min(P, S - k * P)
                    ins = pe.matmul(ps_u, ctx[par][0:w, k, :], pT[par][0:w, k, :], start=(k == 0), stop=(k == KT - 1))
                ins.then_inc(pv_done, 1)

            def output(b):
                pe.wait_ge(u_copied, b + 1)
                pe.wait_ge(summed, b + 1)
                for qt in range(2):
                    ins = pe.matmul(ps_o[:, qt, :], u_sb[:, qt * P:(qt + 1) * P], st.Bw[:, 0:D], start=True, stop=True)
                ins.then_inc(out_made, 1)

            def first():
                make_g(0)
                pe.wait_ge(ctx_loaded[0], 32)
                scores(0, 0, 0)
                make_g(1)
                scores(0, 0, 1)
                turn(0, 0, range(NG))

            def step(b, par, half, at_end):
                pe.wait_ge(ctx_loaded[par], 32 * (half + 1))
                scores(b, par, 0)
                turn(b - 1, 1, (0, 1))
                if not at_end:
                    make_g(b + 1)
                turn(b - 1, 1, (2, 3))
                if not at_end:
                    pe.wait_ge(g_copied, b + 3)
                pv(b - 1, 1 - par)
                scores(b, par, 1)
                output(b - 1)
                turn(b, 0, range(NG))

            def last():
                turn(B - 1, 1, range(NG))
                pv(B - 1, 1)
                output(B - 1)

            drive(pe, first, step, last)

        @block.vector
        def _(dve):
            dve.sem_inc(maxed, 1)
            dve.sem_inc(turn_dve, 1)
            dve.sem_inc(summed, 1)

            def rowmax(b, qt):
                dve.wait_ge(scored, 2 * b + qt + 1)
                dve.wait_ge(turned, NG * (2 * b + qt + 1))
                dve.sem_inc(dve_passed, 1)
                dve.tensor_tensor_reduce(out=probs[qt][:, :], in0=ps_s[:, 0:S], in1=zeros[:, :], scale=-1.0, scalar=BIG,
                                         op0=ALU.add, op1=ALU.min, accum_out=negmax[:, qt:qt + 1]).then_inc(maxed, 1)

            def copy_turned(b, qt, par):
                for g in (1, 3):
                    tiles = TURN_GROUPS[g]
                    w = min(P, S - tiles[0] * P)
                    dve.wait_ge(turned, NG * (2 * b + qt + 2) + g + 1)
                    dve.tensor_copy(pT[par][0:w, tiles[0]:tiles[-1] + 1, qt * P:(qt + 1) * P],
                                    ps_t[1][0:w, 0:P * len(tiles)].rearrange("p (k q) -> p k q", q=P)).then_inc(turn_dve, 1)

            def finish(b, par):
                dve.wait_ge(exped, 2 * b + 2)
                dve.wait_ge(summed, b + 1)
                dve.reciprocal(inv[:, :], rowsum[:, par, :]).then_inc(inverted, 1)
                dve.wait_ge(inverted, b + 1)
                dve.wait_ge(out_made, b + 1)
                for qt in range(2):
                    ins = dve.tensor_scalar(st.MC[:, bass.ds(2 * b + qt, 1), :].squeeze(1), ps_o[:, qt, :], inv[:, qt:qt + 1], None, ALU.mult)
                ins.then_inc(summed, 1)

            def first():
                dve.wait_ge(zeros_ready, 1)
                rowmax(0, 0)
                rowmax(0, 1)
                copy_turned(0, 0, 0)

            def step(b, par, half, at_end):
                rowmax(b, 0)
                copy_turned(b - 1, 1, 1 - par)
                rowmax(b, 1)
                finish(b - 1, 1 - par)
                copy_turned(b, 0, par)

            def last():
                copy_turned(B - 1, 1, 1)
                finish(B - 1, 1)

            drive(dve, first, step, last)

        @block.scalar
        def _(act):
            act.sem_inc(g_copied, 1)
            act.sem_inc(turn_act, 1)

            def copy_g(b, par):
                act.wait_ge(g_made, b + 1)
                act.activation(g_sb[par][:, :], ps_g, ACT.Copy).then_inc(g_copied, 1)

            def exponential(b, par, qt):
                act.wait_ge(maxed, 2 * b + qt + 2)
                act.activation(probs[qt][:, :], probs[qt][:, :], ACT.Exp, scale=-1.0, bias=negmax[:, qt:qt + 1],
                               accum_out=rowsum[:, par, qt:qt + 1]).then_inc(exped, 1)

            def copy_turned(b, qt, par):
                for g in (0, 2):
                    tiles = TURN_GROUPS[g]
                    act.wait_ge(turned, NG * (2 * b + qt + 2) + g + 1)
                    act.activation(pT[par][:, tiles[0]:tiles[-1] + 1, qt * P:(qt + 1) * P],
                                   ps_t[0][:, :].rearrange("p (k q) -> p k q", q=P), ACT.Copy).then_inc(turn_act, 1)

            def copy_u(b):
                act.wait_ge(pv_done, b + 1)
                act.activation(u_sb[:, :], ps_u, ACT.Copy).then_inc(u_copied, 1)

            def first():
                copy_g(0, 0)
                copy_g(1, 1)
                exponential(0, 0, 0)
                copy_turned(0, 0, 0)
                exponential(0, 0, 1)

            def step(b, par, half, at_end):
                copy_turned(b - 1, 1, 1 - par)
                if not at_end:
                    copy_g(b + 1, 1 - par)
                exponential(b, par, 0)
                copy_u(b - 1)
                copy_turned(b, 0, par)
                exponential(b, par, 1)

            def last():
                copy_turned(B - 1, 1, 1)
                copy_u(B - 1)

            drive(act, first, step, last)


class TurnFills:

    def __init__(self, orders, stream):
        self.orders, self.stream = orders, stream

    def bank(self, fill):
        return self.stream(fill) % 2

    def _counted(self, streams, kind):
        return [f for bank in (0, 1) for f in self.orders[kind][bank] if self.stream(f) in streams]

    def skipped(self, streams):
        return len(self._counted(streams, "middle")) - len(self._counted(streams, "first"))

    def count(self, streams, rnd, fill, kind):
        per_round = len(self._counted(streams, "middle"))
        number = self._counted(streams, kind).index(fill) + 1
        if kind == "first":
            return self.skipped(streams) + number
        if kind == "over":
            return per_round * rnd - (per_round - len(self._counted(streams, "last"))) + number
        return per_round * rnd + number

    def wait_filled(self, eng, turned, rnd, fill, kind):
        eng.wait_ge(turned[self.bank(fill)], self.count((0, 2) if self.bank(fill) == 0 else (1, 3), rnd, fill, kind))

    def wait_taken(self, eng, taken, rnd, fill, kind):
        eng.wait_ge(taken[self.stream(fill)], self.count((self.stream(fill),), rnd, fill, kind))

    def wait_free(self, eng, taken, rnd, fill, kind):
        order = self.orders[kind][self.bank(fill)]
        if fill != order[0]:
            self.wait_taken(eng, taken, rnd, order[order.index(fill) - 1], kind)
        elif kind != "first":
            self.wait_taken(eng, taken, rnd - 1, self.orders["middle"][self.bank(fill)][-1],
                            "last" if kind == "over" else "middle")


def grouped_attention_phase(nc, st, io, name, heads, width):
    HG = P // width
    NJ = heads // HG
    J_ALL = B * NJ
    TILES = 2 * HG
    V_PARTS = (KT + 1) // 2
    assert HG == 2 and NJ == 8 and len(TURN_GROUPS) == 4 and V_PARTS == 7
    PV_TILES = [range(0, 4), range(4, 7), range(7, 10), range(10, KT)]

    def round_fills(first=False, over=False):
        def tile_fills(keys, r):
            return [(k, r) for k in keys if not (first and r < (2 if k == 3 else 1)) and not (over and r >= (2 if k == 3 else 1))]
        banks = {0: [], 1: []}
        for r in range(2 * TILES):
            v = [("V", r)] if r < V_PARTS and not over else []
            banks[0] += (v if r % 2 == 0 else []) + tile_fills((0, 2), r)
            banks[1] += tile_fills((3,), r) + (v if r % 2 else []) + tile_fills((1,), r)
        return banks

    fills = TurnFills({"first": round_fills(first=True), "middle": round_fills(), "last": round_fills(),
                       "over": round_fills(over=True)}, lambda fill: fill[1] % 2 if fill[0] == "V" else (0, 1, 0, 3)[fill[0]])

    with Phase(nc, name) as ph:
        ctx_in = ph.sb("ctx_in", [P, S_EVEN])
        ctx_hi = ph.sb("ctx_hi", [P, S_EVEN], F32R)
        ctx_lo = ph.sb("ctx_lo", [P, S_EVEN], F32R)
        mask_in = ph.sb("mask_in", [P, MASK_WORDS], I32)
        mask_bytes = mask_in[:, :].bitcast(U8)[:, 0:S]
        bias = ph.sb("bias", [P, S_EVEN])
        x_hi = ph.sb("x_hi", [P, 2, Q], F32R)
        x_lo = ph.sb("x_lo", [P, 2, Q], F32R)
        a_hi = [ph.sb(f"a_hi{i}", [P, 2, C], F32R) for i in range(HG)]
        a_lo = [ph.sb(f"a_lo{i}", [P, 2, C], F32R) for i in range(HG)]
        wv_hi = ph.sb("wv_hi", [P, 2 * P], F32R)
        wv_lo = ph.sb("wv_lo", [P, 2 * P], F32R)
        g_hi = [ph.sb(f"g_hi{i}", [P, Q], F32R) for i in range(HG)]
        g_lo = [ph.sb(f"g_lo{i}", [P, Q], F32R) for i in range(HG)]
        probs = [ph.sb(f"probs{i}", [P, S_EVEN]) for i in range(2)]
        negmax = ph.sb("negmax", [P, 2])
        rowsum = ph.sb("rowsum", [P, 2, HG, 2])
        inv = ph.sb("inv", [P, HG, 2])
        pT = [[ph.sb(f"pT{i}{k}", [P, KT, Q]) for k in range(HG)] for i in range(2)]
        v_sb = [ph.sb(f"v_sb{i}", [P, KT, 2 * P]) for i in range(2)]
        inv_rows = ph.sb("inv_rows", [P, Q])
        u_sb = ph.sb("u_sb", [P, Q])
        ps_s = ph.ps("ps_s", [P, 4 * BANK])
        ps_t = [ph.ps(f"ps_t{i}", [P, BANK]) for i in range(2)]
        ps_u = ph.ps("ps_u", [P, BANK])
        ps_m = ph.ps("ps_m", [P, BANK])

        ctx_loaded = ph.sem("ctx_loaded")
        mask_loaded = ph.sem("mask_loaded")
        halves = ph.sem("halves")
        x_ready = ph.sem("x_ready")
        ctx_hi_ready = ph.sem("ctx_hi_ready")
        ctx_ready = ph.sem("ctx_ready")
        bias_ready = ph.sem("bias_ready")
        a_ready = ph.sem("a_ready")
        wv_ready = ph.sem("wv_ready")
        g_made = ph.sem("g_made")
        g_hi_ready = ph.sem("g_hi_ready")
        g_ready = ph.sem("g_ready")
        scored = ph.sem("scored")
        maxed = ph.sem("maxed")
        exped = ph.sem("exped")
        turned = [ph.sem(f"turned{i}") for i in range(2)]
        taken = {0: ph.sem("act_taken0"), 1: ph.sem("dve_taken1"), 3: ph.sem("act_taken1")}
        inverted = ph.sem("inverted")
        inv_spread = ph.sem("inv_spread")
        inv_copied = ph.sem("inv_copied")
        pv_done = ph.sem("pv_done")
        u_ready = ph.sem("u_ready")
        out_made = ph.sem("out_made")
        x_added = ph.sem("x_added")
        dve_passed = ph.sem("dve_passed")
        pool_passed = ph.sem("pool_passed")
        block = ph.block()

        def drive(eng, batch):
            batch(0, True, False)
            with eng.Fori(1, B - 1) as b:
                batch(b, False, False)
            batch(B - 1, False, True)

        def in_round(b, j, first):
            return NJ // 2 * b + j // 2, "first" if first and j < 2 else "middle"

        @block.sync
        def _(sp):
            def load(b):
                sp.dma_start(ctx_in[:, :], io["ctxT"][bass.ds(b, 1), :, :].rearrange("a c s -> (a c) s")).then_inc(ctx_loaded, 16)

            def load_mask(b):
                sp.dma_start(mask_in[:, :], io["mask"][bass.ds(b, 1), :].to_broadcast([P, MASK_WORDS])).then_inc(mask_loaded, 16)

            load(0)
            load_mask(0)
            with sp.Fori(1, B) as b:
                sp.wait_ge(ctx_ready, b)
                load(b)
                sp.wait_ge(bias_ready, b)
                load_mask(b)

        @block.gpsimd
        def _(pool):
            SPLITS = 1 + heads + NJ // 2

            def batch(b, first, last):
                n0, done = heads * b, SPLITS * b

                def split(hi, lo, src, ready):
                    nonlocal done
                    done = done + 1
                    pool.sem_inc(pool_passed, 1)
                    pool.tensor_copy(hi, src).then_inc(halves, 1)
                    pool.wait_ge(halves, done)
                    pool.sem_inc(pool_passed, 1)
                    pool.tensor_tensor(lo, src, hi.bitcast(F32), ALU.subtract).then_inc(ready, 1)

                def a_slot(h):
                    if not (first and h < 2):
                        pool.wait_ge(g_made, n0 + h - 1)
                    split(a_hi[h % 2][:, :, :], a_lo[h % 2][:, :, :], st.A[:, :, h * C:(h + 1) * C], a_ready)

                if not first:
                    pool.wait_ge(g_made, n0)
                split(x_hi[:, :, :], x_lo[:, :, :], st.XT[:, :, bass.ts(b, Q)], x_ready)
                for j in range(NJ):
                    a_slot(2 * j)
                    a_slot(2 * j + 1)
                    if j % 2 == 0:
                        if not (first and j == 0):
                            rnd = NJ // 2 * b + j // 2 - 1
                            fills.wait_filled(pool, turned, rnd, ("V", V_PARTS - 1), "first" if first and j == 2 else "middle")
                        split(wv_hi[:, :], wv_lo[:, :], st.Wv[:, j * P:(j + 2) * P], wv_ready)
                    if j == 0:
                        pool.wait_ge(mask_loaded, 16 * b + 16)
                        if not first:
                            pool.wait_ge(maxed, TILES * NJ * b)
                        pool.sem_inc(pool_passed, 1)
                        pool.tensor_scalar(bias[:, 0:S], mask_bytes, NEG, -NEG, ALU.mult, ALU.add).then_inc(bias_ready, 1)

            pool.memset(bias[:, S:S_EVEN], -2 * NEG)
            drive(pool, batch)

        @block.tensor
        def _(pe):
            pe.sem_inc(turned[0], fills.skipped((0,)))
            pe.sem_inc(turned[1], fills.skipped((1, 3)))

            def scores(s):
                i, qt = s // 2, s % 2
                hi, lo = (g[i][:, qt * P:(qt + 1) * P] for g in (g_hi, g_lo))
                for g, c_part, start, stop in ((hi, ctx_hi, True, False), (hi, ctx_lo, False, False),
                                               (lo, ctx_hi, False, True)):
                    for bank, (c, w) in enumerate(EVEN_CHUNKS):
                        ins = pe.matmul(ps_s[:, bank * BANK:bank * BANK + w], g, c_part[:, c:c + w], start=start, stop=stop)
                ins.then_inc(scored, 1)

            def make_g(n, i):
                pe.wait_ge(a_ready, n + 1)
                steps = [(a[i], x, f) for a, x in ((a_hi, x_hi), (a_hi, x_lo), (a_lo, x_hi)) for f in range(2)]
                for k, (a, x, f) in enumerate(steps):
                    ins = pe.matmul(ps_m[:, 0:Q], a[:, f, :], x[:, f, :], start=(k == 0), stop=(k == len(steps) - 1))
                ins.then_inc(g_made, 1)

            def turn(rnd, g, r, kind):
                fills.wait_free(pe, taken, rnd, (g, r), kind)
                source = probs[(r - (2 if g == 3 else 1)) % 2]
                for k in TURN_GROUPS[g]:
                    w = min(P, S - k * P)
                    ins = pe.transpose(ps_t[g % 2][0:w, (k % 4) * P:(k % 4 + 1) * P],
                                       source[:, k * P:k * P + w], st.ident[:, :])
                ins.then_inc(turned[g % 2], 1)

            def make_v(rnd, part, kind):
                if part == 0:
                    pe.wait_ge(wv_ready, rnd + 1)
                fills.wait_free(pe, taken, rnd, ("V", part), kind)
                for k in range(2 * part, min(2 * part + 2, KT)):
                    w = min(P, S - k * P)
                    out = ps_t[part % 2][0:w, (k % 2) * 2 * P:(k % 2 + 1) * 2 * P]
                    c = slice(k * P, k * P + w)
                    pe.matmul(out, ctx_hi[:, c], wv_hi[:, :], start=True, stop=False)
                    pe.matmul(out, ctx_hi[:, c], wv_lo[:, :], start=False, stop=False)
                    ins = pe.matmul(out, ctx_lo[:, c], wv_hi[:, :], start=False, stop=True)
                ins.then_inc(turned[part % 2], 1)

            def pv(j, part):
                v = v_sb[j // 2 % 2]
                for k in PV_TILES[part]:
                    w = min(P, S - k * P)
                    for i in range(HG):
                        head = j % 2 * P + i * width
                        ins = pe.matmul(ps_u[i * width:(i + 1) * width, 0:Q], v[0:w, k, head:head + width],
                                        pT[j % 2][i][0:w, k, :], start=(k == 0), stop=(k == KT - 1))
                if part == len(PV_TILES) - 1:
                    ins.then_inc(pv_done, 1)

            def spread_inverse(J):
                pe.wait_ge(inverted, J + 1)
                for qt in range(2):
                    for i in range(HG):
                        ins = pe.matmul(ps_m[i * width:(i + 1) * width, Q + qt * P:Q + (qt + 1) * P],
                                        inv[:, i, qt:qt + 1].to_broadcast([P, width]), st.ident[:, :],
                                        start=True, stop=True)
                ins.then_inc(inv_spread, 1)

            def output(J, j):
                pe.wait_ge(u_ready, J + 1)
                for qt in range(2):
                    ins = pe.matmul(ps_m[:, qt * D:(qt + 1) * D], u_sb[:, qt * P:(qt + 1) * P],
                                    st.Wo[:, j * D:(j + 1) * D], start=True, stop=True)
                ins.then_inc(out_made, 1)

            def wait_turned(rnd, part, r, kind):
                key = (part, r) if part < 3 else (3, r + 1)
                fills.wait_taken(pe, taken, rnd, key, kind)

            def batch(b, first, last):
                for j in range(NJ):
                    J, n = NJ * b + j, HG * (NJ * b + j)
                    rnd, kind = in_round(b, j, first)
                    started = not (first and j == 0)
                    finishing = not (first and j < 2)
                    ending = last and j == NJ - 1
                    for s in range(TILES):
                        r = TILES * (j % 2) + s
                        if s % 2 == 0:
                            pe.wait_ge(g_ready, n + s // 2 + 1)
                        if j == 0 and s == 0:
                            pe.wait_ge(ctx_ready, b + 1)
                        if started or s > 0:
                            pe.wait_ge(maxed, TILES * J + s)
                        scores(s)
                        if r % 2 == 0 and r < V_PARTS:
                            make_v(rnd, r, kind)
                        if started or s >= 2:
                            turn(rnd, 3, r, kind)
                        if s == 0 and finishing:
                            wait_turned(rnd if j % 2 else rnd - 1, 3, TILES * ((j - 1) % 2),
                                        "first" if first and j == 2 else kind)
                            pv((j - 2) % NJ, 3)
                        if s > 0 and started:
                            if s == 1 and finishing:
                                pe.wait_ge(u_ready, J - 1)
                            wait_turned(rnd, s - 1, TILES * (j % 2), kind)
                            pv((j - 1) % NJ, s - 1)
                        if r % 2 == 1 and r < V_PARTS:
                            make_v(rnd, r, kind)
                        if started or s > 0:
                            pe.wait_ge(exped, TILES * J + s)
                            turn(rnd, 0, r, kind)
                        if s == 0:
                            if finishing:
                                pe.wait_ge(inv_copied, J - 1)
                            make_g(n + 1, 1)
                        if s == 1 and finishing:
                            pe.wait_ge(g_ready, n + 2)
                            output(J - 2, (j - 2) % NJ)
                        if s == 2 and not ending:
                            if finishing:
                                pe.wait_ge(x_added, J - 1)
                            make_g(n + 2, 0)
                        if s == 3 and started:
                            if ending:
                                pe.wait_ge(x_added, J - 1)
                            else:
                                pe.wait_ge(g_ready, n + 3)
                            spread_inverse(J - 1)
                        if started or s > 0:
                            turn(rnd, 1, r, kind)
                            turn(rnd, 2, r, kind)

            make_g(0, 0)
            drive(pe, batch)

            J, rnd = J_ALL, J_ALL // 2
            turn(rnd, 3, 0, "over")
            wait_turned(rnd - 1, 3, TILES, "last")
            pv(NJ - 2, 3)
            pe.wait_ge(exped, TILES * J)
            for g in (0, 1, 2):
                turn(rnd, g, 0, "over")
            turn(rnd, 3, 1, "over")
            pe.wait_ge(inv_copied, J - 1)
            output(J - 2, NJ - 2)
            for part in range(len(PV_TILES)):
                wait_turned(rnd, part, 0, "over")
                pv(NJ - 1, part)
            pe.wait_ge(x_added, J - 1)
            spread_inverse(J - 1)
            pe.wait_ge(inv_copied, J)
            output(J - 1, NJ - 1)

        @block.vector
        def _(dve):
            dve.sem_inc(taken[1], fills.skipped((1,)))

            def rowmax(tile, qt):
                dve.wait_ge(scored, tile + 1)
                dve.sem_inc(dve_passed, 1)
                dve.tensor_tensor_reduce(out=by_chunk(probs[qt]), in0=by_bank(ps_s), in1=by_chunk(bias), scale=-1.0, scalar=BIG,
                                         op0=ALU.add, op1=ALU.min, accum_out=negmax[:, qt:qt + 1]).then_inc(maxed, 1)

            def take_probs(rnd, j, s, kind):
                fills.wait_filled(dve, turned, rnd, (1, TILES * (j % 2) + s), kind)
                j, s = (j, s - 1) if s else (j - 1, TILES - 1)
                dve.tensor_copy(pT[j % 2][s // 2][:, 4:8, s % 2 * P:(s % 2 + 1) * P],
                                ps_t[1][:, :].rearrange("p (k q) -> p k q", q=P)).then_inc(taken[1], 1)

            def take_v(rnd, j, part, kind):
                fills.wait_filled(dve, turned, rnd, ("V", part), kind)
                dve.tensor_copy(v_sb[j // 2 % 2][:, 2 * part:2 * part + 2, :],
                                ps_t[1][:, :].rearrange("p (k c) -> p k c", c=2 * P)).then_inc(taken[1], 1)

            def g_low(n, i):
                dve.wait_ge(g_hi_ready, n + 1)
                dve.tensor_tensor(g_lo[i][:, :], ps_m[:, 0:Q], g_hi[i][:, :].bitcast(F32), ALU.subtract).then_inc(g_ready, 1)

            def context_low(b):
                dve.wait_ge(ctx_hi_ready, b + 1)
                dve.tensor_tensor(ctx_lo[:, :], ctx_in[:, :], ctx_hi[:, :].bitcast(F32), ALU.subtract).then_inc(ctx_ready, 1)

            def invert(J, par):
                dve.wait_ge(exped, TILES * (J + 1))
                dve.reciprocal(inv[:, :, :], rowsum[:, par, :, :]).then_inc(inverted, 1)

            def normalise(J):
                dve.wait_ge(inv_copied, J + 1)
                dve.wait_ge(pv_done, J + 1)
                dve.tensor_tensor(u_sb[:, :], ps_u[:, 0:Q], inv_rows[:, :], ALU.mult).then_inc(u_ready, 1)

            def add(J, b):
                dve.wait_ge(out_made, J + 1)
                x = st.X[:, bass.ds(2 * b, 2), :]
                dve.tensor_tensor(x, ps_m[:, :].rearrange("p (t d) -> p t d", t=2), x, ALU.add).then_inc(x_added, 1)

            def take_statistics(J, b):
                dve.wait_ge(x_added, J + 1)
                dve.sem_inc(dve_passed, 1)
                for qt in range(2):
                    tile_statistics(dve, st, 2 * b + qt)

            def batch(b, first, last):
                for j in range(NJ):
                    J, n = NJ * b + j, HG * (NJ * b + j)
                    rnd, kind = in_round(b, j, first)
                    started, finishing = not (first and j == 0), not (first and j < 2)
                    ending = last and j == NJ - 1
                    for s in range(TILES):
                        r = TILES * (j % 2) + s
                        if started or s >= 2:
                            fills.wait_filled(dve, turned, rnd, (3, r), kind)
                        if j == 0 and s == 0:
                            dve.wait_ge(bias_ready, b + 1)
                        rowmax(TILES * J + s, s % 2)
                        if j == NJ - 1 and s == TILES - 1 and not last:
                            context_low(b + 1)
                        if s == 0 and finishing:
                            normalise(J - 2)
                        if r % 2 == 1 and r < V_PARTS:
                            take_v(rnd, j, r, kind)
                        if s == 0:
                            g_low(n + 1, 1)
                        if s == 1:
                            if started:
                                invert(J - 1, 1 - j % 2)
                            if finishing:
                                add(J - 2, b if j >= 2 else b - 1)
                        if s == 2 and not ending:
                            g_low(n + 2, 0)
                        if s == 2 and j == 1 and not first:
                            take_statistics(J - 2, b - 1)
                        if started or s > 0:
                            take_probs(rnd, j, s, kind)

            context_low(0)
            g_low(0, 0)
            drive(dve, batch)
            J = J_ALL
            normalise(J - 2)
            take_probs(J // 2, 0, 0, "over")
            invert(J - 1, 1)
            add(J - 2, B - 1)
            normalise(J - 1)
            add(J - 1, B - 1)
            take_statistics(J - 1, B - 1)

        @block.scalar
        def _(act):
            act.sem_inc(taken[0], fills.skipped((0,)))
            act.sem_inc(taken[3], fills.skipped((3,)))

            def take_probs(rnd, g, j, s, kind):
                fills.wait_filled(act, turned, rnd, (g, TILES * (j % 2) + s), kind)
                back = 2 if g == 3 else 1
                j, s = (j, s - back) if s >= back else (j - 1, s - back + TILES)
                tiles = TURN_GROUPS[g]
                w = min(P, S - tiles[0] * P)
                act.activation(pT[j % 2][s // 2][0:w, tiles[0]:tiles[-1] + 1, s % 2 * P:(s % 2 + 1) * P],
                               ps_t[g % 2][0:w, 0:P * len(tiles)].rearrange("p (k q) -> p k q", q=P),
                               ACT.Copy).then_inc(taken[3 if g == 3 else 0], 1)

            def take_v(rnd, j, part, kind):
                fills.wait_filled(act, turned, rnd, ("V", part), kind)
                tiles = min(2, KT - 2 * part)
                w = min(P, S - 2 * part * P)
                act.activation(v_sb[j // 2 % 2][0:w, 2 * part:2 * part + tiles, :],
                               ps_t[0][0:w, 0:2 * P * tiles].rearrange("p (k c) -> p k c", c=2 * P),
                               ACT.Copy).then_inc(taken[0], 1)

            def g_high(n, i):
                act.wait_ge(g_made, n + 1)
                act.activation(g_hi[i][:, :], ps_m[:, 0:Q], ACT.Copy).then_inc(g_hi_ready, 1)

            def context_high(b):
                act.wait_ge(ctx_loaded, 16 * b + 16)
                act.activation(ctx_hi[:, :], ctx_in[:, :], ACT.Copy).then_inc(ctx_hi_ready, 1)

            def exponential(tile, par, s):
                act.wait_ge(maxed, tile + 1)
                i, qt = s // 2, s % 2
                act.activation(probs[qt][:, 0:S], probs[qt][:, 0:S], ACT.Exp, scale=-1.0, bias=negmax[:, qt:qt + 1],
                               accum_out=rowsum[:, par, i, qt:qt + 1]).then_inc(exped, 1)

            def copy_inverse(J):
                act.wait_ge(inv_spread, J + 1)
                act.activation(inv_rows[:, :], ps_m[:, Q:2 * Q], ACT.Copy).then_inc(inv_copied, 1)

            def batch(b, first, last):
                for j in range(NJ):
                    J, n = NJ * b + j, HG * (NJ * b + j)
                    rnd, kind = in_round(b, j, first)
                    started = not (first and j == 0)
                    ending = last and j == NJ - 1
                    for s in range(TILES):
                        r = TILES * (j % 2) + s
                        if j == NJ - 1 and s == TILES - 1 and not last:
                            act.wait_ge(scored, TILES * (J + 1))
                            context_high(b + 1)
                        if r % 2 == 0 and r < V_PARTS:
                            take_v(rnd, j, r, kind)
                        if started or s >= 2:
                            take_probs(rnd, 3, j, s, kind)
                        if started or s > 0:
                            take_probs(rnd, 0, j, s, kind)
                        exponential(TILES * J + s, j % 2, s)
                        if s == 0:
                            g_high(n + 1, 1)
                        if s == 2 and not ending:
                            g_high(n + 2, 0)
                        if s == 3 and started:
                            copy_inverse(J - 1)
                        if started or s > 0:
                            take_probs(rnd, 2, j, s, kind)

            context_high(0)
            g_high(0, 0)
            drive(act, batch)
            for g, s in ((3, 0), (0, 0), (2, 0), (3, 1)):
                take_probs(J_ALL // 2, g, 0, s, "over")
            copy_inverse(J_ALL - 1)


def narrow_attention_phase(nc, st, io, name, heads, width):
    HG = 4
    NJ = heads // HG
    J_ALL = B * NJ
    TILES = 2 * HG
    PAD = P // HG
    SCALE = width ** -0.5
    assert PAD == 4 * width and NJ == 4 and len(TURN_GROUPS) == 4 and len(EVEN_CHUNKS) == 4
    PV_TILES = [range(0, 4), range(4, 7), range(7, 10), range(10, KT)]

    V_FILLS = {5: (0, 1), 6: (2,), 7: (3,)}

    def round_fills(first=False, over=False):
        def tile_fills(keys, r):
            return [(k, r) for k in keys if not (first and r < 2) and not (over and r >= 2)]
        banks = {0: [], 1: []}
        for r in range(TILES * NJ):
            v = [("V", g) for g in V_FILLS.get(r, ()) if not over]
            banks[0] += [f for f in v if f[1] % 2 == 0] + tile_fills((0, 2), r)
            banks[1] += [f for f in v if f[1] % 2] + tile_fills((1, 3), r)
        return banks

    fills = TurnFills({"first": round_fills(first=True), "middle": round_fills(), "last": round_fills(),
                       "over": round_fills(over=True)},
                      lambda fill: fill[1] if fill[0] == "V" else fill[0])

    with Phase(nc, name) as ph:
        ctx = ph.sb("ctx", [P, S_EVEN])
        wq = ph.sb("wq", [P, 2, P])
        wk = ph.sb("wk", [P, P])
        wv = ph.sb("wv", [P, P])
        wo = ph.sb("wo", [P, NJ, D])
        head_picks = ph.sb("head_picks", [P, HG])
        bias = ph.sb("bias", [P, S_EVEN])
        q_hi = ph.sb("q_hi", [P, Q], F32R)
        q_lo = ph.sb("q_lo", [P, Q], F32R)
        q_mixed = ph.sb("q_mixed", [P, Q], F32R)
        q_head = [[ph.sb(f"q_head{i}{k}", [P, Q], F32R) for k in range(HG)] for i in range(2)]
        k_hi = ph.sb("k_hi", [P, S_EVEN], F32R)
        k_lo = ph.sb("k_lo", [P, S_EVEN], F32R)
        k_mixed = [ph.sb(f"k_mixed{i}", [P, S_EVEN], F32R) for i in range(2)]
        probs = [ph.sb(f"probs{i}", [P, S_EVEN]) for i in range(HG)]
        negmax = ph.sb("negmax", [P, HG])
        rowsum = ph.sb("rowsum", [P, 2, HG])
        inv = ph.sb("inv", [P, 2, HG])
        turned_size = KT * P
        spare = [st.A[:, :, :].rearrange("p a c -> p (a c)"), st.Bw[:, :]]
        pT = [[spare[i // 2][:, (i % 2) * turned_size:(i % 2 + 1) * turned_size].rearrange("p (k q) -> p k q", q=P)
               for i in range(HG)],
              [ph.sb(f"pT{i}", [P, KT, P])[:, :, :] for i in range(HG)]]
        v_sb = ph.sb("v_sb", [P, KT, P + PAD - width])
        inv_rows = ph.sb("inv_rows", [P, P])
        u_sb = ph.sb("u_sb", [P, P])
        ps_s = ph.ps("ps_s", [P, 4 * BANK])
        ps_t = [ph.ps(f"ps_t{i}", [P, BANK]) for i in range(2)]
        ps_u = ph.ps("ps_u", [P, BANK])
        ps_m = ph.ps("ps_m", [P, BANK])

        weights_loaded = ph.sem("weights_loaded")
        ctx_loaded = ph.sem("ctx_loaded")
        bias_ready = ph.sem("bias_ready")
        q_made = ph.sem("q_made")
        q_hi_ready = ph.sem("q_hi_ready")
        q_ready = ph.sem("q_ready")
        q_spread = ph.sem("q_spread")
        q_picked = ph.sem("q_picked")
        k_made = ph.sem("k_made")
        k_hi_ready = ph.sem("k_hi_ready")
        k_ready = ph.sem("k_ready")
        k_spread = [ph.sem(f"k_spread{i}") for i in range(2)]
        scored = ph.sem("scored")
        maxed = ph.sem("maxed")
        exped = ph.sem("exped")
        turned = [ph.sem(f"turned{i}") for i in range(2)]
        taken = [ph.sem(f"taken{i}") for i in range(4)]
        inverted = ph.sem("inverted")
        inv_spread = ph.sem("inv_spread")
        inv_taken = ph.sem("inv_taken")
        pv_done = ph.sem("pv_done")
        u_ready = ph.sem("u_ready")
        out_made = ph.sem("out_made")
        x_added = ph.sem("x_added")
        dve_passed = ph.sem("dve_passed")
        pool_passed = ph.sem("pool_passed")
        sp_passed = ph.sem("sp_passed")
        block = ph.block()

        def drive(eng, group, finish):
            for j in range(NJ):
                group(0, j, j == 0, False)
            with eng.Fori(1, B - 1) as b:
                for j in range(NJ):
                    group(b, j, False, False)
            for j in range(NJ):
                group(B - 1, j, False, j == NJ - 1)
            finish()

        @block.sync
        def _(sp):
            def load_context(b):
                sp.dma_start(ctx[:, :], io["ctxT"][bass.ds(b, 1), :, :].rearrange("a c s -> (a c) s")).then_inc(ctx_loaded, 16)

            def spread(J, j, par):
                rows = slice(j * PAD, (j + 1) * PAD)
                for copy, part in enumerate((k_hi, k_hi, k_lo, k_lo)):
                    sp.dma_start(k_mixed[par][copy * PAD:(copy + 1) * PAD, :].bitcast(F32), part[rows, :].bitcast(F32)).then_inc(k_spread[par], 16)
                if j != 0 or not isinstance(J, int) or J > 0:
                    sp.wait_ge(q_picked, HG * J)
                    sp.sem_inc(sp_passed, 1)
                for copy, part in enumerate((q_hi, q_lo, q_hi, q_lo)):
                    sp.dma_start(q_mixed[copy * PAD:(copy + 1) * PAD, :].bitcast(F32), part[rows, :].bitcast(F32)).then_inc(q_spread, 16)

            def group(b, j, first, last):
                J = NJ * b + j
                if j == 1 and not (isinstance(b, int) and b == B - 1):
                    kind = "first" if isinstance(b, int) and b == 0 else "middle"
                    fills.wait_filled(sp, turned, b, ("V", 2), kind)
                    sp.sem_inc(sp_passed, 1)
                    fills.wait_filled(sp, turned, b, ("V", 3), kind)
                    sp.sem_inc(sp_passed, 1)
                    load_context(b + 1)
                if last:
                    return
                if not first:
                    sp.wait_ge(scored, TILES * J)
                    sp.sem_inc(sp_passed, 1)
                if j == NJ - 1:
                    sp.wait_ge(k_ready, 4 * (b + 2))
                    sp.sem_inc(sp_passed, 1)
                spread(J + 1, (j + 1) % NJ, (j + 1) % 2)

            sp.dma_start(wq[:, :, :], io[f"{name}_wq"]).then_inc(weights_loaded, 16)
            sp.dma_start(wk[:, :], io[f"{name}_wk"]).then_inc(weights_loaded, 16)
            load_context(0)
            sp.dma_start(wv[:, :], io[f"{name}_wv"]).then_inc(weights_loaded, 16)
            sp.dma_start(wo[:, :, :], io[f"{name}_wo"]).then_inc(weights_loaded, 16)
            sp.dma_start(head_picks[:, :], io["head_picks"]).then_inc(weights_loaded, 16)
            sp.wait_ge(q_ready, 1)
            sp.wait_ge(k_ready, 4)
            spread(0, 0, 0)
            drive(sp, group, lambda: None)

        @block.gpsimd
        def _(pool):
            def pick_heads(J, par):
                pool.wait_ge(q_spread, 64 * (J + 1))
                pool.sem_inc(pool_passed, 1)
                for i in range(HG):
                    pool.tensor_scalar(q_head[par][i][:, :], q_mixed[:, :].bitcast(F32), head_picks[:, i:i + 1], None,
                                       ALU.mult).then_inc(q_picked, 1)

            def group(b, j, first, last):
                J = NJ * b + j
                if not last:
                    if not first:
                        pool.wait_ge(scored, TILES * J)
                    pick_heads(J + 1, (j + 1) % 2)

            pool.memset(v_sb[:, :, P:], 0.0)
            pool.memset(bias[:, 0:S], 0.0)
            pool.memset(bias[:, S:S_EVEN], -NEG).then_inc(bias_ready, 1)
            pool.wait_ge(weights_loaded, 80)
            pick_heads(0, 0)
            drive(pool, group, lambda: None)

        @block.tensor
        def _(pe):
            pe.sem_inc(turned[0], fills.skipped((0, 2)))
            pe.sem_inc(turned[1], fills.skipped((1, 3)))

            def make_q(b):
                for f in range(2):
                    ins = pe.matmul(ps_m[:, 0:Q], wq[:, f, :], st.XT[:, f, bass.ts(b, Q)], start=(f == 0), stop=(f == 1))
                ins.then_inc(q_made, 1)

            def make_k(i):
                c, w = EVEN_CHUNKS[i]
                pe.matmul(ps_m[:, 0:w], wk[:, :], ctx[:, c:c + w], start=True, stop=True).then_inc(k_made, 1)

            def fill(g, put):
                for k in TURN_GROUPS[g]:
                    ins = put(k, ps_t[g % 2][0:min(P, S - k * P), (k % 4) * P:(k % 4 + 1) * P])
                ins.then_inc(turned[g % 2], 1)

            def make_v(g):
                fill(g, lambda k, out: pe.matmul(out, ctx[:, k * P:min(k * P + P, S)], wv[:, :], start=True, stop=True))

            def turn(b, g, r, kind):
                source = probs[(r - 2) % HG]
                fills.wait_free(pe, taken, b, (g, r), kind)
                fill(g, lambda k, out: pe.transpose(out, source[:, k * P:min(k * P + P, S)], st.ident[:, :]))

            def scores(t, s, par):
                qt, i = s // HG, s % HG
                for bank, (c, w) in enumerate(EVEN_CHUNKS):
                    ins = pe.matmul(ps_s[:, bank * BANK:bank * BANK + w], q_head[par][i][:, qt * P:(qt + 1) * P], k_mixed[par][:, c:c + w],
                                    start=True, stop=True)
                ins.then_inc(scored, 1)

            def pv(j, qt, part, half):
                tiles = PV_TILES[part]
                for k in (tiles[:len(tiles) // 2], tiles[len(tiles) // 2:])[half]:
                    w = min(P, S - k * P)
                    for i in range(HG):
                        c = (HG * j + i) * width
                        ins = pe.matmul(ps_u[i * PAD:(i + 1) * PAD, 0:P], v_sb[0:w, k, c:c + PAD],
                                        pT[qt][i][0:w, k, :], start=(k == 0), stop=(k == KT - 1))
                if (part, half) == (len(PV_TILES) - 1, 1):
                    ins.then_inc(pv_done, 1)

            def wait_turned(b, r, part, kind):
                fills.wait_taken(pe, taken, b, (part, r), kind)

            def spread_inverse(m, qt):
                pe.wait_ge(inverted, m + 1)
                for i in range(HG):
                    ins = pe.matmul(ps_m[i * PAD:(i + 1) * PAD, Q:Q + P], inv[:, qt, i:i + 1].to_broadcast([P, PAD]),
                                    st.ident[:, :], start=True, stop=True)
                ins.then_inc(inv_spread, 1)

            def output(m, j):
                pe.wait_ge(u_ready, m + 1)
                pe.matmul(ps_m[:, 0:D], u_sb[:, :], wo[:, j, :], start=True, stop=True).then_inc(out_made, 1)

            def group(b, j, first, last):
                J, par = NJ * b + j, j % 2
                before = (j - 1) % NJ
                at_start = isinstance(b, int) and b == 0
                kind = "first" if at_start else "middle"
                making = j == NJ - 1 and not last
                for s in range(TILES):
                    t, r = TILES * J + s, TILES * j + s
                    if s == 0:
                        pe.wait_ge(q_picked, HG * (J + 1))
                        pe.wait_ge(k_spread[par], 64 * (NJ // 2 * b + j // 2 + 1))
                    if not (first and s == 0):
                        pe.wait_ge(maxed, t)
                    scores(t, s, par)
                    if s < 2:
                        part, unit = s + 2, (before, 0)
                        turned_in = (b, TILES * j - 3) if j else (b - 1, TILES * NJ - 3)
                    elif s < 6:
                        part, unit, turned_in = s - 2, (before, 1), (b, TILES * j + 1)
                    else:
                        part, unit, turned_in = s - 6, (j, 0), (b, TILES * j + 5)
                    if s in (2, 6) and not first:
                        pe.wait_ge(u_ready, 2 * J + s // 4 - 1)
                    if not first or s >= 6:
                        back_kind = "first" if isinstance(b, int) and b == 1 and turned_in[1] > r else kind
                        wait_turned(*turned_in, part, back_kind)
                        pv(*unit, part, 0)
                    if s == 0:
                        if not (at_start and j < 2):
                            pe.wait_ge(x_added, 2 * J - 2)
                        if not first:
                            spread_inverse(2 * J - 2, 0)
                        if making:
                            make_q(b + 1)
                    if 1 <= s < 5 and making:
                        if s == 1:
                            pe.wait_ge(q_ready, b + 2)
                            pe.wait_ge(ctx_loaded, 16 * (b + 2))
                        elif s == 3:
                            pe.wait_ge(x_added, 2 * J - 1)
                        else:
                            pe.wait_ge(k_ready, 4 * (b + 1) + s - 1)
                        make_k(s - 1)
                    if j == 0:
                        for g in V_FILLS.get(s, ()):
                            fills.wait_free(pe, taken, b, ("V", g), kind)
                            make_v(g)
                    if not first or s >= 2:
                        pe.wait_ge(exped, t - 1)
                        turn(b, 0, r, kind)
                        turn(b, 1, r, kind)
                    if not first or s >= 6:
                        pv(*unit, part, 1)
                    if s == 2 and not first:
                        if making:
                            pe.wait_ge(k_ready, 4 * (b + 1) + 2)
                        else:
                            pe.wait_ge(inv_taken, 2 * J - 1)
                        output(2 * J - 2, before)
                    if s == 4 and not first:
                        if making:
                            pe.wait_ge(k_ready, 4 * (b + 1) + 4)
                        else:
                            pe.wait_ge(x_added, 2 * J - 1)
                        spread_inverse(2 * J - 1, 1)
                    if s == 6 and not first:
                        pe.wait_ge(inv_taken, 2 * J)
                        output(2 * J - 1, before)
                    if not first or s >= 2:
                        turn(b, 2, r, kind)
                        turn(b, 3, r, kind)

            def finish():
                J, j = J_ALL, NJ - 1
                for s in range(2):
                    wait_turned(B - 1, TILES * NJ - 3, s + 2, "last")
                    for half in range(2):
                        pv(j, 0, s + 2, half)
                    pe.wait_ge(exped, TILES * J + s - 1)
                    for g in range(4):
                        turn(B, g, s, "over")
                pe.wait_ge(x_added, 2 * J - 2)
                spread_inverse(2 * J - 2, 0)
                pe.wait_ge(inv_taken, 2 * J - 1)
                output(2 * J - 2, j)
                pe.wait_ge(u_ready, 2 * J - 1)
                for part in range(4):
                    wait_turned(B, 1, part, "over")
                    for half in range(2):
                        pv(j, 1, part, half)
                pe.wait_ge(x_added, 2 * J - 1)
                spread_inverse(2 * J - 1, 1)
                pe.wait_ge(inv_taken, 2 * J)
                output(2 * J - 1, j)

            pe.wait_ge(weights_loaded, 80)
            make_q(0)
            pe.wait_ge(ctx_loaded, 16)
            for i in range(4):
                if i == 0:
                    pe.wait_ge(q_ready, 1)
                else:
                    pe.wait_ge(k_ready, i)
                make_k(i)
            drive(pe, group, finish)

        @block.vector
        def _(dve):
            dve.sem_inc(taken[2], fills.skipped((2,)))
            dve.sem_inc(taken[3], fills.skipped((3,)))

            def rowmax(t, s):
                dve.wait_ge(scored, t + 1)
                dve.sem_inc(dve_passed, 1)
                i = s % HG
                dve.tensor_tensor_reduce(out=by_chunk(probs[i]), in0=by_bank(ps_s), in1=by_chunk(bias), scale=-SCALE, scalar=BIG,
                                         op0=ALU.add, op1=ALU.min, accum_out=negmax[:, i:i + 1]).then_inc(maxed, 1)

            def take(g, to):
                tiles = TURN_GROUPS[g]
                w = min(P, S - tiles[0] * P)
                dve.tensor_copy(to[0:w, tiles[0]:tiles[-1] + 1, 0:P],
                                ps_t[g % 2][0:w, 0:P * len(tiles)].rearrange("p (k q) -> p k q", q=P)).then_inc(taken[g], 1)

            def take_probs(b, g, r, kind):
                fills.wait_filled(dve, turned, b, (g, r), kind)
                s = (r - 2) % TILES
                take(g, pT[s // HG][s % HG])

            def q_low(b, first):
                dve.wait_ge(q_hi_ready, b + 1)
                if not first:
                    dve.wait_ge(inv_taken, 2 * (NJ * b - 1) - 1)
                dve.tensor_tensor(q_lo[:, :], ps_m[:, 0:Q], q_hi[:, :].bitcast(F32), ALU.subtract).then_inc(q_ready, 1)

            def k_low(b, i):
                c, w = EVEN_CHUNKS[i]
                dve.wait_ge(k_hi_ready, 4 * b + i + 1)
                dve.tensor_tensor(k_lo[:, c:c + w], ps_m[:, 0:w], k_hi[:, c:c + w].bitcast(F32), ALU.subtract).then_inc(k_ready, 1)

            def invert(m, qt):
                dve.wait_ge(exped, HG * (m + 1))
                dve.reciprocal(inv[:, qt, :], rowsum[:, qt, :]).then_inc(inverted, 1)

            def normalise(m):
                dve.wait_ge(inv_taken, m + 1)
                dve.wait_ge(pv_done, m + 1)
                dve.tensor_tensor(u_sb[:, :], ps_u[:, 0:P], inv_rows[:, :], ALU.mult).then_inc(u_ready, 1)

            def add(m, row):
                dve.wait_ge(out_made, m + 1)
                x = st.X[:, bass.ds(row, 1), :].rearrange("p a d -> p (a d)")
                dve.tensor_tensor(x, ps_m[:, 0:D], x, ALU.add).then_inc(x_added, 1)

            def take_statistics(m, b):
                dve.wait_ge(x_added, m + 1)
                dve.sem_inc(dve_passed, 1)
                for qt in range(2):
                    tile_statistics(dve, st, 2 * b + qt)

            def group(b, j, first, last):
                J, par = NJ * b + j, j % 2
                b_before = b - 1 if j == 0 else b
                making = j == NJ - 1 and not last
                kind = "first" if isinstance(b, int) and b == 0 else "middle"
                for s in range(TILES):
                    rowmax(TILES * J + s, s)
                    if making and s < 5:
                        if s == 0:
                            q_low(b + 1, False)
                        else:
                            k_low(b + 1, s - 1)
                    if j == 0 and s in (6, 7):
                        fills.wait_filled(dve, turned, b, ("V", s - 4), kind)
                        take(s - 4, v_sb)
                    if s in (1, 5) and not first:
                        normalise(2 * J - 2 + s // 4)
                    if s == 7 and j == 0 and not first:
                        take_statistics(2 * J - 1, b - 1)
                    if not first or s >= 2:
                        take_probs(b, 2, TILES * j + s, kind)
                        take_probs(b, 3, TILES * j + s, kind)
                    if s == 2 and not first:
                        add(2 * J - 2, 2 * b_before)
                        invert(2 * J - 1, 1)
                    if s == 6:
                        if not first:
                            add(2 * J - 1, 2 * b_before + 1)
                        invert(2 * J, 0)

            def finish():
                J = J_ALL
                for s in range(2):
                    for g in (2, 3):
                        take_probs(B, g, s, "over")
                invert(2 * J - 1, 1)
                normalise(2 * J - 2)
                add(2 * J - 2, 2 * B - 2)
                normalise(2 * J - 1)
                add(2 * J - 1, 2 * B - 1)
                take_statistics(2 * J - 1, B - 1)

            q_low(0, True)
            for i in range(4):
                k_low(0, i)
            dve.wait_ge(bias_ready, 1)
            drive(dve, group, finish)

        @block.scalar
        def _(act):
            act.sem_inc(taken[0], fills.skipped((0,)))
            act.sem_inc(taken[1], fills.skipped((1,)))

            def take(g, to):
                tiles = TURN_GROUPS[g]
                act.activation(to[:, tiles[0]:tiles[-1] + 1, 0:P], ps_t[g][:, :].rearrange("p (k q) -> p k q", q=P),
                               ACT.Copy).then_inc(taken[g], 1)

            def take_probs(b, g, r, kind):
                fills.wait_filled(act, turned, b, (g, r), kind)
                s = (r - 2) % TILES
                take(g, pT[s // HG][s % HG])

            def q_high(b):
                act.wait_ge(q_made, b + 1)
                act.activation(q_hi[:, :], ps_m[:, 0:Q], ACT.Copy).then_inc(q_hi_ready, 1)

            def k_high(b, i):
                c, w = EVEN_CHUNKS[i]
                act.wait_ge(k_made, 4 * b + i + 1)
                act.activation(k_hi[:, c:c + w], ps_m[:, 0:w], ACT.Copy).then_inc(k_hi_ready, 1)

            def take_inverse(m):
                act.wait_ge(inv_spread, m + 1)
                act.activation(inv_rows[:, :], ps_m[:, Q:Q + P], ACT.Copy).then_inc(inv_taken, 1)

            def exponential(t, s):
                qt, i = s // HG, s % HG
                act.wait_ge(maxed, t + 1)
                act.activation(probs[i][:, 0:S], probs[i][:, 0:S], ACT.Exp, scale=-1.0, bias=negmax[:, i:i + 1],
                               accum_out=rowsum[:, qt, i:i + 1]).then_inc(exped, 1)

            def group(b, j, first, last):
                J = NJ * b + j
                making = j == NJ - 1 and not last
                kind = "first" if isinstance(b, int) and b == 0 else "middle"
                for s in range(TILES):
                    r = TILES * j + s
                    if making and s < 5:
                        if s == 0:
                            q_high(b + 1)
                        else:
                            k_high(b + 1, s - 1)
                    if s == 0 and not first:
                        take_inverse(2 * J - 2)
                    if j == 0 and s == 5:
                        for g in (0, 1):
                            fills.wait_filled(act, turned, b, ("V", g), kind)
                            take(g, v_sb)
                    if not first or s >= 2:
                        take_probs(b, 0, r, kind)
                        take_probs(b, 1, r, kind)
                    exponential(TILES * J + s, s)
                    if s == 4 and not first:
                        take_inverse(2 * J - 1)

            def finish():
                for s in range(2):
                    for g in (0, 1):
                        take_probs(B, g, s, "over")
                take_inverse(2 * J_ALL - 2)
                take_inverse(2 * J_ALL - 1)

            q_high(0)
            for i in range(4):
                k_high(0, i)
            drive(act, group, finish)


def mlp_phase(nc, st, io, name, gate):
    F = 4 * D
    FT = F // P
    TC = BANK
    NC = B * Q // TC
    (w1_hi, w1_lo), (w2_hi, w2_lo) = st.mlp_weights
    with Phase(nc, name) as ph:
        g = ph.sb("g", [P, 2])
        x_hi = [ph.sb(f"x_hi{i}", [P, 2, TC], F32R) for i in range(2)]
        x_lo = [ph.sb(f"x_lo{i}", [P, 2, TC], F32R) for i in range(2)]
        hid = [ph.sb(f"hid{i}", [P, TC]) for i in range(2)]
        hid_hi = [ph.sb(f"hid_hi{i}", [P, FT, TC], F32R) for i in range(2)]
        hid_lo = [ph.sb(f"hid_lo{i}", [P, FT, TC], F32R) for i in range(2)]
        ps_h = [ph.ps(f"ps_h{i}", [P, TC]) for i in range(2)]
        ps_y = [ph.ps(f"ps_y{i}", [P, D]) for i in range(2)]
        loaded = ph.sem("loaded")
        gate_ready = ph.sem("gate_ready")
        x_hi_ready = ph.sem("x_hi_ready")
        x_ready = ph.sem("x_ready")
        hid_made = ph.sem("hid_made")
        gelu_done = ph.sem("gelu_done")
        hi_ready = ph.sem("hi_ready")
        hid_ready = ph.sem("hid_ready")
        y_made = ph.sem("y_made")
        y_added = ph.sem("y_added")
        pool_passed = ph.sem("pool_passed")
        dve_passed = ph.sem("dve_passed")
        block = ph.block()

        @block.sync
        def _(sp):
            sp.dma_start(g[:, 0:1], io[gate].to_broadcast([P, 1])).then_inc(loaded, 16)

        def split_products(out, hi, lo, hi2, lo2, start, stop):
            return [(out, hi, hi2, start, False), (out, hi, lo2, False, False), (out, lo, hi2, False, stop)]

        @block.gpsimd
        def _(pool):
            with pool.Fori(0, NC // 2) as i:
                for par in range(2):
                    c = 2 * i + par
                    src = st.XT[:, :, bass.ts(c, TC)]
                    pool.wait_ge(gelu_done, FT * (2 * i) + 2)
                    pool.sem_inc(pool_passed, 1)
                    pool.tensor_copy(x_hi[par][:, :, :], src).then_inc(x_hi_ready, 1)
                    pool.wait_ge(x_hi_ready, c + 1)
                    pool.sem_inc(pool_passed, 1)
                    pool.tensor_tensor(x_lo[par][:, :, :], src, x_hi[par][:, :, :].bitcast(F32), ALU.subtract).then_inc(x_ready, 1)

        @block.tensor
        def _(pe):
            def multiply(products):
                for out, a, b, start, stop in products:
                    ins = pe.matmul(out, a, b, start=start, stop=stop)
                return ins

            with pe.Fori(0, NC // 2) as i:
                for par in range(2):
                    c = 2 * i + par
                    pe.wait_ge(x_ready, c + 1)
                    for t in range(FT):
                        m = c * FT + t
                        pe.wait_ge(gelu_done, m + 1)
                        w = slice(t * P, (t + 1) * P)
                        for f in range(2):
                            ins = multiply(split_products(ps_h[t % 2][:, :], w1_hi[:, f, w], w1_lo[:, f, w],
                                                          x_hi[par][:, f, :], x_lo[par][:, f, :], f == 0, f == 1))
                        ins.then_inc(hid_made, 1)
                for par in range(2):
                    c = 2 * i + par
                    pe.wait_ge(hid_ready, FT * (c + 1) + 2)
                    for r in range(TC // P):
                        pe.wait_ge(y_added, 4 * c + r + 1)
                        q = slice(r * P, (r + 1) * P)
                        for t in range(FT):
                            ins = multiply(split_products(ps_y[r % 2][:, :], hid_hi[par][:, t, q], hid_lo[par][:, t, q],
                                                          w2_hi[:, t, :], w2_lo[:, t, :], t == 0, t == FT - 1))
                        ins.then_inc(y_made, 1)

        @block.scalar
        def _(act):
            act.sem_inc(gelu_done, 2)
            act.wait_ge(loaded, 16)
            act.activation(g[:, 1:2], g[:, 0:1], ACT.Tanh).then_inc(gate_ready, 1)
            with act.Fori(0, NC // 2) as i:
                for par in range(2):
                    for t in range(FT):
                        m = (2 * i + par) * FT + t
                        act.wait_ge(hid_made, m + 1)
                        act.wait_ge(hid_ready, m + 1)
                        act.activation(hid[t % 2][:, :], ps_h[t % 2][:, :], ACT.Gelu).then_inc(gelu_done, 1)

        @block.vector
        def _(dve):
            dve.sem_inc(y_added, 2)
            dve.sem_inc(hid_ready, 2)
            dve.wait_ge(gate_ready, 1)
            with dve.Fori(0, NC // 2) as i:
                for par in range(2):
                    for t in range(FT):
                        m = (2 * i + par) * FT + t
                        dve.wait_ge(gelu_done, m + 3)
                        dve.tensor_copy(hid_hi[par][:, t, :], hid[t % 2][:, :]).then_inc(hi_ready, 1)
                        dve.wait_ge(hi_ready, m + 1)
                        dve.tensor_tensor(hid_lo[par][:, t, :], hid[t % 2][:, :], hid_hi[par][:, t, :].bitcast(F32),
                                          ALU.subtract).then_inc(hid_ready, 1)
                for r in range(2 * TC // P):
                    j = 8 * i + r
                    x = st.X[:, bass.ds(j, 1), :].squeeze(1)
                    dve.wait_ge(y_made, j + 1)
                    dve.scalar_tensor_tensor(out=x, in0=ps_y[r % 2][:, :], scalar=g[:, 1:2],
                                             in1=x, op0=ALU.mult, op1=ALU.add).then_inc(y_added, 1)
                    dve.wait_ge(y_added, j + 3)
                    dve.sem_inc(dve_passed, 1)
                    tile_statistics(dve, st, j)


def expert_masks_phase(nc, st, io):
    with Phase(nc, "masks") as ph:
        types = ph.sb("types", [P, B, Q], I32)
        is_one = ph.sb("is_one", [P, B, Q])
        pos_in = ph.sb("pos_in", [P, Q], I32)
        pos = ph.sb("pos", [P, 2, Q])
        rows = ph.sb("rows", [P, 2])
        onehot = ph.sb("onehot", [P, 2, Q])
        table = ph.sb("table", [P, 2, 24])
        picked = ph.ps("picked", [P, 2, 24])
        loaded = ph.sem("loaded")
        chain_sem = ph.sem("chain")
        onehot_ready = ph.sem("onehot_ready")
        picks_done = ph.sem("picks_done")
        block = ph.block()

        @block.sync
        def _(sp):
            sp.dma_start(types[:, :, :], io["types"].rearrange("b q -> (b q)").unsqueeze(0).to_broadcast([P, B * Q]).rearrange("p (b q) -> p b q", b=B)).then_inc(loaded, 16)
            sp.dma_start(pos_in[:, :], io["positions"].to_broadcast([P, Q])).then_inc(loaded, 16)
            sp.dma_start(rows[:, :], io["row_numbers"]).then_inc(loaded, 16)
            sp.dma_start(table[:, :, :], io["rope_table"]).then_inc(loaded, 16)
            sp.dma_start(st.head_rows[:, :], io["head_rows"]).then_inc(loaded, 16)

        @block.vector
        def _(dve):
            chain = Chain(dve, chain_sem)
            dve.wait_ge(loaded, 80)
            chain(dve.tensor_scalar(pos[:, 0, :], pos_in[:, :], 0.0, float(Q), ALU.is_lt, ALU.mult))
            chain(dve.tensor_tensor(pos[:, 1, :], pos_in[:, :], pos[:, 0, :], ALU.add))
            chain(dve.tensor_scalar(pos[:, 0, :], pos[:, 1, :], 0.0, float(Q - 1), ALU.max, ALU.min))
            for k in range(2):
                ins = dve.tensor_scalar(onehot[:, k, :], pos[:, 0, :], rows[:, k:k + 1], None, ALU.is_equal)
            ins.then_inc(onehot_ready, 1)
            chain(dve.tensor_scalar(is_one[:, :, :], types[:, :, :], 1.0, None, ALU.is_equal))
            dve.tensor_tensor(st.vm[:, :, 0:Q - 1], is_one[:, :, 0:Q - 1], is_one[:, :, 1:Q], ALU.mult)
            dve.memset(st.vm[:, :, Q - 1:Q], 0.0)
            dve.wait_ge(picks_done, 1)
            dve.tensor_copy(st.rope[:, :, :], picked[:, :, :])

        @block.tensor
        def _(pe):
            pe.wait_ge(onehot_ready, 1)
            for t in range(2):
                for k in range(2):
                    ins = pe.matmul(picked[:, t, :], onehot[:, k, t * P:(t + 1) * P], table[:, k, :],
                                    start=(k == 0), stop=(k == 1))
            ins.then_inc(picks_done, 1)


def self_attention_phase(nc, st, io):
    H, W = 16, 16
    with Phase(nc, "self") as ph:
        wqkv = ph.sb("wqkv", [P, 2, 2, 3 * D])
        wd = ph.sb("wd", [P, 2, 2, D])
        causal = ph.sb("causal", [P, Q])
        z = ph.sb("z", [P, 2, 2, Q])
        rot_a = ph.sb("rot_a", [P, 2, 2 * D])
        rot_b = ph.sb("rot_b", [P, 2, 2 * D])
        v_sb = ph.sb("v_sb", [P, 2, D])
        kT = ph.sb("kT", [P, 2, Q])
        qT = ph.sb("qT", [P, 2, Q])
        qm = ph.sb("qm", [P, H, Q])
        neg = ph.sb("neg", [P, 2, 3 * P])
        probs = ph.sb("probs", [P, 2, 3 * P])
        negmax = ph.sb("negmax", [P, 2, 2])
        rowsum = ph.sb("rowsum", [P, 2, H])
        inv = ph.sb("inv", [P, 2, H])
        pT = ph.sb("pT", [P, 2, 3 * P])
        o_sb = ph.sb("o_sb", [P, 2, D])
        oT = ph.sb("oT", [P, 2, 2, Q])
        ps_qk = [ph.ps(f"ps_qk{i}", [P, BANK]) for i in range(2)]
        ps_v = ph.ps("ps_v", [P, 2, D])
        ps_t = [ph.ps(f"ps_t{i}", [P, BANK]) for i in range(2)]
        ps_oT = ph.ps("ps_oT", [P, 2, Q])
        ps_y = ph.ps("ps_y", [P, 2, D])
        loaded = ph.sem("loaded")
        z_ready = ph.sem("z_ready")
        qk_made = ph.sem("qk_made")
        v_made = ph.sem("v_made")
        v_ready = ph.sem("v_ready")
        chain = ph.sem("chain")
        rot_ready = ph.sem("rot_ready")
        qkT_made = ph.sem("qkT_made")
        qkT_ready = ph.sem("qkT_ready")
        qm_ready = ph.sem("qm_ready")
        scored = ph.sem("scored")
        maxed = ph.sem("maxed")
        exped = ph.sem("exped")
        turned = ph.sem("turned")
        pT_ready = ph.sem("pT_ready")
        pv_done = ph.sem("pv_done")
        inverted = ph.sem("inverted")
        o_ready = ph.sem("o_ready")
        oT_made = ph.sem("oT_made")
        oT_ready = ph.sem("oT_ready")
        y_made = ph.sem("y_made")
        y_added = ph.sem("y_added")
        dve_passed = ph.sem("dve_passed")
        pool_passed = ph.sem("pool_passed")
        block = ph.block()

        @block.sync
        def _(sp):
            for e, n in enumerate("vl"):
                sp.dma_start(wqkv[:, e, :, :], io[f"L1_{n}_qkv"]).then_inc(loaded, 16)
                sp.dma_start(wd[:, e, :, :], io[f"L1_{n}_dense"]).then_inc(loaded, 16)
            sp.dma_start(causal[:, :], io["causal"]).then_inc(loaded, 16)

        @block.tensor
        def _(pe):
            pe.sem_inc(turned, 2)
            pe.sem_inc(pv_done, 2)
            pe.wait_ge(loaded, 80)

            def project_qk(b, t):
                for i in range(4):
                    e, f = divmod(i, 2)
                    ins = pe.matmul(ps_qk[t][:, :], z[:, e, f, t * P:(t + 1) * P], wqkv[:, e, f, 0:2 * D],
                                    start=(i == 0), stop=(i == 3))
                ins.then_inc(qk_made, 1)

            def project_v(b):
                for t in range(2):
                    for i in range(4):
                        e, f = divmod(i, 2)
                        ins = pe.matmul(ps_v[:, t, :], z[:, e, f, t * P:(t + 1) * P], wqkv[:, e, f, 2 * D:3 * D],
                                        start=(i == 0), stop=(i == 3))
                ins.then_inc(v_made, 1)

            def turn_qk(b, t):
                pe.wait_ge(rot_ready, 2 * b + t + 1)
                for i in range(4):
                    ins = pe.transpose(ps_t[t][:, i * P:(i + 1) * P], rot_a[:, t, i * P:(i + 1) * P],
                                       st.ident[:, :])
                ins.then_inc(qkT_made, 1)

            def batch(b, at_end):
                n0 = b * H
                for h in range(H + 2):
                    if h < H:
                        n = n0 + h
                        f = h // 8
                        if h == 0:
                            pe.wait_ge(qkT_ready, 2 * b + 2)
                        pe.wait_ge(qm_ready, n + 1)
                        pe.wait_ge(maxed, 2 * n + 2)
                        s = ps_qk[h % 2]
                        pe.matmul(s[:, 0:P], qm[:, h, 0:P], kT[:, f, 0:P], start=True, stop=True)
                        pe.matmul(s[:, P:3 * P], qm[:, h, P:2 * P], kT[:, f, :], start=True, stop=True)\
                            .then_inc(scored, 1)
                    elif not at_end:
                        if h == H:
                            pe.wait_ge(z_ready, b + 2)
                        pe.wait_ge(maxed, 2 * (n0 + h) + 2)
                        project_qk(b + 1, h - H)
                    if 1 <= h <= H:
                        n = n0 + h - 1
                        p = (h - 1) % 2
                        pe.wait_ge(exped, 2 * n + 6)
                        pe.wait_ge(pT_ready, n + 1)
                        for i in range(3):
                            ins = pe.transpose(ps_t[p][:, i * P:(i + 1) * P], probs[:, p, i * P:(i + 1) * P],
                                               st.ident[:, :])
                        ins.then_inc(turned, 1)
                    if h >= 2:
                        n = n0 + h - 2
                        p = (h - 2) % 2
                        c = slice((h - 2) * W, (h - 1) * W)
                        pe.wait_ge(pT_ready, n + 3)
                        if h == 2:
                            pe.wait_ge(v_ready, b + 1)
                        pe.matmul(ps_v[:, 0, c], pT[:, p, 0:P], v_sb[:, 0, c], start=True, stop=True)
                        pe.matmul(ps_v[:, 1, c], pT[:, p, P:2 * P], v_sb[:, 0, c], start=True, stop=False)
                        pe.matmul(ps_v[:, 1, c], pT[:, p, 2 * P:3 * P], v_sb[:, 1, c], start=False, stop=True)\
                            .then_inc(pv_done, 1)
                pe.wait_ge(o_ready, b + 1)
                if not at_end:
                    project_v(b + 1)
                for f in range(2):
                    for t in range(2):
                        ins = pe.transpose(ps_oT[:, f, t * P:(t + 1) * P], o_sb[:, t, f * P:(f + 1) * P],
                                           st.ident[:, :])
                ins.then_inc(oT_made, 1)
                if not at_end:
                    for t in range(2):
                        turn_qk(b + 1, t)
                pe.wait_ge(oT_ready, b + 1)
                pe.wait_ge(y_added, b + 1)
                for t in range(2):
                    for i in range(4):
                        e, f = divmod(i, 2)
                        ins = pe.matmul(ps_y[:, t, :], oT[:, e, f, t * P:(t + 1) * P], wd[:, e, f, :],
                                        start=(i == 0), stop=(i == 3))
                ins.then_inc(y_made, 1)

            pe.wait_ge(z_ready, 1)
            for t in range(2):
                project_qk(0, t)
            project_v(0)
            for t in range(2):
                turn_qk(0, t)
            with pe.Fori(0, B - 1) as b:
                batch(b, False)
            batch(B - 1, True)

        @block.vector
        def _(dve):
            dve.sem_inc(maxed, 4)
            dve.sem_inc(y_added, 1)
            dve.wait_ge(loaded, 80)

            def pick(to, src, b, sem, seen):
                for f in range(2):
                    ins = dve.tensor_tensor(to[:, 0, f, :], src[:, f, :], st.vm[:, bass.ds(b, 1), :].squeeze(1), ALU.mult)
                ins.then_inc(chain, 1)
                dve.wait_ge(chain, seen)
                dve.tensor_tensor(to[:, 1, :, :], src, to[:, 0, :, :], ALU.subtract).then_inc(sem, 1)

            def pick_tokens(b, links):
                pick(z, st.XT[:, :, bass.ts(b, Q)], b, z_ready, links + 1)

            def rotate(b, t, links):
                cos = st.rope[:, t, 0:8].unsqueeze(1).to_broadcast([P, 64, 8])
                msin = st.rope[:, t, 8:16].unsqueeze(1).to_broadcast([P, 32, 8])
                sin = st.rope[:, t, 16:24].unsqueeze(1).to_broadcast([P, 32, 8])
                pairs = ps_qk[t][:, :].rearrange("p (g h e) -> p g h e", h=2, e=8)
                rb = rot_b[:, t, :].rearrange("p (g h e) -> p g h e", h=2, e=8)
                dve.wait_ge(qk_made, 2 * b + t + 1)
                dve.tensor_tensor(rot_a[:, t, :].rearrange("p (g e) -> p g e", e=8),
                                  ps_qk[t][:, :].rearrange("p (g e) -> p g e", e=8), cos, ALU.mult).then_inc(chain, 1)
                dve.tensor_tensor(rb[:, :, 0, :], pairs[:, :, 1, :], msin, ALU.mult).then_inc(chain, 1)
                dve.tensor_tensor(rb[:, :, 1, :], pairs[:, :, 0, :], sin, ALU.mult).then_inc(chain, 1)
                dve.wait_ge(chain, links + 3)
                dve.tensor_tensor(rot_a[:, t, :], rot_a[:, t, :], rot_b[:, t, :], ALU.add).then_inc(rot_ready, 1)

            def add(b):
                dve.wait_ge(y_made, b + 1)
                dve.tensor_tensor(st.X[:, bass.ds(2 * b, 2), :], ps_y[:, :, :], st.X[:, bass.ds(2 * b, 2), :],
                                  ALU.add).then_inc(y_added, 1)

            def take_statistics(b):
                dve.wait_ge(y_added, b + 2)
                dve.sem_inc(dve_passed, 1)
                for t in range(2):
                    tile_statistics(dve, st, 2 * b + t)

            def batch(b, at_end, at_start=False):
                n0 = b * H
                k0 = 7 + 8 * b
                for h in range(H):
                    n = n0 + h
                    p = h % 2
                    dve.wait_ge(exped, 2 * n + 2)
                    dve.wait_ge(scored, n + 1)
                    dve.sem_inc(dve_passed, 1)
                    dve.tensor_tensor_reduce(out=neg[:, p, 0:P], in0=ps_qk[p][:, 0:P], in1=causal[:, P:2 * P],
                                             scale=-1.0, scalar=BIG, op0=ALU.add, op1=ALU.min,
                                             accum_out=negmax[:, p, 0:1]).then_inc(maxed, 1)
                    dve.tensor_tensor_reduce(out=neg[:, p, P:3 * P], in0=ps_qk[p][:, P:3 * P], in1=causal[:, :],
                                             scale=-1.0, scalar=BIG, op0=ALU.add, op1=ALU.min,
                                             accum_out=negmax[:, p, 1:2]).then_inc(maxed, 1)
                    if h == 1 and not at_start:
                        add(b - 1)
                    if h == 3 and not at_start:
                        take_statistics(b - 1)
                    if h == 5 and not at_end:
                        dve.wait_ge(v_made, b + 1)
                        pick_tokens(b + 1, k0)
                if not at_end:
                    rotate(b + 1, 0, k0 + 1)
                dve.wait_ge(exped, 2 * n0 + 2 * H + 4)
                dve.reciprocal(inv[:, :, :], rowsum[:, :, :]).then_inc(inverted, 1)
                dve.wait_ge(inverted, b + 1)
                dve.wait_ge(pv_done, n0 + H + 2)
                dve.tensor_tensor(o_sb[:, :, :].rearrange("p t (h w) -> p (t h) w", w=W),
                                  ps_v[:, :, :].rearrange("p t (h w) -> p (t h) w", w=W),
                                  inv[:, :, :].rearrange("p t h -> p (t h)").unsqueeze(2).to_broadcast([P, 2 * H, W]),
                                  ALU.mult).then_inc(o_ready, 1)
                if not at_end:
                    rotate(b + 1, 1, k0 + 4)
                dve.wait_ge(oT_made, b + 1)
                pick(oT, ps_oT[:, :, :], b, oT_ready, k0 + (1 if at_end else 8))

            pick_tokens(0, 0)
            rotate(0, 0, 1)
            rotate(0, 1, 4)
            batch(0, False, True)
            with dve.Fori(1, B - 1) as b:
                batch(b, False)
            batch(B - 1, True)
            add(B - 1)
            take_statistics(B - 1)

        @block.scalar
        def _(act):
            act.sem_inc(exped, 4)
            act.sem_inc(pT_ready, 2)

            def copy_projections(b):
                act.wait_ge(v_made, b + 1)
                act.activation(v_sb[:, :, :], ps_v[:, :, :], ACT.Copy).then_inc(v_ready, 1)
                for t in range(2):
                    act.wait_ge(qkT_made, 2 * b + t + 1)
                    act.activation(qT[:, :, t * P:(t + 1) * P],
                                   ps_t[t][:, 0:2 * P].rearrange("p (f q) -> p f q", f=2), ACT.Copy)
                    act.activation(kT[:, :, t * P:(t + 1) * P],
                                   ps_t[t][:, 2 * P:4 * P].rearrange("p (f q) -> p f q", f=2),
                                   ACT.Copy).then_inc(qkT_ready, 1)

            def batch(b, at_end):
                n0 = b * H
                for h in range(H + 1):
                    if h < H:
                        n = n0 + h
                        p = h % 2
                        for t in range(2):
                            act.wait_ge(maxed, 2 * n + t + 5)
                            act.wait_ge(turned, n + 1)
                            cols = slice(0, P) if t == 0 else slice(P, 3 * P)
                            act.activation(probs[:, p, cols], neg[:, p, cols], ACT.Exp, scale=-1.0,
                                           bias=negmax[:, p, t:t + 1],
                                           accum_out=rowsum[:, t, h:h + 1]).then_inc(exped, 1)
                    if h >= 1:
                        n = n0 + h - 1
                        p = (h - 1) % 2
                        act.wait_ge(turned, n + 3)
                        act.wait_ge(pv_done, n + 1)
                        act.activation(pT[:, p, :], ps_t[p][:, 0:3 * P], ACT.Copy).then_inc(pT_ready, 1)
                if not at_end:
                    copy_projections(b + 1)

            copy_projections(0)
            with act.Fori(0, B - 1) as b:
                batch(b, False)
            batch(B - 1, True)

        @block.gpsimd
        def _(pool):
            with pool.Fori(0, B) as b:
                pool.wait_ge(qkT_ready, 2 * b + 2)
                pool.sem_inc(pool_passed, 1)
                for h in range(H):
                    pool.tensor_scalar(qm[:, h, :], qT[:, h // 8, :], st.head_rows[:, h % 8:h % 8 + 1], None,
                                       ALU.mult).then_inc(qm_ready, 1)


def expert_mlp_phase(nc, st, io):
    FT = (EXPERT_F + P - 1) // P
    TC = Q
    NC = B * Q // TC
    starts = [min(t * P, EXPERT_F - P) for t in range(FT)]
    (wg_hi, wg_lo), (wu_hi, wu_lo), (wd_hi, wd_lo) = st.expert_weights
    with Phase(nc, "experts") as ph:
        lm = ph.sb("lm", [P, B * Q])
        x_hi = ph.sb("x_hi", [P, 2, TC], F32R)
        x_lo = ph.sb("x_lo", [P, 2, TC], F32R)
        z_hi = [ph.sb(f"z_hi{i}", [P, 2, 2, TC], F32R) for i in range(2)]
        z_lo = [ph.sb(f"z_lo{i}", [P, 2, 2, TC], F32R) for i in range(2)]
        act_g = [ph.sb(f"act_g{i}", [P, TC]) for i in range(2)]
        hid = [ph.sb(f"hid{i}", [P, TC]) for i in range(2)]
        h_hi = [ph.sb(f"h_hi{i}", [P, TC], F32R) for i in range(2)]
        h_lo = [ph.sb(f"h_lo{i}", [P, TC], F32R) for i in range(2)]
        hx_hi = ph.sb("hx_hi", [P, 2, FT, TC], F32R)
        hx_lo = ph.sb("hx_lo", [P, 2, FT, TC], F32R)
        ps_g = [ph.ps(f"ps_g{i}", [P, BANK]) for i in range(2)]
        ps_u = [ph.ps(f"ps_u{i}", [P, BANK]) for i in range(2)]
        ps_y = [ph.ps(f"ps_y{i}", [P, BANK]) for i in range(2)]
        lm_ready = ph.sem("lm_ready")
        x_split = ph.sem("x_split")
        z_ready = ph.sem("z_ready")
        made = ph.sem("made")
        silu_done = ph.sem("silu_done")
        steps = ph.sem("steps")
        hx_ready = ph.sem("hx_ready")
        y_made = ph.sem("y_made")
        y_added = ph.sem("y_added")
        pool_passed = ph.sem("pool_passed")
        block = ph.block()
        vm_flat = st.vm[:, :, :].rearrange("p b q -> p (b q)")

        def drive(eng, chunk):
            chunk(0, 0, True)
            with eng.Fori(0, (NC - 2) // 2) as i:
                chunk(2 * i + 1, 1, False)
                chunk(2 * i + 2, 0, False)
            chunk(NC - 1, 1, False)

        @block.gpsimd
        def _(pool):
            def chunk(c, par, first):
                src = st.XT[:, :, bass.ts(c, TC)]
                if not first:
                    pool.wait_ge(z_ready, 8 * c)
                pool.sem_inc(pool_passed, 1)
                pool.tensor_copy(x_hi[:, :, :], src).then_inc(x_split, 1)
                pool.wait_ge(x_split, 2 * c + 1)
                pool.sem_inc(pool_passed, 1)
                pool.tensor_tensor(x_lo[:, :, :], src, x_hi[:, :, :].bitcast(F32), ALU.subtract).then_inc(x_split, 1)
                pool.wait_ge(x_split, 2 * c + 2)
                if not (first or isinstance(c, int) and c < 2):
                    pool.wait_ge(made, FT * (c - 1))
                pool.sem_inc(pool_passed, 1)
                for z, x in ((z_hi, x_hi), (z_lo, x_lo)):
                    for e, mask in enumerate((vm_flat, lm)):
                        for f in range(2):
                            pool.tensor_tensor(z[par][:, e, f, :], x[:, f, :].bitcast(F32), mask[:, bass.ts(c, TC)],
                                               ALU.mult).then_inc(z_ready, 1)

            pool.tensor_scalar(lm[:, :], vm_flat, -1.0, 1.0, ALU.mult, ALU.add).then_inc(lm_ready, 1)
            pool.wait_ge(lm_ready, 1)
            chunk(0, 0, True)
            chunk(1, 1, False)
            with pool.Fori(1, NC // 2) as i:
                chunk(2 * i, 0, False)
                chunk(2 * i + 1, 1, False)

        @block.tensor
        def _(pe):
            def chunk(c, par, first):
                pe.wait_ge(z_ready, 8 * (c + 1))
                for t in range(FT):
                    if not (first and t < 2):
                        pe.wait_ge(hx_ready, 4 * (FT * c + t - 1))
                    w = slice(starts[t], starts[t] + P)
                    for out, hi, lo in ((ps_g, wg_hi, wg_lo), (ps_u, wu_hi, wu_lo)):
                        for e in range(2):
                            for f in range(2):
                                pe.matmul(out[t % 2][:, 0:TC], hi[:, e, f, w], z_hi[par][:, e, f, :],
                                          start=(e == 0 and f == 0), stop=False)
                                pe.matmul(out[t % 2][:, 0:TC], hi[:, e, f, w], z_lo[par][:, e, f, :],
                                          start=False, stop=False)
                                ins = pe.matmul(out[t % 2][:, 0:TC], lo[:, e, f, w], z_hi[par][:, e, f, :],
                                                start=False, stop=(e == 1 and f == 1))
                    ins.then_inc(made, 1)
                if not first:
                    pe.wait_ge(y_added, 2 * c)
                for tiles in (range(FT - 1), range(FT - 1, FT)):
                    pe.wait_ge(hx_ready, 4 * (FT * c + tiles[-1] + 1))
                    for r in range(TC // P):
                        q = slice(r * P, (r + 1) * P)
                        for t in tiles:
                            for e in range(2):
                                pe.matmul(ps_y[r][:, 0:D], hx_hi[:, e, t, q], wd_hi[:, e, t, :],
                                          start=(t == 0 and e == 0), stop=False)
                                pe.matmul(ps_y[r][:, 0:D], hx_hi[:, e, t, q], wd_lo[:, e, t, :], start=False, stop=False)
                                ins = pe.matmul(ps_y[r][:, 0:D], hx_lo[:, e, t, q], wd_hi[:, e, t, :],
                                                start=False, stop=(t == FT - 1 and e == 1))
                        if tiles[-1] == FT - 1:
                            ins.then_inc(y_made, 1)

            drive(pe, chunk)

        @block.scalar
        def _(act):
            def chunk(c, par, first):
                for t in range(FT):
                    if not (first and t < 2):
                        act.wait_ge(hx_ready, 4 * (FT * c + t - 1))
                    act.wait_ge(made, FT * c + t + 1)
                    act.activation(act_g[t % 2][:, :], ps_g[t % 2][:, 0:TC], ACT.Silu).then_inc(silu_done, 1)

            drive(act, chunk)

        @block.vector
        def _(dve):
            def chunk(c, par, first):
                tokens = bass.ts(c, TC)
                for t in range(FT):
                    m = FT * c + t
                    i = t % 2
                    if not (first and t < 2):
                        dve.wait_ge(hx_ready, 4 * (m - 1))
                    dve.wait_ge(silu_done, m + 1)
                    dve.tensor_tensor(hid[i][:, :], act_g[i][:, :], ps_u[i][:, 0:TC], ALU.mult).then_inc(steps, 1)
                    dve.wait_ge(steps, 3 * m + 1)
                    dve.tensor_copy(h_hi[i][:, :], hid[i][:, :]).then_inc(steps, 1)
                    dve.wait_ge(steps, 3 * m + 2)
                    dve.tensor_tensor(h_lo[i][:, :], hid[i][:, :], h_hi[i][:, :].bitcast(F32), ALU.subtract).then_inc(steps, 1)
                    for e, mask in enumerate((vm_flat, lm)):
                        dve.tensor_tensor(hx_hi[:, e, t, :], h_hi[i][:, :].bitcast(F32), mask[:, tokens],
                                          ALU.mult).then_inc(hx_ready, 1)
                    dve.wait_ge(steps, 3 * m + 3)
                    for e, mask in enumerate((vm_flat, lm)):
                        dve.tensor_tensor(hx_lo[:, e, t, :], h_lo[i][:, :].bitcast(F32), mask[:, tokens],
                                          ALU.mult).then_inc(hx_ready, 1)
                for r in range(2):
                    x = st.X[:, bass.ds(2 * c + r, 1), :].squeeze(1)
                    dve.wait_ge(y_made, 2 * c + r + 1)
                    dve.tensor_tensor(x, ps_y[r][:, 0:D], x, ALU.add).then_inc(y_added, 1)

            dve.wait_ge(lm_ready, 1)
            drive(dve, chunk)


def memory_weights_phase(nc, st, io):
    with Phase(nc, "memw") as ph:
        w = ph.sb("w", [P, 2, C])
        loaded = ph.sem("loaded")
        block = ph.block()

        @block.sync
        def _(sp):
            sp.dma_start(w[:, :, :], io["L2_mem"]).then_inc(loaded, 16)
            sp.dma_start(st.Bw[:, 0:D], io["L2_memT"]).then_inc(loaded, 16)
            sp.wait_ge(loaded, 32)

        @block.vector
        def _(dve):
            dve.wait_ge(loaded, 32)
            dve.tensor_scalar(st.A[:, :, 0:C], w[:, :, :], D ** -0.5, None, ALU.mult)


def gate_phase(nc, st, io):
    with Phase(nc, "gate") as ph:
        wg = ph.sb("wg", [P, 4, D])
        bias = ph.sb("bias", [P, D])
        norm_w = ph.sb("norm_w", [P, D])
        mc = [ph.sb(f"mc{i}", [P, D]) for i in range(2)]
        zT = [ph.sb(f"zT{i}", [P, 4, P]) for i in range(2)]
        g = [ph.sb(f"g{i}", [P, D]) for i in range(2)]
        rows = ph.sb("rows", [P, 4, NT])
        ps_t = [ph.ps(f"ps_t{i}", [P, BANK]) for i in range(2)]
        ps_z = [ph.ps(f"ps_z{i}", [P, D]) for i in range(2)]
        loaded = ph.sem("loaded")
        mc_ready = ph.sem("mc_ready")
        hs_ready = ph.sem("hs_ready")
        turned = ph.sem("turned")
        zT_ready = ph.sem("zT_ready")
        z_made = ph.sem("z_made")
        summed = ph.sem("summed")
        pool_passed = ph.sem("pool_passed")
        sig_done = ph.sem("sig_done")
        scaled = ph.sem("scaled")
        fused = ph.sem("fused")
        stats_taken = ph.sem("stats_taken")
        dve_passed = ph.sem("dve_passed")
        chain_sem = ph.sem("chain")
        root_asked = ph.sem("root_asked")
        root_taken = ph.sem("root_taken")
        block = ph.block()

        @block.sync
        def _(sp):
            sp.dma_start(wg[:, :, :], io["L2_gateT"]).then_inc(loaded, 16)
            sp.dma_start(bias[:, :], io["L2_gate_b"].to_broadcast([P, D])).then_inc(loaded, 16)
            sp.dma_start(norm_w[:, :], io["L2_norm_w"].to_broadcast([P, D])).then_inc(loaded, 16)

        @block.gpsimd
        def _(pool):
            pool.wait_ge(loaded, 48)
            with pool.Fori(0, NT // 2) as i:
                for par in range(2):
                    j = 2 * i + par
                    pool.wait_ge(turned, j + 1)
                    pool.sem_inc(pool_passed, 1)
                    pool.tensor_copy(mc[par][:, :], st.MC[:, bass.ds(j, 1), :].squeeze(1)).then_inc(mc_ready, 1)
                    pool.wait_ge(z_made, j + 1)
                    pool.sem_inc(pool_passed, 1)
                    pool.tensor_copy(zT[par][:, 0:2, :], st.XT[:, :, bass.ts(j, P)]).then_inc(hs_ready, 1)

        @block.tensor
        def _(pe):
            pe.sem_inc(turned, 2)
            pe.sem_inc(z_made, 2)
            pe.wait_ge(loaded, 48)
            with pe.Fori(0, NT // 2) as i:
                for par in range(2):
                    j = 2 * i + par
                    pe.wait_ge(mc_ready, j + 1)
                    pe.wait_ge(zT_ready, j + 1)
                    for f in range(2):
                        ins = pe.transpose(ps_t[par][:, f * P:(f + 1) * P], mc[par][:, f * P:(f + 1) * P],
                                           st.ident[:, :])
                    ins.then_inc(turned, 1)
                for par in range(2):
                    j = 2 * i + par
                    pe.wait_ge(hs_ready, j + 1)
                    pe.wait_ge(zT_ready, j + 3)
                    pe.wait_ge(summed, j + 1)
                    for f in range(4):
                        ins = pe.matmul(ps_z[par][:, :], zT[par][:, f, :], wg[:, f, :], start=(f == 0), stop=(f == 3))
                    ins.then_inc(z_made, 1)

        @block.scalar
        def _(act):
            act.sem_inc(zT_ready, 2)
            with act.Fori(0, NT // 2) as i:
                for par in range(2):
                    j = 2 * i + par
                    act.wait_ge(turned, j + 3)
                    act.wait_ge(z_made, j + 1)
                    act.activation(zT[par][:, 2:4, :], ps_t[par][:, 0:2 * P].rearrange("p (f q) -> p f q", f=2),
                                   ACT.Copy).then_inc(zT_ready, 1)
                for par in range(2):
                    j = 2 * i + par
                    act.wait_ge(summed, j + 3)
                    act.activation(g[par][:, :], g[par][:, :], ACT.Sigmoid).then_inc(sig_done, 1)
            act.wait_ge(root_asked, 1)
            act.activation(rows[:, 1, :], rows[:, 1, :], ACT.Sqrt).then_inc(root_taken, 1)

        @block.vector
        def _(dve):
            dve.sem_inc(summed, 2)
            dve.sem_inc(fused, 2)
            dve.wait_ge(loaded, 48)
            with dve.Fori(0, NT // 2) as i:
                for par in range(2):
                    dve.wait_ge(fused, 2 * i + par + 1)
                    dve.wait_ge(z_made, 2 * i + par + 3)
                    dve.tensor_tensor(g[par][:, :], ps_z[par][:, :], bias[:, :], ALU.add).then_inc(summed, 1)
                for par in range(2):
                    j = 2 * i + par
                    dve.wait_ge(sig_done, j + 1)
                    dve.tensor_tensor(g[par][:, :], g[par][:, :], st.MC[:, bass.ds(j, 1), :].squeeze(1),
                                      ALU.mult).then_inc(scaled, 1)
                    dve.wait_ge(scaled, j + 1)
                    dve.tensor_tensor(st.X[:, bass.ds(j, 1), :].squeeze(1), g[par][:, :],
                                      st.X[:, bass.ds(j, 1), :].squeeze(1), ALU.add).then_inc(fused, 1)
                for par in range(2):
                    dve.wait_ge(fused, 2 * i + par + 3)
                    dve.sem_inc(dve_passed, 1)
                    tile_statistics(dve, st, 2 * i + par).then_inc(stats_taken, 1)
            dve.wait_ge(stats_taken, NT)
            chain = Chain(dve, chain_sem)
            row_statistics(dve, chain, st.stats, rows, 1e-6, True, root_asked, root_taken)
            with dve.Fori(0, NT) as j:
                x = st.X[:, bass.ds(j, 1), :].squeeze(1)
                dve.scalar_tensor_tensor(out=x, in0=x, scalar=rows[:, 1, bass.ds(j, 1)], in1=norm_w[:, :],
                                         op0=ALU.mult, op1=ALU.mult)


class State:
    pass


def expert_layer(nc, st, io, stages):
    with ExitStack() as ctx:
        def sb(name, shape):
            return ctx.enter_context(nc.sbuf_tensor(name, shape, F32))

        st.vm = sb("vm", [P, B, Q])
        st.rope = sb("rope", [P, 2, 24])
        st.head_rows = sb("head_rows", [P, 8])
        for stage, args in stages:
            stage(nc, st, io, *args)


def expert_mlp(nc, st, io):
    FT = (EXPERT_F + P - 1) // P
    shapes = {"gate": [P, 2, 2, EXPERT_F], "up": [P, 2, 2, EXPERT_F], "down": [P, 2, FT, D]}
    with ExitStack() as ctx:
        st.expert_weights = [[ctx.enter_context(nc.sbuf_tensor(f"{n}_{part}", shape, F32R)) for part in ("hi", "lo")]
                             for n, shape in shapes.items()]

        def pieces(ph, st):
            staging = [st.A[:, :, :].rearrange("p a c -> p (a c)")[:, 0:4 * EXPERT_F], st.Bw[:, 0:4 * EXPERT_F],
                       ph.sb("down", [P, 2 * FT * D])[:, :]]
            return [([f"L1_{e}_{n}" for e in "vl"], staging[i], *(w[:, :, :, :].rearrange("p e f c -> p (e f c)")
                                                                for w in st.expert_weights[i]))
                    for i, n in enumerate(shapes)]

        norm_phase(nc, st, io, "L1_norm3", "rms", "L1_ln_post_attn_w", None, 1e-6, (SplitWeights, pieces))
        expert_mlp_phase(nc, st, io)


def perceiver_mlp(nc, st, io, n):
    F = 4 * D
    shapes = {"w1": [P, 2, F], "w2": [P, F // P, D]}
    with ExitStack() as ctx:
        st.mlp_weights = [[ctx.enter_context(nc.sbuf_tensor(f"{n}_{w}_{part}", shape, F32R)) for part in ("hi", "lo")]
                          for w, shape in shapes.items()]

        def pieces(ph, st):
            return [([f"{n}_mlp_{w}"], st.A[:, i, :], *(w[:, :, :].rearrange("p f c -> p (f c)") for w in st.mlp_weights[i]))
                    for i, w in enumerate(shapes)]

        norm_phase(nc, st, io, f"{n}_norm2", "ln", f"{n}_ln_ff_g", f"{n}_ln_ff_b", 1e-5, (SplitWeights, pieces))
        mlp_phase(nc, st, io, f"{n}_mlp", f"{n}_ff_gate")


def memory_layer(nc, st, io, stages):
    with nc.sbuf_tensor("MC", [P, NT, D], F32) as st.MC:
        for stage, args in stages:
            stage(nc, st, io, *args)


def build(nc, io, stages):
    with ExitStack() as ctx:
        def sb(name, shape):
            return ctx.enter_context(nc.sbuf_tensor(name, shape, F32))

        st = State()
        st.ident = sb("ident", [P, P])
        st.X = sb("X", [P, NT, D])
        st.stats = sb("stats", [P, NT, 6])
        st.XT = sb("XT", [P, 2, B * Q])
        st.A = sb("A", [P, 2, 16 * C])
        st.Bw = sb("Bw", [P, 16 * D])
        st.Wv, st.Wo = st.Bw[:, 0:8 * P], st.Bw[:, 8 * P:8 * P + 8 * D]
        for stage, args in stages:
            stage(nc, st, io, *args)


def perceiver_stages(n):
    return [
        (norm_phase, (f"{n}_norm1", "ln", f"{n}_ln_q_g", f"{n}_ln_q_b", 1e-5,
                      (GatedWeights, f"{n}_w", 16, 64, 64 ** -0.5, f"{n}_attn_gate"), True)),
        (grouped_attention_phase, (f"{n}_attn", 16, 64)),
        (perceiver_mlp, (n,)),
    ]


EXPERT_STAGES = [
    (expert_masks_phase, ()),
    (norm_phase, ("L1_norm1", "rms", "L1_ln_in_w", None, 1e-6)),
    (self_attention_phase, ()),
    (norm_phase, ("L1_norm2", "rms", "L1_ln_post_cross_w", None, 1e-6)),
    (narrow_attention_phase, ("L1_cross", 16, 8)),
    (expert_mlp, ()),
]

MEMORY_STAGES = [
    (norm_phase, ("L2_turn", "plain")),
    (memory_weights_phase, ()),
    (memory_attention_phase, ()),
    (gate_phase, ()),
]

STAGES = ([(load_phase, ())] + perceiver_stages("L0") + [(expert_layer, (EXPERT_STAGES,))]
          + [(memory_layer, (MEMORY_STAGES,))] + perceiver_stages("L3") + [(store_phase, ())])


def layout(inputs):
    import numpy as np

    def heads_first(w, width):
        w = np.asarray(w)
        return w.reshape(w.shape[0], -1, width).transpose(2, 1, 0)

    def tiled(w):
        w = np.asarray(w)
        return w.reshape(-1, P, w.shape[1]).transpose(1, 0, 2)

    def halves(v):
        return np.asarray(v).reshape(2, P).T

    ctx = np.asarray(inputs["ctx_1024"])
    padded = np.zeros((B, SP, C), ctx.dtype)
    padded[:, :S] = ctx
    mask = np.zeros((B, 4 * MASK_WORDS), np.bool_)
    mask[:, :S] = np.asarray(inputs["mask_BxS2_bk0"])
    a = {
        "ident": np.eye(P, dtype=np.float32),
        "x": np.asarray(inputs["x"]).reshape(B * Q, D),
        "ctxT": padded[:, :S_EVEN].transpose(0, 2, 1),
        "ctx": padded.reshape(B, KT, P, C).transpose(0, 2, 1, 3),
        "mask": mask.view(np.int32),
    }
    for n in ("L0", "L3"):
        def w(k):
            return np.asarray(inputs[f"{n}_xattn_{k}"])
        for k in ("ln_q_g", "ln_q_b", "ln_ff_g", "ln_ff_b"):
            a[f"{n}_{k}"] = halves(w(k))
        kv = w("Wkv")
        a[f"{n}_w_wq"] = heads_first(w("Wq"), 64)
        a[f"{n}_w_wk"] = heads_first(kv[:, :1024], 64)
        a[f"{n}_w_wv"] = kv[:, 1024:]
        a[f"{n}_w_wo"] = tiled(w("Wo"))
        a[f"{n}_attn_gate"] = w("attn_gate").reshape(1, 1)
        a[f"{n}_ff_gate"] = w("ff_gate").reshape(1, 1)
        a[f"{n}_mlp_w1"] = tiled(w("W1"))
        a[f"{n}_mlp_w2"] = tiled(w("W2"))
    def w(k):
        return np.asarray(inputs[f"L1_xattn_{k}"])
    for k in ("ln_in_w", "ln_post_attn_w", "ln_post_cross_w"):
        a[f"L1_{k}"] = halves(w(k))
    for e in "vl":
        a[f"L1_{e}_qkv"] = tiled(w(f"{e}_qkv"))
        a[f"L1_{e}_dense"] = tiled(w(f"{e}_dense"))
        a[f"L1_{e}_gate"] = tiled(w(f"{e}_gate"))
        a[f"L1_{e}_up"] = tiled(w(f"{e}_up"))
        down = np.zeros((768, D), np.float32)
        down[:640] = w(f"{e}_down")[:640]
        down[720:] = w(f"{e}_down")[640:]
        a[f"L1_{e}_down"] = tiled(down)
    ckv = w("ckv_w")
    a["L1_cross_wq"] = tiled(w("cq_w"))
    a["L1_cross_wk"] = ckv[:, :C]
    a["L1_cross_wv"] = ckv[:, C:]
    a["L1_cross_wo"] = np.pad(w("cdense_w").reshape(4, 4, 8, D), ((0, 0), (0, 0), (0, 24), (0, 0))).reshape(4, P, D).transpose(1, 0, 2)
    a["L2_mem"] = tiled(inputs["L2_xattn_W_mem"])
    a["L2_memT"] = np.asarray(inputs["L2_xattn_W_mem"]).T
    a["L2_gateT"] = tiled(np.asarray(inputs["L2_xattn_W_gate"]).T)
    a["L2_gate_b"] = np.asarray(inputs["L2_xattn_b_gate"]).reshape(1, D)
    a["L2_norm_w"] = np.asarray(inputs["L2_xattn_norm_w"]).reshape(1, D)
    a["types"] = np.asarray(inputs["mask_BxS_ik0"])
    a["positions"] = np.asarray(inputs["pos_1xS"])
    freqs = np.outer(np.arange(Q, dtype=np.float32),
                     (1.0 / 10000.0 ** (np.arange(0, 16, 2, dtype=np.float32) / np.float32(16))).astype(np.float32))
    cos, sin = np.cos(freqs).astype(np.float32), np.sin(freqs).astype(np.float32)
    a["rope_table"] = tiled(np.concatenate([cos, -sin, sin], axis=1))
    a["row_numbers"] = np.arange(Q, dtype=np.float32).reshape(2, P).T
    a["head_rows"] = np.kron(np.eye(8, dtype=np.float32), np.full((16, 1), 0.25, np.float32))
    a["head_picks"] = (np.arange(P)[:, None] // 8 % 4 == np.arange(4)).astype(np.float32)
    a["causal"] = np.concatenate([np.zeros((P, P), np.float32),
                                  np.triu(np.full((P, P), -NEG, np.float32), 1)], axis=1)
    return a


def kernel(**inputs):
    import numpy as np
    import concourse.bacc as bacc
    from concourse.bass_utils import run_bass_kernel_spmd

    nc = bacc.Bacc("TRN2", target_bir_lowering=False, num_devices=1)
    arrays = {k: np.ascontiguousarray(v) for k, v in layout(inputs).items()}
    io = {k: nc.dram_tensor(f"in_{k}", v.shape, mybir.dt.from_np(v.dtype), kind="ExternalInput").ap()
          for k, v in arrays.items()}
    io["out"] = nc.dram_tensor("out", (B * Q, D), F32, kind="ExternalOutput").ap()
    build(nc, io, STAGES)
    r = run_bass_kernel_spmd(nc, [{f"in_{k}": v for k, v in arrays.items()}], core_ids=[0])
    return r.results[0]["out"].reshape(B, Q, D)
```
